# Optimizing a Trainium2 kernel written in Bass

```python
import numpy as np
import jax
import jax.numpy as jnp

def _softmax(x, axis=-1):
    return jax.nn.softmax(x, axis=axis)

def _gelu(x):
    return jax.nn.gelu(x, approximate=True)

def _silu(x):
    return jax.nn.silu(x)

def _sigmoid(x):
    return jax.nn.sigmoid(x)

def _layernorm(x, axis=-1, eps=1e-05):
    m = jnp.mean(x, axis=axis, keepdims=True)
    v = jnp.var(x, axis=axis, keepdims=True)
    return (x - m) / jnp.sqrt(v + eps)

def _scatter_add(tgt, idx, src, axis=0):
    return tgt.at[idx].add(src)

def _segment_sum(src, seg, n):
    return jax.ops.segment_sum(src, seg, n)
kernel_name = 'mk_flamingo_gated_d2_seqx_r8_421dc9'

def setup_inputs(seed: int=0):
    np.random.seed(seed)
    _w = jnp.asarray

    def _rec_inputs():
        import jax
        import jax.numpy as jnp
        _rk = jax.random.key(seed)
        x = 2.818e-05 + 1 * jax.random.normal(jax.random.fold_in(_rk, 1), (4, 256, 256), jnp.float32)
        _lenS = 256 - jax.random.randint(jax.random.fold_in(_rk, 7), (4,), 0, max(1, 256 // 4) + 1, jnp.int32)
        _lenS2 = 256 - jax.random.randint(jax.random.fold_in(_rk, 8), (4,), 0, max(1, 256 // 4) + 1, jnp.int32)
        _ctx_1024P = jax.random.normal(jax.random.fold_in(_rk, 11), (4, 16, 128), jnp.float32)
        _ctx_1024c = jax.random.dirichlet(jax.random.fold_in(_rk, 511), 0.3 * jnp.ones((16,), jnp.float32), (4, 256))
        _ctx_1024t = jnp.einsum('bsk,bkd->bsd', _ctx_1024c, _ctx_1024P)
        _ctx_1024t = _ctx_1024t * jax.lax.rsqrt(jnp.mean(jnp.square(_ctx_1024t)) + 1e-12) * 0.953939
        ctx_1024 = 7.22013e-05 + 1.00017 * (_ctx_1024t + 0.3 * jax.random.normal(jax.random.fold_in(_rk, 611), (4, 256, 128), jnp.float32))
        _validS = jnp.arange(256)[None, :] < _lenS[:, None]
        _validS2 = jnp.arange(256)[None, :] < _lenS2[:, None]
        _causal = jnp.tril(jnp.ones((256, 256), dtype=bool))
        mask_BxS2_bf1 = jnp.ones((4, 256), dtype=bool)
        _g = jax.random.normal(jax.random.fold_in(_rk, 9001), (2, 2), jnp.float32)
        _g = jnp.sign(_g) * jnp.maximum(jnp.abs(_g), 1.0) + (_g == 0) * 1.0
        g_xattn = _g[0]
        g_ffn = _g[1]
        return (x, ctx_1024, mask_BxS2_bf1, g_xattn, g_ffn)
    x, ctx_1024, mask_BxS2_bf1, g_xattn, g_ffn = _rec_inputs()

    def _L0_xattn_setup():
        import jax, jax.numpy as jnp
        import numpy as np
        B_, L_, D_MODEL = (4, 256, 128)
        D_STATE, D_CONV, EXPAND = (16, 4, 2)
        D_INNER = EXPAND * D_MODEL
        DT_RANK = (D_MODEL + 15) // 16

        def silu(x):
            return x * jax.nn.sigmoid(x)
        key = jax.random.key(seed)
        ks = jax.random.split(key, 10)
        f32 = jnp.float32
        hidden_states = jax.random.normal(ks[0], (B_, L_, D_MODEL), dtype=f32)
        z = jax.random.normal(ks[1], (B_, D_INNER, L_), dtype=f32)
        in_proj_w = jax.random.normal(ks[2], (D_INNER, D_MODEL), dtype=f32) * 0.02
        conv_w = jax.random.normal(ks[3], (D_INNER, 1, D_CONV), dtype=f32) * 0.1
        conv_b = jax.random.normal(ks[4], (D_INNER,), dtype=f32) * 0.02
        x_proj_w = jax.random.normal(ks[5], (DT_RANK + 2 * D_STATE, D_INNER), dtype=f32) * 0.02
        dt_proj_w = jax.random.uniform(ks[6], (D_INNER, DT_RANK), dtype=f32, minval=-DT_RANK ** (-0.5), maxval=DT_RANK ** (-0.5))
        dt = jnp.exp(jax.random.uniform(ks[7], (D_INNER,), dtype=f32, minval=np.log(0.001), maxval=np.log(0.1)))
        dt_proj_b = jnp.log(jnp.expm1(dt))
        A_log = jnp.log(jnp.broadcast_to(jnp.arange(1, D_STATE + 1, dtype=f32), (D_INNER, D_STATE)))
        D = jnp.ones((D_INNER,), f32)
        return {'hidden_states': hidden_states, 'z': z, 'in_proj_w': in_proj_w, 'conv_w': conv_w, 'conv_b': conv_b, 'x_proj_w': x_proj_w, 'dt_proj_w': dt_proj_w, 'dt_proj_b': dt_proj_b, 'A_log': A_log, 'D': D}
    _L0_xattn_all = _L0_xattn_setup()
    _L0_xattn_in = {k: v for k, v in _L0_xattn_all.items() if k in ('in_proj_w', 'conv_w', 'conv_b', 'x_proj_w', 'dt_proj_w', 'dt_proj_b', 'A_log', 'D')}
    del _L0_xattn_all

    def _L0_ffn_setup():
        import jax, jax.numpy as jnp
        import numpy as np
        E = 64
        K = 8
        H = 256
        I = 96
        CAP = 64

        def _moe(hidden_states, gate_w, wg, wu, wd):
            B, S, Hd = hidden_states.shape
            x = hidden_states.reshape(-1, Hd)
            T = x.shape[0]
            logits = x @ gate_w.T
            probs = jax.nn.softmax(logits.astype(jnp.float32), axis=-1)
            w, sel = jax.lax.top_k(probs, K)
            w = w / jnp.sum(w, axis=-1, keepdims=True)
            w = w.astype(x.dtype)
            eid = sel.reshape(-1)
            tok = jnp.repeat(jnp.arange(T), K)
            oh = jax.nn.one_hot(eid, E, dtype=jnp.int32)
            pos = jnp.sum(jnp.cumsum(oh, axis=0) * oh, axis=-1) - 1
            valid = pos < CAP
            slot = jnp.where(valid, pos, CAP)
            xin = jnp.zeros((E, CAP + 1, Hd), x.dtype).at[eid, slot].set(x[tok])
            inp = xin[:, :CAP]
            h = jax.nn.silu(jnp.einsum('ech,ehi->eci', inp, wg)) * jnp.einsum('ech,ehi->eci', inp, wu)
            out = jnp.einsum('eci,eih->ech', h, wd)
            out_pad = jnp.concatenate([out, jnp.zeros((E, 1, Hd), out.dtype)], axis=1)
            g = out_pad[eid, slot] * (w.reshape(-1) * valid.astype(w.dtype))[:, None]
            y = jnp.zeros((T, Hd), x.dtype).at[tok].add(g)
            return y.reshape(B, S, Hd)
        key = jax.random.key(seed)
        k1, k2, k3, k4, k5 = jax.random.split(key, 5)
        hidden_states = jax.random.normal(k1, (1, 256, H), dtype=jnp.float32)
        gate_w = jax.random.normal(k2, (E, H), dtype=jnp.float32) * 0.02
        wg = jax.random.normal(k3, (E, H, I), dtype=jnp.float32) * 0.02
        wu = jax.random.normal(k4, (E, H, I), dtype=jnp.float32) * 0.02
        wd = jax.random.normal(k5, (E, I, H), dtype=jnp.float32) * 0.02
        return {'hidden_states': hidden_states, 'gate_w': gate_w, 'wg': wg, 'wu': wu, 'wd': wd}
    _L0_ffn_all = _L0_ffn_setup()
    _L0_ffn_in = {k: v for k, v in _L0_ffn_all.items() if k in ('gate_w', 'wg', 'wu', 'wd')}
    del _L0_ffn_all

    def _L1_xattn_setup():
        import jax, jax.numpy as jnp
        import numpy as np
        N_HEADS = 16
        N_KV_HEADS = 8
        HEAD_DIM = 128
        D_TEXT = 256
        D_VISION = 128
        GROUPS = N_HEADS // N_KV_HEADS
        key = jax.random.key(seed)
        ks = jax.random.split(key, 6)
        B, T_text, T_vis = (4, 256, 72)
        text_hidden = jax.random.normal(ks[0], (B, T_text, D_TEXT), dtype=jnp.float32)
        vision_tokens = jax.random.normal(ks[1], (B, T_vis, D_VISION), dtype=jnp.float32)
        vision_mask = jnp.ones((B, T_vis), dtype=bool)
        s = 0.02
        Wq = jax.random.normal(ks[2], (D_TEXT, N_HEADS * HEAD_DIM), dtype=jnp.float32) * s
        Wk = jax.random.normal(ks[3], (D_VISION, N_KV_HEADS * HEAD_DIM), dtype=jnp.float32) * s
        Wv = jax.random.normal(ks[4], (D_VISION, N_KV_HEADS * HEAD_DIM), dtype=jnp.float32) * s
        Wo = jax.random.normal(ks[5], (N_HEADS * HEAD_DIM, D_TEXT), dtype=jnp.float32) * s
        return {'text_hidden': text_hidden, 'vision_tokens': vision_tokens, 'vision_mask': vision_mask, 'Wq': Wq, 'Wk': Wk, 'Wv': Wv, 'Wo': Wo}
    _L1_xattn_all = _L1_xattn_setup()
    _L1_xattn_in = {k: v for k, v in _L1_xattn_all.items() if k in ('Wq', 'Wk', 'Wv', 'Wo')}
    del _L1_xattn_all

    def _L1_ffn_setup():
        import jax, jax.numpy as jnp
        import numpy as np
        EPS = 1e-05

        def rms_norm(x):
            return x * jax.lax.rsqrt(jnp.mean(x * x, axis=-1, keepdims=True) + EPS)

        def act_quant(x):
            scale = 127.0 / jnp.clip(jnp.max(jnp.abs(x), axis=-1, keepdims=True), 1e-05)
            q = jnp.clip(jnp.round(x * scale), -128.0, 127.0) / scale
            return x + jax.lax.stop_gradient(q - x)

        def weight_quant(w):
            scale = 1.0 / jnp.clip(jnp.mean(jnp.abs(w)), 1e-05)
            q = jnp.clip(jnp.round(w * scale), -1.0, 1.0) / scale
            return w + jax.lax.stop_gradient(q - w)

        def bitlinear158(x, w, b):
            xq = act_quant(rms_norm(x))
            wq = weight_quant(w)
            return jnp.einsum('bsd,od->bso', xq, wq) + b

        def layer_norm(x, g, b):
            mu = jnp.mean(x, axis=-1, keepdims=True)
            var = jnp.mean((x - mu) ** 2, axis=-1, keepdims=True)
            return (x - mu) * jax.lax.rsqrt(var + EPS) * g + b
        key = jax.random.key(seed)
        ks = jax.random.split(key, 3)
        d, inner = (256, 1024)
        x = jax.random.normal(ks[0], (4, 256, d), dtype=jnp.float32)
        w1 = jax.random.normal(ks[1], (inner, d), dtype=jnp.float32) * 0.02
        b1 = jnp.zeros((inner,), jnp.float32)
        ln_g = jnp.ones((inner,), jnp.float32)
        ln_b = jnp.zeros((inner,), jnp.float32)
        w2 = jax.random.normal(ks[2], (d, inner), dtype=jnp.float32) * 0.02
        b2 = jnp.zeros((d,), jnp.float32)
        return {'x': x, 'w1': w1, 'b1': b1, 'ln_g': ln_g, 'ln_b': ln_b, 'w2': w2, 'b2': b2}
    _L1_ffn_all = _L1_ffn_setup()
    _L1_ffn_in = {k: v for k, v in _L1_ffn_all.items() if k in ('w1', 'b1', 'ln_g', 'ln_b', 'w2', 'b2')}
    del _L1_ffn_all
    return {'x': x, 'ctx_1024': ctx_1024, 'mask_BxS2_bf1': mask_BxS2_bf1, 'g_xattn': g_xattn, 'g_ffn': g_ffn, 'L0_xattn_in_proj_w': _L0_xattn_in['in_proj_w'], 'L0_xattn_conv_w': _L0_xattn_in['conv_w'], 'L0_xattn_conv_b': _L0_xattn_in['conv_b'], 'L0_xattn_x_proj_w': _L0_xattn_in['x_proj_w'], 'L0_xattn_dt_proj_w': _L0_xattn_in['dt_proj_w'], 'L0_xattn_dt_proj_b': _L0_xattn_in['dt_proj_b'], 'L0_xattn_A_log': _L0_xattn_in['A_log'], 'L0_xattn_D': _L0_xattn_in['D'], 'L0_ffn_gate_w': _L0_ffn_in['gate_w'], 'L0_ffn_wg': _L0_ffn_in['wg'], 'L0_ffn_wu': _L0_ffn_in['wu'], 'L0_ffn_wd': _L0_ffn_in['wd'], 'L1_xattn_Wq': _L1_xattn_in['Wq'], 'L1_xattn_Wk': _L1_xattn_in['Wk'], 'L1_xattn_Wv': _L1_xattn_in['Wv'], 'L1_xattn_Wo': _L1_xattn_in['Wo'], 'L1_ffn_w1': _L1_ffn_in['w1'], 'L1_ffn_b1': _L1_ffn_in['b1'], 'L1_ffn_ln_g': _L1_ffn_in['ln_g'], 'L1_ffn_ln_b': _L1_ffn_in['ln_b'], 'L1_ffn_w2': _L1_ffn_in['w2'], 'L1_ffn_b2': _L1_ffn_in['b2']}

def reference(x, ctx_1024, mask_BxS2_bf1, g_xattn, g_ffn, L0_xattn_in_proj_w, L0_xattn_conv_w, L0_xattn_conv_b, L0_xattn_x_proj_w, L0_xattn_dt_proj_w, L0_xattn_dt_proj_b, L0_xattn_A_log, L0_xattn_D, L0_ffn_gate_w, L0_ffn_wg, L0_ffn_wu, L0_ffn_wd, L1_xattn_Wq, L1_xattn_Wk, L1_xattn_Wv, L1_xattn_Wo, L1_ffn_w1, L1_ffn_b1, L1_ffn_ln_g, L1_ffn_ln_b, L1_ffn_w2, L1_ffn_b2):
    import jax
    import jax.numpy as jnp

    def _L0_xattn_ref(hidden_states, z, in_proj_w, conv_w, conv_b, x_proj_w, dt_proj_w, dt_proj_b, A_log, D):
        import jax, jax.numpy as jnp
        import numpy as np
        B_, L_, D_MODEL = (4, 256, 128)
        D_STATE, D_CONV, EXPAND = (16, 4, 2)
        D_INNER = EXPAND * D_MODEL
        DT_RANK = (D_MODEL + 15) // 16

        def silu(x):
            return x * jax.nn.sigmoid(x)
        Bsz, L, _ = hidden_states.shape
        d_inner, _, d_conv = conv_w.shape
        dt_rank = dt_proj_w.shape[1]
        d_state = A_log.shape[1]
        x = jnp.einsum('bld,ed->bel', hidden_states, in_proj_w)
        xc = jax.lax.conv_general_dilated(x, conv_w, window_strides=(1,), padding=[(d_conv - 1, 0)], feature_group_count=d_inner, dimension_numbers=('NCH', 'OIH', 'NCH'))
        x = silu(xc + conv_b[None, :, None])
        x_dbl = jnp.einsum('bdl,ed->bel', x, x_proj_w)
        dt_low, Bm, Cm = jnp.split(x_dbl, [dt_rank, dt_rank + d_state], axis=1)
        dt = jnp.einsum('brl,dr->bdl', dt_low, dt_proj_w)
        dt = jax.nn.softplus(dt + dt_proj_b[None, :, None])
        A = -jnp.exp(A_log)
        dt_t = jnp.moveaxis(dt, -1, 0)
        B_t = jnp.moveaxis(Bm, -1, 0)
        C_t = jnp.moveaxis(Cm, -1, 0)
        u_t = jnp.moveaxis(x, -1, 0)

        def step(state, inp):
            d, b, c, u = inp
            dA = jnp.exp(d[..., None] * A)
            state = state * dA + (d * u)[..., None] * b[:, None, :]
            y = jnp.einsum('bdn,bn->bd', state, c)
            return (state, y)
        state0 = jnp.zeros((Bsz, d_inner, d_state), x.dtype)
        _, ys = jax.lax.scan(step, state0, (dt_t, B_t, C_t, u_t))
        y = jnp.moveaxis(ys, 0, 2)
        y = y + D[None, :, None] * x
        y = y * silu(z)
        return jnp.swapaxes(y, 1, 2)

    def _L0_ffn_ref(hidden_states, gate_w, wg, wu, wd):
        import jax, jax.numpy as jnp
        import numpy as np
        E = 64
        K = 8
        H = 256
        I = 96
        CAP = 64

        def _moe(hidden_states, gate_w, wg, wu, wd):
            B, S, Hd = hidden_states.shape
            x = hidden_states.reshape(-1, Hd)
            T = x.shape[0]
            logits = x @ gate_w.T
            probs = jax.nn.softmax(logits.astype(jnp.float32), axis=-1)
            w, sel = jax.lax.top_k(probs, K)
            w = w / jnp.sum(w, axis=-1, keepdims=True)
            w = w.astype(x.dtype)
            eid = sel.reshape(-1)
            tok = jnp.repeat(jnp.arange(T), K)
            oh = jax.nn.one_hot(eid, E, dtype=jnp.int32)
            pos = jnp.sum(jnp.cumsum(oh, axis=0) * oh, axis=-1) - 1
            valid = pos < CAP
            slot = jnp.where(valid, pos, CAP)
            xin = jnp.zeros((E, CAP + 1, Hd), x.dtype).at[eid, slot].set(x[tok])
            inp = xin[:, :CAP]
            h = jax.nn.silu(jnp.einsum('ech,ehi->eci', inp, wg)) * jnp.einsum('ech,ehi->eci', inp, wu)
            out = jnp.einsum('eci,eih->ech', h, wd)
            out_pad = jnp.concatenate([out, jnp.zeros((E, 1, Hd), out.dtype)], axis=1)
            g = out_pad[eid, slot] * (w.reshape(-1) * valid.astype(w.dtype))[:, None]
            y = jnp.zeros((T, Hd), x.dtype).at[tok].add(g)
            return y.reshape(B, S, Hd)
        return _moe(hidden_states, gate_w, wg, wu, wd)

    def _L1_xattn_ref(text_hidden, vision_tokens, vision_mask, Wq, Wk, Wv, Wo):
        import jax, jax.numpy as jnp
        import numpy as np
        N_HEADS = 16
        N_KV_HEADS = 8
        HEAD_DIM = 128
        D_TEXT = 256
        D_VISION = 128
        GROUPS = N_HEADS // N_KV_HEADS
        B, T_text, _ = text_hidden.shape
        T_vis = vision_tokens.shape[1]
        scale = jnp.float32(np.sqrt(HEAD_DIM))
        q = (text_hidden @ Wq).reshape(B, T_text, N_HEADS, HEAD_DIM).transpose(0, 2, 1, 3)
        k = (vision_tokens @ Wk).reshape(B, T_vis, N_KV_HEADS, HEAD_DIM).transpose(0, 2, 1, 3)
        v = (vision_tokens @ Wv).reshape(B, T_vis, N_KV_HEADS, HEAD_DIM).transpose(0, 2, 1, 3)
        k = jnp.repeat(k, GROUPS, axis=1)
        v = jnp.repeat(v, GROUPS, axis=1)
        scores = jnp.einsum('bhtd,bhsd->bhts', q, k) / scale
        mask = vision_mask[:, None, None, :]
        scores = jnp.where(mask, scores, -jnp.inf)
        attn = jax.nn.softmax(scores, axis=-1)
        attn = jnp.nan_to_num(attn, nan=0.0)
        out = jnp.einsum('bhts,bhsd->bhtd', attn, v)
        out = out.transpose(0, 2, 1, 3).reshape(B, T_text, N_HEADS * HEAD_DIM)
        return out @ Wo

    def _L1_ffn_ref(x, w1, b1, ln_g, ln_b, w2, b2):
        import jax, jax.numpy as jnp
        import numpy as np
        EPS = 1e-05

        def rms_norm(x):
            return x * jax.lax.rsqrt(jnp.mean(x * x, axis=-1, keepdims=True) + EPS)

        def act_quant(x):
            scale = 127.0 / jnp.clip(jnp.max(jnp.abs(x), axis=-1, keepdims=True), 1e-05)
            q = jnp.clip(jnp.round(x * scale), -128.0, 127.0) / scale
            return x + jax.lax.stop_gradient(q - x)

        def weight_quant(w):
            scale = 1.0 / jnp.clip(jnp.mean(jnp.abs(w)), 1e-05)
            q = jnp.clip(jnp.round(w * scale), -1.0, 1.0) / scale
            return w + jax.lax.stop_gradient(q - w)

        def bitlinear158(x, w, b):
            xq = act_quant(rms_norm(x))
            wq = weight_quant(w)
            return jnp.einsum('bsd,od->bso', xq, wq) + b

        def layer_norm(x, g, b):
            mu = jnp.mean(x, axis=-1, keepdims=True)
            var = jnp.mean((x - mu) ** 2, axis=-1, keepdims=True)
            return (x - mu) * jax.lax.rsqrt(var + EPS) * g + b
        h = jax.nn.silu(bitlinear158(x, w1, b1))
        h = jax.nn.gelu(h, approximate=False)
        h = layer_norm(h, ln_g, ln_b)
        return bitlinear158(h, w2, b2)
    x = x + jnp.tanh(g_xattn[0]) * _L0_xattn_ref(ctx_1024, _layernorm(x, axis=-1), L0_xattn_in_proj_w, L0_xattn_conv_w, L0_xattn_conv_b, L0_xattn_x_proj_w, L0_xattn_dt_proj_w, L0_xattn_dt_proj_b, L0_xattn_A_log, L0_xattn_D)
    x = x + jnp.tanh(g_ffn[0]) * _L0_ffn_ref(_layernorm(x, axis=-1), L0_ffn_gate_w, L0_ffn_wg, L0_ffn_wu, L0_ffn_wd)
    x = x + jnp.tanh(g_xattn[1]) * _L1_xattn_ref(_layernorm(x, axis=-1), ctx_1024, mask_BxS2_bf1, L1_xattn_Wq, L1_xattn_Wk, L1_xattn_Wv, L1_xattn_Wo)
    x = x + jnp.tanh(g_ffn[1]) * _L1_ffn_ref(_layernorm(x, axis=-1), L1_ffn_w1, L1_ffn_b1, L1_ffn_ln_g, L1_ffn_ln_b, L1_ffn_w2, L1_ffn_b2)
    return x

_drawn_inputs = setup_inputs


def setup_inputs(seed=0):
    import zlib

    import numpy as np

    out = dict(_drawn_inputs(seed))
    spreads = {'g_ffn': (-1.0, 0.6),
     'L0_xattn_D': (1.0, 0.6),
     'L1_ffn_b1': (0.0, 0.1),
     'L1_ffn_ln_g': (1.0, 0.57),
     'L1_ffn_ln_b': (0.0, 0.468),
     'L1_ffn_b2': (0.0, 0.1)}
    factors = {'L0_xattn_in_proj_w': 4.48,
     'L0_xattn_conv_w': 4.625,
     'L0_xattn_conv_b': 7.361,
     'L0_xattn_x_proj_w': 8.0,
     'L0_xattn_dt_proj_w': 8.0,
     'L0_xattn_dt_proj_b': 8.0,
     'L0_xattn_A_log': 8.0,
     'L0_ffn_gate_w': 8.0,
     'L0_ffn_wg': 8.0,
     'L0_ffn_wu': 8.0,
     'L0_ffn_wd': 8.0,
     'L1_xattn_Wq': 8.0,
     'L1_xattn_Wk': 8.0}
    for name, (base, spread) in spreads.items():
        noise = np.random.default_rng([zlib.crc32(name.encode()), seed]).standard_normal(out[name].shape)
        drawn = base * np.exp(spread * noise) if base else spread * noise
        out[name] = jnp.asarray(drawn.astype(out[name].dtype))
    for name, factor in factors.items():
        out[name] = (out[name] * factor).astype(out[name].dtype)
    return out
```

```python
from contextlib import ExitStack

import concourse.bass as bass
from concourse import mybir

ALU = mybir.AluOpType
ACT = mybir.ActivationFunctionType
AX = mybir.AxisListType
F32 = mybir.dt.float32
F32R = mybir.dt.float32r
BF16 = mybir.dt.bfloat16
I32 = mybir.dt.int32
U32 = mybir.dt.uint32
U8 = mybir.dt.uint8
P = 128


class Chain:

    def __init__(self, engine, sem):
        self.engine, self.sem, self.base, self.n = engine, sem, 0, 0

    def step(self, ins):
        self.n += 1
        ins.then_inc(self.sem, 1)

    def wait(self, back=0):
        self.engine.wait_ge(self.sem, self.base + self.n - back)

    def link(self, ins):
        self.step(ins)
        self.wait()

B, L, H, DM = 4, 256, 256, 128
NT = B * L // P
NS, NCONV, DTR = 16, 4, 8
DT = H // P
E, K, CAP, I = 64, 8, 64, 96
SLOTS = E * CAP
NH, NKV, DH = 16, 8, 128
FI = 1024
FT = FI // P
EPS = 1e-5
MAGIC = 12582912.0
GROUP = 4
RING = 4
NG = E // GROUP
NPAIR = E // 2
PAD = NCONV - 1
MASKED = -1e30


def build_program(nc, t, out):
    with ExitStack() as ctx:
        mamba_scope = ExitStack()

        def sb(name, shape, dt=F32, scope=ctx):
            return scope.enter_context(nc.sbuf_tensor(name, shape, dt))

        def sem(name):
            return ctx.enter_context(nc.semaphore(name))

        ps = ctx.enter_context(nc.psum_tensor("ps", [P, 8, 512], F32))

        xin = nc.dram_tensor("expert_in", (SLOTS, H), F32, kind="Internal").ap()
        eout = nc.dram_tensor("expert_out", (SLOTS + 1, H), F32, kind="Internal").ap()

        ident = sb("ident", [P, P])
        identb = sb("identb", [P, P], BF16)
        ones = sb("ones", [P, P])
        onesb = sb("onesb", [P, P], BF16)
        before = sb("before", [P, P], BF16)
        mhalf = sb("mhalf", [P, 8])
        x = sb("x", [P, NT, H])
        xn = sb("xn", [P, NT, H])
        ctxT = sb("ctxT", [P, B, PAD + L])
        ctx_tm = sb("ctx_tm", [P, NT, DM])
        gates = sb("gates", [P, 4])
        tg = sb("tg", [P, 4])
        stats = sb("stats", [P, NT, 6])
        mv = sb("mv", [P, NT, 2])
        ve = sb("ve", [P, NT])
        rstd = sb("rstd", [P, NT])
        idx_s = sb("idx_s", [P, NT * K], I32)
        idx_g = sb("idx_g", [P, NT * K], I32)
        wv = sb("wv", [P, NT * K])
        mbias = sb("mbias", [P, B, L], BF16)
        alive = sb("alive", [P, B])
        wgu = sb("wgu", [P, RING, 2, GROUP, 2 * I])
        wdn = sb("wdn", [P, RING, GROUP, H])
        gwT = sb("gwT", [P, 2, E])

        def msb(name, shape, dt=F32):
            return sb(name, shape, dt, mamba_scope)

        mk8 = msb("mk8", [P, B, L], U8)
        zeros = msb("zeros", [P, 8 * H])
        gw_nat = msb("gw_nat", [E, H])
        win = msb("win", [P, DT, DM])
        convw = msb("convw", [P, DT, NCONV])
        convb = msb("convb", [P, DT])
        xpw = msb("xpw", [DTR + 2 * NS, H])
        dtw = msb("dtw", [P, DT, DTR])
        dtb = msb("dtb", [P, DT])
        alog = msb("alog", [P, DT, NS])
        amat = msb("amat", [P, DT, NS])
        dskip = msb("dskip", [P, DT])
        wink = msb("wink", [P, DT, NCONV, DM])
        winT = msb("winT", [P, DT, NCONV, P])
        xpT = msb("xpT", [P, DT, P])
        dtwT = msb("dtwT", [P, H])
        u = msb("u", [P, DT, B * L])
        dtv = msb("dtv", [P, DT, B * L])
        du = msb("du", [P, DT, B * L])
        sz = msb("sz", [P, NT, L])
        nmr = msb("nmr", [P, NT])
        split = msb("split", [P, B * L], BF16)
        rest = msb("rest", [P, B * L])
        dtlow = msb("dtlow", [P, B * L])
        picks = msb("picks", [P, 32], BF16)
        sel = msb("sel", [P, 2 * NS, P], BF16)
        sp = [msb(f"sp{k}", [P, B * L]) for k in range(4)]
        dbu = msb("dbu", [P, 2, 512])
        hst = msb("hst", [P, 2, 512])
        hc = msb("hc", [P, 2, 512])
        yz = msb("yz", [P, DT, 512])
        xnT = msb("xnT", [P, 4, 2, P])
        iota_e = msb("iota_e", [P, E])
        iota_slot = msb("iota_slot", [P, E])
        nmax = msb("nmax", [P, 4])
        lsub = msb("lsub", [P, 4, E])
        pexp = msb("pexp", [P, 4, E])
        top8 = msb("top8", [P, 4, K])
        eid = msb("eid", [P, 4, K], U32)
        eidf = msb("eidf", [P, 4, K])
        left = msb("left", [P, 4, E])
        chosen = msb("chosen", [P, NT, E], BF16)
        wsum = msb("wsum", [P, 4])
        over = msb("over", [P, 4, E])
        slotv = msb("slotv", [P, 4, E])
        hot = msb("hot", [P, 4, K, E])
        slotk = msb("slotk", [P, 4, K])
        keep = msb("keep", [P, 4, K])
        slotg = msb("slotg", [P, 4, K])
        mamba_scope.close()

        mqk = [sb(f"mqk{k}", [P, NH, 2, DM], F32R) for k in range(2)]
        nvo = [sb(f"nvo{k}", [P, NH, H], F32R) for k in range(2)]
        w1T = sb("w1T", [P, 2, FI], BF16)
        w2T = sb("w2T", [P, FT, H], BF16)
        wmean = sb("wmean", [P, 2])
        wscale = sb("wscale", [P, 2])
        ebuf = sb("ebuf", [P, 8 * H])
        xe = ebuf[:, 0:4 * H].rearrange("p (a h) -> p a h", a=4)
        xeT = ebuf[:, 4 * H:6 * H].rearrange("p (a b c) -> p a b c", a=2, b=2)
        eo = ebuf[:, 6 * H:8 * H].rearrange("p (a h) -> p a h", a=2)
        w1 = ebuf[:].rearrange("p (a h) -> p a h", a=FT)
        sg = sb("sg", [I, 2, P])
        hT = sb("hT", [I, 2, P])

        prep_scope = ExitStack()

        def psb(name, shape, dt=F32):
            return sb(name, shape, dt, prep_scope)

        wq = psb("wq", [P, 2, NH * DH])
        wkv = psb("wkv", [P, 2, NKV * DH])
        wk, wvv, w2 = wkv[:, 0], wkv[:, 1], wkv
        wo = psb("wo", [P, NH, H])
        wqT = psb("wqT", [P, 2, 2, L])
        wkT = psb("wkT", [P, NKV, DM])
        wvT = psb("wvT", [P, NKV, DM])
        wabs = psb("wabs", [P, 2])
        wtern = psb("wtern", [P, 2 * FI], BF16)
        prep_scope.close()

        G = sb("G", [P, 2, K, H])
        xb = ebuf[:, 0:2 * H].rearrange("p (a h) -> p a h", a=2)
        mb = sb("mb", [P, L], BF16)
        spare = sb("spare", [P, 2])
        xnT3 = [sb(f"xnT3_{k}", [P, 2, L], F32R) for k in range(2)]
        cT = [sb(f"cT{k}", [P, L], F32R) for k in range(2)]
        cS = [sb(f"cS{k}", [P, 2, DM], F32R) for k in range(2)]
        qT = [sb(f"qT{k}", [P, 2, 2, L], F32R) for k in range(2)]
        sneg = ebuf[:, 2 * H:6 * H].rearrange("p (a b l) -> p a b l", a=2, b=2)
        smin = sb("smin", [P, 2, 2])
        pr = sb("pr", [P, 2, 2, L])
        psum_ = sb("psum_", [P, 2, 2])
        pinv = sb("pinv", [P, 2, 2])
        pn = sb("pn", [P, 2, 2, L])
        pT = [sb(f"pT{k}", [P, 2, 2, L], F32R) for k in range(2)]
        oT = [sb(f"oT{k}", [P, 2, L], F32R) for k in range(2)]
        flat_a = wgu[:].rearrange("p a b c d -> p (a b c d)")
        flat_b = wdn[:].rearrange("p a b c -> p (a b c)")
        hbuf = flat_a[:, 0:2 * FI].rearrange("p (a n) -> p a n", a=2)
        sqbuf = flat_a[:, 2 * FI:3 * FI]
        lng, lnb, b1v = (flat_a[:, k * FI:(k + 1) * FI] for k in (3, 4, 5))
        b2v = flat_b[:, 0:H]
        xq = flat_b[:, H:2 * H].bitcast(BF16)[:, 0:H]
        xqT = flat_b[:, 2 * H:3 * H].bitcast(BF16)[:, 0:H]
        hq = flat_b[:, 3 * H:5 * H].bitcast(BF16)
        hqT = flat_b[:, 5 * H:7 * H].bitcast(BF16)
        yb = flat_b[:, 7 * H:9 * H].rearrange("p (a n) -> p a n", a=2)
        fs = sb("fs", [P, 16])

        d_ctx, d_win, d_small, d_x = sem("d_ctx"), sem("d_win"), sem("d_small"), sem("d_x")
        d_zero, d_attn, d_ffn = sem("d_zero"), sem("d_attn"), sem("d_ffn")
        d_w = [sem(f"d_w{k}") for k in range(RING)]
        d_scat = [sem("d_scat0"), sem("d_scat1")]
        consts_ready, zeros_ready = sem("consts_ready"), sem("zeros_ready")
        pads_ready, wink_ready = sem("pads_ready"), sem("wink_ready")
        ctxT_in_psum, winT_in_psum, smallT_in_psum = sem("ctxT_in_psum"), sem("winT_in_psum"), sem("smallT_in_psum")
        ctxT_ready, winT_ready, smallT_ready = sem("ctxT_ready"), sem("winT_ready"), sem("smallT_ready")
        conv_done, u_ready = sem("conv_done"), sem("u_ready")
        xdbl_done, dtlow_ready, split_ready = sem("xdbl_done"), sem("dtlow_ready"), sem("split_ready")
        dtraw_done, sp_exp, sp_u, sp_ln, dt_ready = (sem("dtraw_done"), sem("sp_exp"), sem("sp_u"), sem("sp_ln"),
                                                     sem("dt_ready"))
        sel_ready, a_exp, a_ready = sem("sel_ready"), sem("a_exp"), sem("a_ready")
        ve_ready, rstd_ready = sem("ve_ready"), sem("rstd_ready")
        nmr_ready, sz_ready, tg_ready = sem("nmr_ready"), sem("sz_ready"), sem("tg_ready")
        da_zeroed = sem("da_zeroed")
        bc_ready, da_ready, dbu_ready = sem("bc_ready"), sem("da_ready"), sem("dbu_ready")
        scanned, hc_ready, y_added = sem("scanned"), sem("hc_ready"), sem("y_added")
        yz_ready, yT_ready, x1_ready = sem("yz_ready"), sem("yT_ready"), sem("x1_ready")
        xn_ready, xnT_in_psum, xnT_ready = sem("xn_ready"), sem("xnT_in_psum"), sem("xnT_ready")
        logits_ready, lsub_ready, pexp_ready = sem("logits_ready"), sem("lsub_ready"), sem("pexp_ready")
        chosen_ready, pos_ready, idx_ready = sem("chosen_ready"), sem("pos_ready"), sem("idx_ready")
        dve_steps, act_steps, pool_steps = sem("dve_steps"), sem("act_steps"), sem("pool_steps")
        d_out = [sem("d_out0"), sem("d_out1")]
        d_vec = sem("d_vec")
        d_xe = [sem(f"d_xe{k}") for k in range(4)]
        d_eo = [sem(f"d_eo{k}") for k in range(2)]
        kvT_in_psum, kvT_ready = sem("kvT_in_psum"), sem("kvT_ready")
        wqT_in_psum, wqT_ready = sem("wqT_in_psum"), sem("wqT_ready")
        mn_done, mn_hi, mn_ready = sem("mn_done"), sem("mn_hi"), sem("mn_ready")
        wabs_ready, wsum_done, wtern_ready = sem("wabs_ready"), sem("wsum_done"), sem("wtern_ready")
        wternT_in_psum, wternT_ready, mask_ready = sem("wternT_in_psum"), sem("wternT_ready"), sem("mask_ready")
        xeT_in_psum, xeT_ready, gu_done = sem("xeT_in_psum"), sem("xeT_ready"), sem("gu_done")
        sg_ready, hT_ready, down_done, eo_ready = sem("sg_ready"), sem("hT_ready"), sem("down_done"), sem("eo_ready")
        d_gath = [sem(f"d_gath{k}") for k in range(2)]
        combined, ve3_ready, rstd3_ready = sem("combined"), sem("ve3_ready"), sem("rstd3_ready")
        xn3_ready, xnT3_in_psum, xnT3_hi, xnT3_ready = (sem("xn3_ready"), sem("xnT3_in_psum"), sem("xnT3_hi"),
                                                        sem("xnT3_ready"))
        c_hi, c_ready = sem("c_hi"), sem("c_ready")
        q_done, q_hi, q_ready = sem("q_done"), sem("q_hi"), sem("q_ready")
        s_done, s_masked, p_exp, p_inv, p_ready = (sem("s_done"), sem("s_masked"), sem("p_exp"), sem("p_inv"),
                                                   sem("p_ready"))
        pT_in_psum, pT_hi, pT_ready = sem("pT_in_psum"), sem("pT_hi"), sem("pT_ready")
        av_done, o_hi, o_ready, o_added = sem("av_done"), sem("o_hi"), sem("o_ready"), sem("o_added")
        x3_ready = sem("x3_ready")
        f_ve, f_root, f_xn, f_sq = sem("f_ve"), sem("f_root"), sem("f_xn"), sem("f_sq")
        f_q, f_qT, f_qTr, f_h, f_hs, f_act = (sem("f_q"), sem("f_qT"), sem("f_qTr"), sem("f_h"), sem("f_hs"),
                                              sem("f_act"))
        f_hn, f_sq2, f_hq, f_hqT, f_hqTr, f_y, f_out = (sem("f_hn"), sem("f_sq2"), sem("f_hq"), sem("f_hqT"),
                                                        sem("f_hqTr"), sem("f_y"), sem("f_out"))
        mb_ready = sem("mb_ready")
        f_hs1, f_steps = sem("f_hs1"), sem("f_steps")
        comb_steps, ln_steps, inv_steps = sem("comb_steps"), sem("ln_steps"), sem("inv_steps")

        block = ctx.enter_context(nc.Block())

        def bank(k):
            return ps[:, k, :]

        def cols(ap, a, b):
            return ap[:, a:b]

        @block.sync
        def _(sp_):
            dma = sp_.dma_start
            dma(ctx_tm[:], t["ctx_1024"].rearrange("b (c p) d -> p (b c) d", p=P)).then_inc(d_ctx, 16)
            with nc.allow_non_contiguous_dma(reason="a few hundred values"):
                dma(win[:], t["L0_xattn_in_proj_w"].rearrange("(t p) d -> p t d", p=P)).then_inc(d_win, 16)
                dma(convw[:], t["L0_xattn_conv_w"].rearrange("(t p) a k -> p t (a k)", p=P)).then_inc(d_win, 16)
                dma(xpw[:], t["L0_xattn_x_proj_w"]).then_inc(d_small, 16)
                dma(dtw[:], t["L0_xattn_dt_proj_w"].rearrange("(t p) r -> p t r", p=P)).then_inc(d_small, 16)
                dma(gw_nat[:], t["L0_ffn_gate_w"]).then_inc(d_small, 16)
                dma(convb[:], t["L0_xattn_conv_b"].rearrange("(t p) -> p t", p=P)).then_inc(d_small, 16)
                dma(dtb[:], t["L0_xattn_dt_proj_b"].rearrange("(t p) -> p t", p=P)).then_inc(d_small, 16)
                dma(dskip[:], t["L0_xattn_D"].rearrange("(t p) -> p t", p=P)).then_inc(d_small, 16)
                dma(alog[:], t["L0_xattn_A_log"].rearrange("(t p) n -> p t n", p=P)).then_inc(d_small, 16)
                dma(gates[:, 0:2], t["g_xattn"].partition_broadcast(P)).then_inc(d_small, 16)
                dma(gates[:, 2:4], t["g_ffn"].partition_broadcast(P)).then_inc(d_small, 16)
            dma(x[:], t["x"].rearrange("b (c p) h -> p (b c) h", p=P)).then_inc(d_x, 16)
            dma(mk8[:].rearrange("p b l -> p (b l)"),
                t["mask"].rearrange("b l -> (b l)").partition_broadcast(P)).then_inc(d_small, 16)
            sp_.wait_ge(zeros_ready, 1)
            for k in range(4):
                dma(xin[1024 * k:1024 * (k + 1)].rearrange("(p r) h -> p (r h)", p=P), zeros[:]).then_inc(d_zero, 16)
            dma(eout[SLOTS:SLOTS + 1], zeros[0:1, 0:H]).then_inc(d_zero, 16)

            def weights(group, slot, wait):
                if wait is not None:
                    sp_.wait_ge(down_done, wait)
                es = slice(group * GROUP, group * GROUP + GROUP) if isinstance(group, int) else \
                    bass.ds(group * GROUP, GROUP)
                for k, name in enumerate(("L0_ffn_wg", "L0_ffn_wu")):
                    dma(wgu[:, slot, k], t[name][es].rearrange("e (p j) i -> p e (j i)", j=2)).then_inc(d_w[slot], 16)
                dma(wdn[0:I, slot], t["L0_ffn_wd"][es].rearrange("e i h -> i e h")).then_inc(d_w[slot], 16)

            for g in range(RING):
                weights(g, g, None)
            sp_.wait_ge(idx_ready, 2)
            dma(wk, t["L1_xattn_Wk"]).then_inc(d_attn, 16)
            dma(wvv, t["L1_xattn_Wv"]).then_inc(d_attn, 16)
            dma(wq[:], t["L1_xattn_Wq"].rearrange("(j p) n -> p j n", p=P)).then_inc(d_attn, 16)
            dma(wo[:], t["L1_xattn_Wo"].rearrange("(h p) n -> p h n", p=P)).then_inc(d_attn, 16)
            dma(w1, t["L1_ffn_w1"].rearrange("(c p) h -> p c h", p=P)).then_inc(d_ffn, 16)
            sp_.wait_ge(kvT_in_psum, 4)
            dma(w2[:], t["L1_ffn_w2"].rearrange("(c p) n -> p c n", p=P)).then_inc(d_ffn, 16)
            sp_.wait_ge(d_scat[0], 16 * 32)
            sp_.wait_ge(d_scat[1], 16 * 32)
            sp_.wait_ge(wtern_ready, 1)

            def rows(p, j, wait):
                if wait is not None:
                    sp_.wait_ge(xeT_in_psum, wait)
                at = slice(P * p, P * p + P) if isinstance(p, int) else bass.ds(P * p, P)
                dma(xe[:, j % 4], xin[at]).then_inc(d_xe[j % 4], 16)

            for p in range(4):
                rows(p, p, None)

            def feed(r, last):
                for j in range(8):
                    if not (last and j >= 4):
                        rows(8 * r + j + 4, j + 4, 8 * r + j + 1)
                    if j % 2 and not last:
                        weights(4 * r + j // 2 + 4, j // 2, 8 * r + j + 1)

            with sp_.Fori(0, NPAIR // 8 - 1) as r:
                feed(r, False)
            feed(NPAIR // 8 - 1, True)
            sp_.wait_ge(down_done, NPAIR)
            for dst, name in ((b1v, "L1_ffn_b1"), (lng, "L1_ffn_ln_g"), (lnb, "L1_ffn_ln_b"), (b2v, "L1_ffn_b2")):
                dma(dst, t[name].partition_broadcast(P)).then_inc(d_vec, 16)
            out_rows = out.rearrange("b (c p) h -> (b c) p h", p=P)

            def store(c, k):
                sp_.wait_ge(f_out, c + 1)
                dst = out_rows[c] if isinstance(c, int) else \
                    out_rows[bass.ds(c, 1)].rearrange("a p h -> (a p) h")
                dma(dst, yb[:, k, :]).then_inc(d_out[k], 16)

            with sp_.Fori(0, NT // 2) as r:
                for k in range(2):
                    store(2 * r + k, k)
            for k in range(2):
                sp_.wait_ge(d_out[k], 16 * (NT // 2))
                sp_.wait_ge(d_eo[k], 16 * (NPAIR // 2))
            sp_.wait_ge(d_zero, 80)

        @block.gpsimd
        def _(pool):
            chain = Chain(pool, pool_steps)
            nc.gpsimd.memset(ident[:], 0.0).then_inc(pool_steps, 1)
            nc.gpsimd.memset(ones[:], 1.0).then_inc(pool_steps, 1)
            nc.gpsimd.memset(onesb[:], 1.0).then_inc(pool_steps, 1)
            nc.gpsimd.memset(picks[:], 0.0).then_inc(pool_steps, 1)
            chain.n = 4
            chain.wait()
            chain.link(nc.gpsimd.affine_select(out=ident[:], in_=ident[:], compare_op=ALU.not_equal, fill=1.0, base=0,
                                               pattern=[[-1, P]], channel_multiplier=1))
            nc.gpsimd.tensor_copy(identb[:], ident[:]).then_inc(consts_ready, 1)
            nc.gpsimd.affine_select(out=before[:], in_=onesb[:], compare_op=ALU.is_gt, fill=0.0, base=0,
                                    pattern=[[1, P]], channel_multiplier=-1).then_inc(consts_ready, 1)
            nc.gpsimd.memset(mhalf[:], -0.5).then_inc(consts_ready, 1)
            for part in (0, 64, 96):
                chain.link(nc.gpsimd.affine_select(out=picks[:], in_=picks[:], compare_op=ALU.not_equal, fill=1.0,
                                                   base=-part, pattern=[[-1, 32]], channel_multiplier=1))
            nc.gpsimd.tensor_copy(sel[:], picks[:].unsqueeze(2).to_broadcast([P, 32, P])).then_inc(sel_ready, 1)
            nc.gpsimd.iota(iota_e[:], [[1, E]], base=0, channel_multiplier=0,
                           allow_small_or_imprecise_dtypes=True).then_inc(consts_ready, 1)
            nc.gpsimd.iota(iota_slot[:], [[CAP, E]], base=0, channel_multiplier=0,
                           allow_small_or_imprecise_dtypes=True).then_inc(consts_ready, 1)
            pool.wait_ge(consts_ready, 3)
            pool.wait_ge(ve_ready, 1)
            nc.gpsimd.tensor_tensor(rstd[:], ve[:], mhalf[:], ALU.pow).then_inc(rstd_ready, 1)
            pool.wait_ge(d_zero, 80)
            for hb in range(2):
                pool.wait_ge(ve_ready, 2 + hb)
                nc.gpsimd.tensor_tensor(rstd[:, 4 * hb:4 * hb + 4], ve[:, 4 * hb:4 * hb + 4], mhalf[:, 0:4],
                                        ALU.pow).then_inc(rstd_ready, 1)
                pool.wait_ge(idx_ready, hb + 1)
                pool.wait_ge(xn_ready, 4 * (hb + 1))
                for c in range(4 * hb, 4 * hb + 4):
                    for k in range(K):
                        nc.gpsimd.indirect_dma_start(
                            xin, bass.IndirectOffsetOnAxis(ap=idx_s[:, c * K + k:c * K + k + 1], axis=0),
                            xn[:, c, :], None, bounds_check=SLOTS - 1, oob_is_err=False).then_inc(d_scat[hb], 16)

            def put(p, j):
                pool.wait_ge(eo_ready, p + 1)
                at = slice(P * p, P * p + P) if isinstance(p, int) else bass.ds(P * p, P)
                pool.dma_start(eout[at], eo[:, j % 2]).then_inc(d_eo[j % 2], 16)

            with pool.Fori(0, NPAIR // 2) as r:
                for j in range(2):
                    put(2 * r + j, j)
            for k in range(2):
                pool.wait_ge(d_eo[k], 16 * (NPAIR // 2))
            pool.wait_ge(mn_ready, 2 * NKV)
            pool.wait_ge(wternT_ready, 4)
            for b in range(B):
                if b:
                    pool.wait_ge(combined, 2 * b)
                for cc in range(2):
                    for k in range(K):
                        at = (2 * b + cc) * K + k
                        nc.gpsimd.indirect_dma_start(
                            G[:, cc, k, :], None, eout, bass.IndirectOffsetOnAxis(ap=idx_g[:, at:at + 1], axis=0),
                            bounds_check=SLOTS, oob_is_err=False).then_inc(d_gath[cc], 16)
                pool.wait_ge(ve3_ready, b + 1)
                nc.gpsimd.tensor_tensor(rstd[:, 2 * b:2 * b + 2], ve[:, 2 * b:2 * b + 2], mhalf[:, 0:2], ALU.pow)\
                    .then_inc(rstd3_ready, 1)
                for i in range(NH * b, NH * b + NH):
                    pool.wait_ge(p_inv, i + 1)
                    if i > 1:
                        pool.wait_ge(pT_in_psum, i - 1)
                    for tt in range(2):
                        last = nc.gpsimd.tensor_scalar(pn[:, i % 2, tt, :], pr[:, i % 2, tt, :],
                                                       pinv[:, i % 2, tt:tt + 1], 1.0, ALU.mult, ALU.mult)
                    last.then_inc(p_ready, 1)
            with pool.Fori(0, NT) as c:
                for k, at in enumerate((0, 1, 2, 1)):
                    pool.wait_ge(f_ve, 4 * c + k + 1)
                    nc.gpsimd.tensor_tensor(fs[:, 4 + at:5 + at], fs[:, at:at + 1], mhalf[:, 0:1], ALU.pow)\
                        .then_inc(f_root, 1)

        @block.scalar
        def _(act):
            chain = Chain(act, act_steps)
            A = nc.scalar.activation
            act.wait_ge(pads_ready, 1)
            for k in range(2):
                act.wait_ge(ctxT_in_psum, k + 1)
                A(ctxT[:, 2 * k:2 * k + 2, PAD:], bank(k).rearrange("p (b l) -> p b l", b=2), ACT.Copy)\
                    .then_inc(ctxT_ready, 1)
            for d in range(DT):
                act.wait_ge(winT_in_psum, d + 1)
                A(winT[:, d], bank(2 + d).rearrange("p (k e) -> p k e", k=NCONV), ACT.Copy).then_inc(winT_ready, 1)
            act.wait_ge(d_small, 160)
            for d in range(DT):
                for hb in range(2):
                    act.wait_ge(conv_done, 2 * d + hb + 1)
                    A(u[:, d, 512 * hb:512 * hb + 512], bank(2 * d + hb), ACT.Silu,
                      bias=convb[:, d:d + 1]).then_inc(u_ready, 1)
            act.wait_ge(nmr_ready, 1)
            act.wait_ge(rstd_ready, 1)
            for c in range(NT):
                last = A(sz[:, c, :], x[:, c, :], ACT.Silu, scale=rstd[:, c:c + 1], bias=nmr[:, c:c + 1])
            last.then_inc(sz_ready, 1)
            A(tg[:], gates[:], ACT.Tanh).then_inc(tg_ready, 1)
            A(amat[:], alog[:], ACT.Exp).then_inc(a_exp, 1)
            for d in range(DT):
                act.wait_ge(dtraw_done, 2 * d + 2)
                chain.link(A(sp[2 * d][:], ps[:, 2 * d:2 * d + 2, :].rearrange("p a b -> p (a b)"), ACT.Abs,
                             bias=dtb[:, d:d + 1]))
                A(sp[2 * d + 1][:], sp[2 * d][:], ACT.Exp, scale=-1.0).then_inc(sp_exp, 1)
            for d in range(DT):
                act.wait_ge(sp_u, d + 1)
                A(dtv[:, d], sp[2 * d][:], ACT.Ln).then_inc(sp_ln, 1)

            act.wait_ge(a_ready, 1)
            act.wait_ge(dt_ready, 2)
            act.wait_ge(da_zeroed, 1)

            def decays(hb, m):
                for j in range(4):
                    n, d = 2 * m + j // 2, j % 2
                    if hb > 0 or isinstance(m, int) is False or m > 0 or j > 1:
                        act.wait_ge(scanned, 32 * hb + 4 * m + j - 1)
                    scale = amat[:, d, n:n + 1] if isinstance(m, int) else amat[:, d, bass.ds(n, 1)]
                    A(bank(d).rearrange("p (b l) -> p b l", b=2)[:, :, 1:],
                      dtv[:, d, 512 * hb:512 * hb + 512].rearrange("p (b l) -> p b l", b=2)[:, :, 1:],
                      ACT.Exp, scale=scale).then_inc(da_ready, 1)

            for hb in range(2):
                decays(hb, 0)
                with act.Fori(1, NS // 2) as m:
                    decays(hb, m)
                act.wait_ge(xnT_in_psum, hb + 1)
                for k in range(2):
                    A(xnT[:, 2 * k:2 * k + 2].rearrange("p a b c -> p (a b c)"), bank(6 + k), ACT.Copy)\
                        .then_inc(xnT_ready, 1)
                act.wait_ge(lsub_ready, hb + 1)
                A(pexp[:], lsub[:], ACT.Exp).then_inc(pexp_ready, 1)


            for k in range(4):
                act.wait_ge(kvT_in_psum, k + 1)
                dst = (wkT, wvT)[k // 2]
                A(dst[:, 4 * (k % 2):4 * (k % 2) + 4, :].rearrange("p a b -> p (a b)"), bank(k), ACT.Copy)\
                    .then_inc(kvT_ready, 1)
            for g in range(NKV):
                act.wait_ge(wqT_in_psum, g + 1)
                if g > 1:
                    act.wait_ge(mn_done, 2 * g - 3)
                A(wqT[:, g % 2].rearrange("p a b -> p (a b)"), bank(4 + g % 2), ACT.Copy).then_inc(wqT_ready, 1)
                for k, dst in enumerate((mqk, nvo)):
                    act.wait_ge(mn_done, 2 * g + k + 1)
                    A(dst[0][:, 2 * g:2 * g + 2].rearrange("p a b c -> p (a b c)" if k == 0 else "p a b -> p (a b)"),
                      bank(6 + k), ACT.Copy).then_inc(mn_hi, 1)
            for k in range(4):
                act.wait_ge(wternT_in_psum, k + 1)
                dst = w1T[:, k, :] if k < 2 else w2T[:, 4 * k - 8:4 * k - 4, :].rearrange("p a b -> p (a b)")
                A(dst, bank(k).bitcast(BF16), ACT.Copy).then_inc(wternT_ready, 1)

            def turn(p, j):
                act.wait_ge(xeT_in_psum, p + 1)
                if not isinstance(p, int) or p > 1:
                    act.wait_ge(gu_done, p - 1)
                A(xeT[:, j % 2].rearrange("p a b -> p (a b)"), bank(j % 2)[:, 0:2 * P], ACT.Copy).then_inc(xeT_ready, 1)

            def gate(p, j):
                act.wait_ge(gu_done, p + 1)
                if not isinstance(p, int) or p > 1:
                    act.wait_ge(hT_ready, p - 1)
                A(sg[:, j % 2, :], ps[0:I, 2 + j % 2, 0:P], ACT.Silu).then_inc(sg_ready, 1)

            turn(0, 0)
            turn(1, 1)
            gate(0, 0)
            turn(2, 0)
            gate(1, 1)
            turn(3, 1)
            gate(2, 0)
            with act.Fori(1, NPAIR // 2 - 1) as r:
                for j in range(2):
                    turn(2 * r + j + 2, j)
                    gate(2 * r + j + 1, j + 1)
            gate(NPAIR - 1, 1)

            def split_hi(b):
                if not isinstance(b, int) or b:
                    act.wait_ge(o_added, NH * b)
                src = ctxT[:, b, PAD:] if isinstance(b, int) else \
                    ctxT[:, bass.ds(b, 1), PAD:].rearrange("p a l -> p (a l)")
                A(cT[0][:], src, ACT.Copy).then_inc(c_hi, 1)
                A(cS[0][:], ctx_tm[:, bass.ds(2 * b, 2), :], ACT.Copy).then_inc(c_hi, 1)
                act.wait_ge(xnT3_in_psum, b + 1)
                A(xnT3[0][:].rearrange("p a b -> p (a b)"), bank(0), ACT.Copy).then_inc(xnT3_hi, 1)

            def q_high(b, hp):
                i = 8 * b + hp
                act.wait_ge(q_done, i + 1)
                if not isinstance(b, int) or b or hp > 1:
                    act.wait_ge(s_done, 2 * i - 2)
                A(qT[0][:, hp % 2].rearrange("p a b -> p (a b)"), bank(0), ACT.Copy).then_inc(q_hi, 1)

            def exps(b, h):
                i = NH * b + h
                act.wait_ge(s_masked, i + 1)
                if not isinstance(b, int) or b or h > 1:
                    act.wait_ge(p_ready, i - 1)
                for tt in range(2):
                    last = A(pr[:, h % 2, tt, :], sneg[:, h % 2, tt, :], ACT.Exp, scale=-1.0,
                             bias=smin[:, h % 2, tt:tt + 1], accum_out=psum_[:, h % 2, tt:tt + 1])
                last.then_inc(p_exp, 1)

            def pT_high(b, h):
                i = NH * b + h
                act.wait_ge(pT_in_psum, i + 1)
                if not isinstance(b, int) or b or h > 1:
                    act.wait_ge(av_done, i - 1)
                A(pT[0][:, h % 2].rearrange("p a b -> p (a b)"), bank(3 + h % 2), ACT.Copy).then_inc(pT_hi, 1)

            def o_high(b, h):
                i = NH * b + h
                act.wait_ge(av_done, i + 1)
                if not isinstance(b, int) or b or h > 1:
                    act.wait_ge(o_added, i - 1)
                A(oT[0][:, h % 2], bank(5)[:, 0:L], ACT.Copy).then_inc(o_hi, 1)

            def attend(b):
                split_hi(b)
                q_high(b, 0)
                for h in range(NH + 2):
                    if h % 2 == 1 and h // 2 + 1 < NH // 2:
                        q_high(b, h // 2 + 1)
                    if h < NH:
                        exps(b, h)
                    if 1 <= h <= NH:
                        pT_high(b, h - 1)
                    if h >= 2:
                        o_high(b, h - 2)

            attend(0)
            with act.Fori(1, B) as b:
                attend(b)

            def ffn(c, k):
                act.wait_ge(f_xn, c + 1)
                A(sqbuf[:, 0:H], xn[:, k, :], ACT.Square, accum_out=fs[:, 8:9]).then_inc(f_sq, 1)
                act.wait_ge(f_qT, c + 1)
                A(xqT, bank(0).bitcast(BF16)[:, 0:H], ACT.Copy).then_inc(f_qTr, 1)
                act.wait_ge(f_h, c + 1)
                A(hbuf[:, k, :], hbuf[:, k, :], ACT.Silu).then_inc(f_hs, 1)
                act.wait_ge(f_hs, c + 1)
                A(hbuf[:, k, :], hbuf[:, k, :], ACT.Gelu).then_inc(f_act, 1)
                act.wait_ge(f_hn, c + 1)
                A(sqbuf, hbuf[:, k, :], ACT.Square, accum_out=fs[:, 9:10]).then_inc(f_sq2, 1)
                act.wait_ge(f_hqT, c + 1)
                A(hqT, bank(3).bitcast(BF16), ACT.Copy).then_inc(f_hqTr, 1)

            with act.Fori(0, NT // 2) as r:
                for k in range(2):
                    ffn(2 * r + k, k)

        @block.tensor
        def _(pe):
            pe.wait_ge(consts_ready, 1)
            pe.wait_ge(d_ctx, 16)
            for k in range(2):
                for j in range(4):
                    last = pe.transpose(ps[:, k, P * j:P * j + P], ctx_tm[:, 4 * k + j, :], ident[:])
                last.then_inc(ctxT_in_psum, 1)
            for d in range(DT):
                pe.wait_ge(wink_ready, d + 1)
                for k in range(NCONV):
                    last = pe.transpose(ps[:, 2 + d, P * k:P * k + P], wink[:, d, k, :], ident[:])
                last.then_inc(winT_in_psum, 1)
            pe.wait_ge(d_small, 160)
            n_x = DTR + 2 * NS
            for d in range(DT):
                pe.transpose(ps[:, 4, n_x * d:n_x * d + n_x], xpw[:, P * d:P * d + P], ident[0:n_x, 0:n_x])
            for d in range(DT):
                pe.transpose(ps[0:DTR, 5, P * d:P * d + P], dtw[:, d, :], ident[:])
            for d in range(2):
                last = pe.transpose(ps[:, 6, E * d:E * d + E], gw_nat[:, P * d:P * d + P], ident[0:E, 0:E])
            last.then_inc(smallT_in_psum, 1)
            for d in range(DT):
                for hb in range(2):
                    pe.wait_ge(ctxT_ready, 2)
                    pe.wait_ge(winT_ready, 2)
                    for k in range(NCONV):
                        last = pe.matmul(bank(2 * d + hb), winT[:, d, k, :], ctxT[:, 2 * hb:2 * hb + 2, k:k + L],
                                         start=(k == 0), stop=(k == NCONV - 1))
                    last.then_inc(conv_done, 1)
            pe.wait_ge(smallT_ready, 1)
            for hb in range(2):
                for d in range(DT):
                    pe.wait_ge(u_ready, 2 * d + hb + 1)
                    last = pe.matmul(bank(4 + hb), xpT[:, d, :], u[:, d, 512 * hb:512 * hb + 512],
                                     start=(d == 0), stop=(d == 1))
                last.then_inc(xdbl_done, 1)
            pe.wait_ge(dtlow_ready, 1)
            pe.wait_ge(u_ready, 4)
            for d in range(DT):
                for hb in range(2):
                    pe.matmul(bank(2 * d + hb), dtwT[32:32 + DTR, P * d:P * d + P],
                              dtlow[32:32 + DTR, 512 * hb:512 * hb + 512], start=True, stop=True)\
                        .then_inc(dtraw_done, 1)
            pe.wait_ge(sel_ready, 1)
            pe.wait_ge(split_ready, 1)

            def spread(hb, n, parity):
                for k, row in ((4, n), (6, NS + n)):
                    pick = sel[:, row, :] if isinstance(row, int) else \
                        sel[:, bass.ds(row, 1), :].rearrange("p a m -> p (a m)")
                    last = pe.matmul(bank(k + parity), pick, split[:, 512 * hb:512 * hb + 512], start=True, stop=True)
                last.then_inc(bc_ready, 1)

            def add_states(hb, m, first, last_turn):
                for j in range(4):
                    i = 32 * hb + 4 * m + j
                    pe.wait_ge(hc_ready, i + 1)
                    pe.matmul(bank(2 + j % 2), ident[:], hc[:, j % 2, :], start=(first and j < 2),
                              stop=(last_turn and j > 1)).then_inc(y_added, 1)
                    if j % 2 and not last_turn:
                        spread(hb, 2 * m + 2 + j // 2, j // 2)

            for hb in range(2):
                if hb:
                    pe.wait_ge(x1_ready, 1)
                    pe.wait_ge(pos_ready, 1)
                    pe.wait_ge(idx_ready, 1)
                    pe.wait_ge(yz_ready, 1)
                    pe.wait_ge(xnT_ready, 2)
                pe.wait_ge(dt_ready, 2)
                spread(hb, 0, 0)
                spread(hb, 1, 1)
                add_states(hb, 0, True, False)
                with pe.Fori(1, NS // 2 - 1) as m:
                    add_states(hb, m, False, False)
                add_states(hb, NS // 2 - 1, False, True)
                pe.wait_ge(yz_ready, hb + 1)
                for b in range(2):
                    for lt in range(2):
                        for d in range(DT):
                            last = pe.transpose(ps[:, 4 + b, H * lt + P * d:H * lt + P * d + P],
                                                yz[:, d, L * b + P * lt:L * b + P * lt + P], ident[:])
                last.then_inc(yT_ready, 1)
                for c in range(4):
                    pe.wait_ge(xn_ready, 4 * hb + c + 1)
                    for d in range(2):
                        last = pe.transpose(ps[:, 6 + c // 2, H * (c % 2) + P * d:H * (c % 2) + P * d + P],
                                            xn[:, 4 * hb + c, P * d:P * d + P], ident[:])
                last.then_inc(xnT_in_psum, 1)
                pe.wait_ge(xnT_ready, 2 * hb + 2)
                pe.wait_ge(x1_ready, hb + 1)
                for c in range(4):
                    for d in range(2):
                        last = pe.matmul(ps[:, 4, E * c:E * c + E], xnT[:, c, d, :], gwT[:, d, :],
                                         start=(d == 0), stop=(d == 1))
                last.then_inc(logits_ready, 1)
                pe.wait_ge(consts_ready, 2)
                pe.wait_ge(chosen_ready, hb + 1)
                for c in range(4):
                    for e in range(4 * hb + c + 1):
                        same = e == 4 * hb + c
                        last = pe.matmul(ps[:, 5, E * c:E * c + E], (before if same else onesb)[:], chosen[:, e, :],
                                         start=(e == 0), stop=same)
                last.then_inc(pos_ready, 1)


            pe.wait_ge(d_attn, 64)
            for k in range(4):
                src = (wk, wvv)[k // 2]
                for j in range(4):
                    at = P * (4 * (k % 2) + j)
                    last = pe.transpose(ps[:, k, P * j:P * j + P], src[:, at:at + P], ident[:])
                last.then_inc(kvT_in_psum, 1)

            def turn_wq(g):
                if g > 1:
                    pe.wait_ge(wqT_ready, g - 1)
                for hh in range(2):
                    for j in range(2):
                        last = pe.transpose(ps[:, 4 + g % 2, L * hh + P * j:L * hh + P * j + P],
                                            wq[:, j, P * (2 * g + hh):P * (2 * g + hh) + P], ident[:])
                last.then_inc(wqT_in_psum, 1)

            turn_wq(0)
            pe.wait_ge(kvT_ready, 4)
            for g in range(NKV):
                if g + 1 < NKV:
                    turn_wq(g + 1)
                pe.wait_ge(wqT_ready, g + 1)
                if g:
                    pe.wait_ge(mn_ready, 2 * g - 1)
                for hh in range(2):
                    for j in range(2):
                        last = pe.matmul(ps[:, 6, L * hh + P * j:L * hh + P * j + P],
                                         wqT[:, g % 2, hh, P * j:P * j + P], wkT[:, g, :], start=True, stop=True)
                last.then_inc(mn_done, 1)
                if g:
                    pe.wait_ge(mn_ready, 2 * g)
                for hh in range(2):
                    last = pe.matmul(ps[:, 7, L * hh:L * hh + L], wvT[:, g, :], wo[:, 2 * g + hh, :],
                                     start=True, stop=True)
                last.then_inc(mn_done, 1)
            pe.wait_ge(wabs_ready, 1)
            pe.matmul(ps[:, 0, 0:2], ones[:], wabs[:], start=True, stop=True).then_inc(wsum_done, 1)
            for k in range(4):
                if k % 2 == 0:
                    pe.wait_ge(wtern_ready, k // 2 + 1)
                for j in range(8):
                    if k < 2:
                        src, at = wtern[:, H * j + P * k:H * j + P * k + P], P * j
                    else:
                        src = wtern[:, FI * (j % 2) + P * (4 * (k - 2) + j // 2):][:, 0:P]
                        at = H * (j // 2) + P * (j % 2)
                    last = pe.transpose(bank(k).bitcast(BF16)[:, at:at + P], src, identb[:])
                last.then_inc(wternT_in_psum, 1)

            def turn_rows(p, j):
                pe.wait_ge(d_xe[j % 4], 16 * (p // 4 + 1) if isinstance(p, int) else 4 * (p - j % 4) + 16)
                if not isinstance(p, int) or p > 1:
                    pe.wait_ge(xeT_ready, p - 1)
                for k in range(2):
                    last = pe.transpose(ps[:, j % 2, P * k:P * k + P], xe[:, j % 4, k::2], ident[:])
                last.then_inc(xeT_in_psum, 1)

            def gate_up(p, j, r):
                slot = j // 2 % 4
                if j % 2 == 0:
                    pe.wait_ge(d_w[slot], 48 * r + 48)
                pe.wait_ge(xeT_ready, p + 1)
                if not isinstance(p, int) or p > 1:
                    pe.wait_ge(hT_ready, p - 1)
                for w in range(2):
                    for e in range(2):
                        for k in range(2):
                            last = pe.matmul(ps[0:I, 2 + j % 2, P * w + CAP * e:P * w + CAP * e + CAP],
                                             wgu[:, slot, w, 2 * (j % 2) + e, I * k:I * k + I],
                                             xeT[:, j % 2, k, CAP * e:CAP * e + CAP], start=(k == 0), stop=(k == 1))
                last.then_inc(gu_done, 1)

            def down(p, j):
                slot = j // 2 % 4
                pe.wait_ge(hT_ready, p + 1)
                if not isinstance(p, int) or p > 1:
                    pe.wait_ge(eo_ready, p - 1)
                for e in range(2):
                    last = pe.matmul(ps[CAP * e:CAP * e + CAP, 4 + j % 2, 0:H], hT[:, j % 2, CAP * e:CAP * e + CAP],
                                     wdn[0:I, slot, 2 * (j % 2) + e, :], start=True, stop=True)
                last.then_inc(down_done, 1)

            def expert_turn(r, first, last):
                for j in range(8):
                    if not (last and j == 7):
                        turn_rows(8 * r + j + 1, j + 1)
                    gate_up(8 * r + j, j, r)
                    if not (first and j == 0):
                        down(8 * r + j - 1, (j - 1) % 8)

            pe.wait_ge(wternT_ready, 4)
            pe.wait_ge(mn_ready, 2 * NKV)
            turn_rows(0, 0)
            expert_turn(0, True, False)
            with pe.Fori(1, NPAIR // 8 - 1) as r:
                expert_turn(r, False, False)
            expert_turn(NPAIR // 8 - 1, False, True)
            down(NPAIR - 1, 7)

            def mm3(o, lhs, rhs, start, stop):
                pe.matmul(o, lhs[0], rhs[0], start=start, stop=False)
                pe.matmul(o, lhs[0], rhs[1], start=False, stop=False)
                return pe.matmul(o, lhs[1], rhs[0], start=False, stop=stop)

            def turn_xn3(b):
                pe.wait_ge(xn3_ready, b + 1)
                if not isinstance(b, int) or b:
                    pe.wait_ge(q_ready, 8 * b)
                else:
                    pe.wait_ge(eo_ready, NPAIR)
                for j in range(2):
                    for cc in range(2):
                        last = pe.transpose(ps[:, 0, L * j + P * cc:L * j + P * cc + P],
                                            xn[:, cc, P * j:P * j + P], ident[:])
                last.then_inc(xnT3_in_psum, 1)

            def queries(b, hp):
                i = 8 * b + hp
                if hp == 0:
                    pe.wait_ge(xnT3_ready, b + 1)
                else:
                    pe.wait_ge(q_ready, i)
                for hh in range(2):
                    for j in range(2):
                        last = mm3(ps[:, 0, L * hh:L * hh + L], [m[:, 2 * hp + hh, j, :] for m in mqk],
                                   [v[:, j, :] for v in xnT3], j == 0, j == 1)
                last.then_inc(q_done, 1)

            def scores(b, h):
                i = NH * b + h
                if h % 2 == 0:
                    pe.wait_ge(q_ready, 8 * b + h // 2 + 1)
                if h == 0:
                    pe.wait_ge(c_ready, b + 1)
                if not isinstance(b, int) or b or h > 1:
                    pe.wait_ge(s_masked, i - 1)
                for tt in range(2):
                    last = mm3(ps[:, 1 + h % 2, L * tt:L * tt + L],
                               [q[:, h // 2 % 2, h % 2, P * tt:P * tt + P] for q in qT], [v[:] for v in cT], True, True)
                last.then_inc(s_done, 1)

            def turn_p(b, h):
                i = NH * b + h
                pe.wait_ge(p_ready, i + 1)
                if not isinstance(b, int) or b or h > 1:
                    pe.wait_ge(pT_ready, i - 1)
                for st in range(2):
                    for tt in range(2):
                        last = pe.transpose(ps[:, 3 + h % 2, L * st + P * tt:L * st + P * tt + P],
                                            pn[:, h % 2, tt, P * st:P * st + P], ident[:])
                last.then_inc(pT_in_psum, 1)

            def values(b, h):
                i = NH * b + h
                pe.wait_ge(pT_ready, i + 1)
                if not isinstance(b, int) or b or h:
                    pe.wait_ge(o_ready, i)
                for st in range(2):
                    last = mm3(ps[:, 5, 0:L], [v[:, st, :] for v in cS], [v[:, h % 2, st, :] for v in pT],
                               st == 0, st == 1)
                last.then_inc(av_done, 1)

            def project(b, h):
                i = NH * b + h
                pe.wait_ge(o_ready, i + 1)
                if h == 0 and (not isinstance(b, int) or b):
                    pe.wait_ge(x3_ready, b)
                for tt in range(2):
                    last = mm3(ps[:, 6 + tt, 0:H], [v[:, h % 2, P * tt:P * tt + P] for v in oT],
                               [n[:, h, :] for n in nvo], h == 0, h == NH - 1)
                last.then_inc(o_added, 1)

            def attend(b):
                turn_xn3(b)
                queries(b, 0)
                for h in range(NH + 3):
                    if h < NH:
                        scores(b, h)
                    if h % 2 == 0 and h // 2 + 1 < NH // 2:
                        queries(b, h // 2 + 1)
                    if h >= 3:
                        project(b, h - 3)
                    if 2 <= h <= NH + 1:
                        values(b, h - 2)
                    if 1 <= h <= NH:
                        turn_p(b, h - 1)

            attend(0)
            with pe.Fori(1, B) as b:
                attend(b)

            def ffn(c):
                pe.wait_ge(f_q, c + 1)
                for j in range(2):
                    last = pe.transpose(bank(0).bitcast(BF16)[:, P * j:P * j + P], xq[:, P * j:P * j + P], identb[:])
                last.then_inc(f_qT, 1)
                pe.wait_ge(f_qTr, c + 1)
                for n in range(2):
                    for j in range(2):
                        last = pe.matmul(bank(1 + n), xqT[:, P * j:P * j + P], w1T[:, j, 512 * n:512 * n + 512],
                                         start=(j == 0), stop=(j == 1))
                last.then_inc(f_hs1, 1)
                pe.wait_ge(f_hq, c + 1)
                for j in range(FT):
                    last = pe.transpose(bank(3).bitcast(BF16)[:, P * j:P * j + P], hq[:, P * j:P * j + P], identb[:])
                last.then_inc(f_hqT, 1)
                pe.wait_ge(f_hqTr, c + 1)
                for j in range(FT):
                    last = pe.matmul(ps[:, 4, 0:H], hqT[:, P * j:P * j + P], w2T[:, j, :],
                                     start=(j == 0), stop=(j == FT - 1))
                last.then_inc(f_y, 1)

            pe.wait_ge(x3_ready, B)
            with pe.Fori(0, NT) as c:
                ffn(c)

        @block.vector
        def _(dve):
            V = nc.vector
            chain = Chain(dve, dve_steps)
            V.memset(zeros[:], 0.0).then_inc(zeros_ready, 1)
            V.memset(ctxT[:, :, 0:PAD], 0.0).then_inc(pads_ready, 1)
            chain.step(V.memset(xpT[:], 0.0))
            chain.step(V.memset(split[32:64, :], 0.0))
            dve.wait_ge(d_win, 32)
            for d in range(DT):
                for k in range(NCONV):
                    last = V.tensor_scalar(wink[:, d, k, :], win[:, d, :], convw[:, d, k:k + 1], None, ALU.mult)
                last.then_inc(wink_ready, 1)
            chain.wait()
            dve.wait_ge(smallT_in_psum, 1)
            n_x = DTR + 2 * NS
            small = ps[:, 4, 0:DT * n_x].rearrange("p (d r) -> p d r", d=DT)
            for at in (0, 64, 96):
                V.tensor_copy(xpT[:, :, at:at + 2 * NS], small[:, :, DTR:])
            V.tensor_copy(xpT[:, :, 32:32 + DTR], small[:, :, 0:DTR])
            V.tensor_copy(dtwT[32:32 + DTR, :], ps[0:DTR, 5, 0:H])
            V.tensor_copy(gwT[:], ps[:, 6, 0:2 * E].rearrange("p (d e) -> p d e", d=2)).then_inc(smallT_ready, 1)
            dve.wait_ge(d_small, 160)
            chain.link(V.tensor_copy(mbias[:], mk8[:]))
            chain.link(V.tensor_reduce(alive[:], mbias[:], AX.X, ALU.max))
            V.tensor_scalar(mbias[:], mbias[:], -1.0, -MASKED, ALU.add, ALU.mult).then_inc(mask_ready, 1)
            dve.wait_ge(d_x, 16)
            for c in range(NT):
                chain.step(V.bn_stats(stats[:, c, :], x[:, c, :]))
            chain.wait()
            for c in range(NT):
                chain.step(V.bn_aggr(mv[:, c, :], stats[:, c, :]))
            chain.wait()
            V.tensor_scalar(ve[:], mv[:, :, 1], EPS, None, ALU.add).then_inc(ve_ready, 1)
            dve.wait_ge(rstd_ready, 1)
            V.scalar_tensor_tensor(nmr[:], mv[:, :, 0], -1.0, rstd[:], ALU.mult, ALU.mult).then_inc(nmr_ready, 1)
            dve.wait_ge(xdbl_done, 2)
            xdbl = ps[:, 4:6, :].rearrange("p a b -> p (a b)")
            V.tensor_copy(dtlow[32:32 + DTR, :], xdbl[32:32 + DTR, :]).then_inc(dtlow_ready, 1)
            chain.step(V.tensor_copy(split[0:32, :], xdbl[0:32, :]))
            chain.link(V.tensor_copy(split[64:128, :], xdbl[64:128, :]))
            chain.link(V.tensor_tensor(rest[64:128, :], xdbl[64:128, :], split[64:128, :], ALU.subtract))
            chain.link(V.tensor_copy(split[64:128, :], rest[64:128, :]))
            chain.link(V.tensor_tensor(rest[96:128, :], rest[96:128, :], split[96:128, :], ALU.subtract))
            V.tensor_copy(split[96:128, :], rest[96:128, :]).then_inc(split_ready, 1)
            dve.wait_ge(a_exp, 1)
            V.tensor_scalar(amat[:], amat[:], -1.0, None, ALU.mult).then_inc(a_ready, 1)
            for d in range(DT):
                dve.wait_ge(sp_exp, d + 1)
                V.tensor_scalar(sp[2 * d][:], sp[2 * d + 1][:], 1.0, None, ALU.add).then_inc(sp_u, 1)
            for d in range(DT):
                dve.wait_ge(sp_u, d + 1)
                chain.link(V.scalar_tensor_tensor(sp[2 * d + 1][:], sp[2 * d][:], -1.0, sp[2 * d + 1][:],
                                                  ALU.add, ALU.subtract))
                dve.wait_ge(sp_ln, d + 1)
                chain.step(V.tensor_tensor(dtv[:, d], dtv[:, d], sp[2 * d + 1][:], ALU.subtract))
                chain.link(V.tensor_scalar(sp[2 * d][:], ps[:, 2 * d:2 * d + 2, :].rearrange("p a b -> p (a b)"),
                                           dtb[:, d:d + 1], 0.0, ALU.add, ALU.max))
                chain.link(V.tensor_tensor(dtv[:, d], dtv[:, d], sp[2 * d][:], ALU.add))
                chain.step(V.tensor_tensor(du[:, d], dtv[:, d], u[:, d], ALU.mult))
                V.tensor_copy(nmax[:, 0:1], dtb[:, 0:1]).then_inc(dt_ready, 1)
            chain.wait()
            for k in range(2):
                last = V.memset(bank(k).rearrange("p (b l) -> p b l", b=2)[:, :, 0:1], 0.0)
            last.then_inc(da_zeroed, 1)

            def drive(hb, m, j):
                i = 32 * hb + 4 * m + j
                dve.wait_ge(bc_ready, 16 * hb + 2 * m + j // 2 + 1)
                if hb or not isinstance(m, int) or m or j > 1:
                    dve.wait_ge(scanned, i - 1)
                V.tensor_tensor(dbu[:, j % 2, :], du[:, j % 2, 512 * hb:512 * hb + 512],
                                bank(4 + (j % 4) // 2), ALU.mult).then_inc(dbu_ready, 1)

            def scan_four(hb, m, last_turn):
                for j in range(4):
                    i = 32 * hb + 4 * m + j
                    past_two = hb or not isinstance(m, int) or m or j > 1
                    dve.wait_ge(da_ready, i + 1)
                    dve.wait_ge(dbu_ready, i + 1)
                    if past_two:
                        dve.wait_ge(hc_ready, i - 1)
                    V.tensor_tensor_scan(hst[:, j % 2, :], bank(j % 2), dbu[:, j % 2, :], 0.0, ALU.mult, ALU.add)\
                        .then_inc(scanned, 1)
                    if j < 3:
                        drive(hb, m, j + 1)
                    elif not last_turn:
                        drive(hb, m + 1, 0)
                    dve.wait_ge(scanned, i + 1)
                    if past_two:
                        dve.wait_ge(y_added, i - 1)
                    V.tensor_tensor(hc[:, j % 2, :], hst[:, j % 2, :], bank(6 + j // 2), ALU.mult)\
                        .then_inc(hc_ready, 1)

            for hb in range(2):
                drive(hb, 0, 0)
                scan_four(hb, 0, False)
                with dve.Fori(1, NS // 2 - 1) as m:
                    scan_four(hb, m, False)
                scan_four(hb, NS // 2 - 1, True)
                dve.wait_ge(y_added, 32 * (hb + 1))
                dve.wait_ge(sz_ready, 1)
                for d in range(DT):
                    chain.step(V.scalar_tensor_tensor(yz[:, d, :], u[:, d, 512 * hb:512 * hb + 512],
                                                      dskip[:, d:d + 1], bank(2 + d), ALU.mult, ALU.add))
                chain.wait()
                for d in range(DT):
                    last = V.tensor_tensor(yz[:, d, :].rearrange("p (b l) -> p b l", b=2),
                                           yz[:, d, :].rearrange("p (b l) -> p b l", b=2),
                                           sz[:, 4 * hb + d:4 * hb + 4:2, :], ALU.mult)
                last.then_inc(yz_ready, 1)
                dve.wait_ge(yT_ready, hb + 1)
                dve.wait_ge(tg_ready, 1)
                half = x[:, 4 * hb:4 * hb + 4, :].rearrange("p c h -> p (c h)")
                for b in range(2):
                    part = half[:, 512 * b:512 * b + 512]
                    chain.step(V.scalar_tensor_tensor(part, bank(4 + b), tg[:, 0:1], part, ALU.mult, ALU.add))
                chain.wait()
                for c in range(4 * hb, 4 * hb + 4):
                    last = V.bn_stats(stats[:, c, :], x[:, c, :])
                    chain.step(last)
                chain.wait()
                for c in range(4 * hb, 4 * hb + 4):
                    chain.step(V.bn_aggr(mv[:, c, :], stats[:, c, :]))
                chain.wait()
                V.tensor_scalar(ve[:, 4 * hb:4 * hb + 4], mv[:, 4 * hb:4 * hb + 4, 1], EPS, None, ALU.add)\
                    .then_inc(ve_ready, 1)
                V.tensor_copy(wsum[:, 0:1], tg[:, 0:1]).then_inc(x1_ready, 1)
                dve.wait_ge(rstd_ready, 2 + hb)
                for c in range(4 * hb, 4 * hb + 4):
                    V.tensor_scalar(xn[:, c, :], x[:, c, :], mv[:, c, 0:1], rstd[:, c:c + 1],
                                    ALU.subtract, ALU.mult).then_inc(xn_ready, 1)
                dve.wait_ge(logits_ready, hb + 1)
                logits = ps[:, 4, 0:4 * E].rearrange("p (c e) -> p c e", c=4)
                chain.link(V.tensor_reduce(nmax[:], logits, AX.X, ALU.max))
                V.tensor_tensor(lsub[:], logits, nmax[:].unsqueeze(2).to_broadcast([P, 4, E]), ALU.subtract)\
                    .then_inc(lsub_ready, 1)
                dve.wait_ge(pexp_ready, hb + 1)
                for c in range(4):
                    chain.step(V.max(top8[:, c, :], pexp[:, c, :]))
                chain.wait()
                for c in range(4):
                    V.max_index(eid[:, c, :], top8[:, c, :], pexp[:, c, :])
                    chain.step(V.match_replace(left[:, c, :], top8[:, c, :], pexp[:, c, :], -1.0))
                chain.wait()
                V.tensor_scalar(chosen[:, 4 * hb:4 * hb + 4, :], left[:], -1.0, None, ALU.is_equal)\
                    .then_inc(chosen_ready, 1)
                chain.step(V.tensor_copy(eidf[:], eid[:]))
                chain.step(V.tensor_reduce(wsum[:], top8[:], AX.X, ALU.add))
                chain.wait()
                chain.link(V.reciprocal(wsum[:], wsum[:]))
                chain.step(V.tensor_tensor(hot[:], iota_e[:].unsqueeze(1).unsqueeze(1).to_broadcast([P, 4, K, E]),
                                           eidf[:].unsqueeze(3).to_broadcast([P, 4, K, E]), ALU.is_equal))
                dve.wait_ge(pos_ready, hb + 1)
                pos = ps[:, 5, 0:4 * E].rearrange("p (c e) -> p c e", c=4)
                chain.step(V.tensor_scalar(over[:], pos, float(CAP), 2.0 * SLOTS, ALU.is_ge, ALU.mult))
                chain.step(V.tensor_tensor(slotv[:], pos, iota_slot[:].unsqueeze(1).to_broadcast([P, 4, E]), ALU.add))
                chain.wait()
                chain.link(V.tensor_tensor(slotv[:], slotv[:], over[:], ALU.add))
                for c in range(4):
                    chain.step(V.tensor_tensor(hot[:, c], hot[:, c],
                                               slotv[:, c, :].unsqueeze(1).to_broadcast([P, K, E]), ALU.mult))
                chain.wait()
                chain.link(V.tensor_reduce(slotk[:], hot[:], AX.X, ALU.add))
                span = slice(4 * K * hb, 4 * K * (hb + 1))
                flat = slotk[:].rearrange("p c k -> p (c k)")
                chain.step(V.tensor_scalar(keep[:], slotk[:], float(SLOTS), None, ALU.is_lt))
                chain.step(V.tensor_scalar(slotg[:], slotk[:], float(SLOTS), None, ALU.min))
                V.tensor_copy(idx_s[:, span], flat)
                chain.wait()
                chain.step(V.tensor_tensor(keep[:], keep[:], top8[:], ALU.mult))
                V.tensor_copy(idx_g[:, span], slotg[:].rearrange("p c k -> p (c k)"))
                chain.wait()
                V.tensor_tensor(wv[:, span].rearrange("p (c k) -> p c k", c=4), keep[:],
                                wsum[:].unsqueeze(2).to_broadcast([P, 4, K]), ALU.mult).then_inc(idx_ready, 1)

            dve.wait_ge(d_ffn, 32)
            chain.step(V.tensor_reduce(wabs[:, 0:1], ebuf[:], AX.X, ALU.add,
                                       apply_absolute_value=True))
            V.tensor_reduce(wabs[:, 1:2], w2[:].rearrange("p a b -> p (a b)"), AX.X, ALU.add,
                            apply_absolute_value=True).then_inc(wabs_ready, 1)
            for g in range(NKV):
                for k, dst in enumerate((mqk, nvo)):
                    dve.wait_ge(mn_hi, 2 * g + k + 1)
                    shape = "p a b c -> p (a b c)" if k == 0 else "p a b -> p (a b)"
                    V.tensor_tensor(dst[1][:, 2 * g:2 * g + 2].rearrange(shape), bank(6 + k),
                                    dst[0][:, 2 * g:2 * g + 2].rearrange(shape).bitcast(F32), ALU.subtract)\
                        .then_inc(mn_ready, 1)
            dve.wait_ge(wsum_done, 1)
            chain.link(V.tensor_scalar(wmean[:], ps[:, 0, 0:2], 1.0 / (H * FI), 1e-5, ALU.mult, ALU.max))
            chain.link(V.reciprocal(wscale[:], wmean[:]))
            for k, flat in enumerate((ebuf[:], w2[:].rearrange("p a b -> p (a b)"))):
                chain.link(V.tensor_scalar(flat, flat, wscale[:, k:k + 1], MAGIC, ALU.mult, ALU.add))
                chain.link(V.tensor_scalar(flat, flat, MAGIC, 1.0, ALU.subtract, ALU.min))
                if k:
                    dve.wait_ge(wternT_in_psum, 2)
                V.tensor_scalar(wtern[:], flat, -1.0, None, ALU.max).then_inc(wtern_ready, 1)

            def gated(p, j):
                dve.wait_ge(sg_ready, p + 1)
                if not isinstance(p, int) or p > 1:
                    dve.wait_ge(down_done, p - 1)
                V.tensor_tensor(hT[:, j % 2, :], sg[:, j % 2, :], ps[0:I, 2 + j % 2, P:2 * P], ALU.mult)\
                    .then_inc(hT_ready, 1)

            def take_out(p, j):
                dve.wait_ge(down_done, p + 1)
                if not isinstance(p, int) or p > 1:
                    dve.wait_ge(d_eo[j % 2], 16 * (p // 2) if isinstance(p, int) else 8 * (p - j % 2))
                V.tensor_copy(eo[:, j % 2, :], ps[:, 4 + j % 2, 0:H]).then_inc(eo_ready, 1)

            gated(0, 0)
            gated(1, 1)
            take_out(0, 0)
            gated(2, 0)
            take_out(1, 1)
            with dve.Fori(1, NPAIR // 2 - 1) as r:
                for j in range(2):
                    gated(2 * r + j + 1, j + 1)
                    take_out(2 * r + j, j)
            gated(NPAIR - 1, 1)
            take_out(NPAIR - 2, 0)
            take_out(NPAIR - 1, 1)

            def hold():
                V.memset(spare[:, 0:1], 0.0)

            def combine(b):
                for cc in range(2):
                    c = 2 * b + cc
                    dve.wait_ge(d_gath[cc], 16 * K * (b + 1))
                    for k in range(K):
                        w = wv[:, c * K + k:c * K + k + 1] if isinstance(b, int) else wv[:, bass.ds(c * K + k, 1)]
                        if k == 0:
                            last = V.tensor_scalar(G[:, cc, 0, :], G[:, cc, 0, :], w, None, ALU.mult)
                        else:
                            dve.wait_ge(comb_steps, 8 * c + k)
                            last = V.scalar_tensor_tensor(G[:, cc, 0, :], G[:, cc, k, :], w, G[:, cc, 0, :],
                                                          ALU.mult, ALU.add)
                        last.then_inc(comb_steps, 1)
                    xc = x[:, bass.ds(c, 1), :].rearrange("p a h -> p (a h)")
                    dve.wait_ge(comb_steps, 8 * c + 8)
                    V.scalar_tensor_tensor(xb[:, cc, :], G[:, cc, 0, :], tg[:, 2:3], xc, ALU.mult, ALU.add)\
                        .then_inc(combined, 1)
                    dve.wait_ge(combined, c + 1)
                    V.bn_stats(stats[:, cc, :], xb[:, cc, :]).then_inc(ln_steps, 1)
                    dve.wait_ge(ln_steps, 2 * c + 1)
                    hold()
                    V.bn_aggr(mv[:, cc, :], stats[:, cc, :]).then_inc(ln_steps, 1)
                dve.wait_ge(ln_steps, 4 * b + 4)
                V.tensor_scalar(ve[:, bass.ds(2 * b, 2)], mv[:, 0:2, 1], EPS, None, ALU.add).then_inc(ve3_ready, 1)
                dve.wait_ge(rstd3_ready, b + 1)
                if isinstance(b, int) and b == 0:
                    dve.wait_ge(d_scat[0], 16 * 32)
                else:
                    dve.wait_ge(xnT3_in_psum, b)
                for cc in range(2):
                    c = 2 * b + cc
                    last = V.tensor_scalar(xn[:, cc, :], xb[:, cc, :], mv[:, cc, 0:1], rstd[:, bass.ds(c, 1)],
                                           ALU.subtract, ALU.mult)
                last.then_inc(xn3_ready, 1)
                V.tensor_copy(mb[:], mbias[:, bass.ds(b, 1), :].rearrange("p a l -> p (a l)")).then_inc(mb_ready, 1)

            def low(dst, src, hi, s):
                V.tensor_tensor(dst, src, hi.bitcast(F32), ALU.subtract).then_inc(s, 1)

            def split_lo(b):
                dve.wait_ge(c_hi, 2 * b + 2)
                V.tensor_tensor(cT[1][:], ctxT[:, bass.ds(b, 1), PAD:].rearrange("p a l -> p (a l)"),
                                cT[0][:].bitcast(F32), ALU.subtract)
                low(cS[1][:].rearrange("p a b -> p (a b)"),
                    ctx_tm[:, bass.ds(2 * b, 2), :].rearrange("p a b -> p (a b)"),
                    cS[0][:].rearrange("p a b -> p (a b)"), c_ready)
                dve.wait_ge(xnT3_hi, b + 1)
                low(xnT3[1][:].rearrange("p a b -> p (a b)"), bank(0), xnT3[0][:].rearrange("p a b -> p (a b)"),
                    xnT3_ready)

            def q_low(b, hp):
                dve.wait_ge(q_hi, 8 * b + hp + 1)
                if not isinstance(b, int) or b or hp > 1:
                    dve.wait_ge(s_done, 2 * (8 * b + hp) - 2)
                low(qT[1][:, hp % 2].rearrange("p a b -> p (a b)"), bank(0),
                    qT[0][:, hp % 2].rearrange("p a b -> p (a b)"), q_ready)

            def masked(b, h):
                i = NH * b + h
                dve.wait_ge(s_done, i + 1)
                if not isinstance(b, int) or b or h > 1:
                    dve.wait_ge(p_exp, i - 1)
                if h == 0:
                    dve.wait_ge(mb_ready, b + 1)
                hold()
                for tt in range(2):
                    last = V.tensor_tensor_reduce(sneg[:, h % 2, tt, :], ps[:, 1 + h % 2, L * tt:L * tt + L], mb[:],
                                                  -(DH ** -0.5), 3e38, ALU.add, ALU.min,
                                                  accum_out=smin[:, h % 2, tt:tt + 1])
                last.then_inc(s_masked, 1)

            def inverse(b, h):
                i = NH * b + h
                dve.wait_ge(p_exp, i + 1)
                if not isinstance(b, int) or b or h > 1:
                    dve.wait_ge(p_ready, i - 1)
                V.reciprocal(pinv[:, h % 2, :], psum_[:, h % 2, :]).then_inc(inv_steps, 1)
                dve.wait_ge(inv_steps, i + 1)
                V.tensor_scalar(pinv[:, h % 2, :], pinv[:, h % 2, :], alive[:, bass.ds(b, 1)], None, ALU.mult)\
                    .then_inc(p_inv, 1)

            def pT_low(b, h):
                i = NH * b + h
                dve.wait_ge(pT_hi, i + 1)
                if not isinstance(b, int) or b or h > 1:
                    dve.wait_ge(av_done, i - 1)
                low(pT[1][:, h % 2].rearrange("p a b -> p (a b)"), bank(3 + h % 2),
                    pT[0][:, h % 2].rearrange("p a b -> p (a b)"), pT_ready)

            def o_low(b, h):
                i = NH * b + h
                dve.wait_ge(o_hi, i + 1)
                if not isinstance(b, int) or b or h > 1:
                    dve.wait_ge(o_added, i - 1)
                low(oT[1][:, h % 2], bank(5)[:, 0:L], oT[0][:, h % 2], o_ready)

            def attend(b):
                combine(b)
                split_lo(b)
                q_low(b, 0)
                for h in range(NH + 2):
                    if h < NH:
                        masked(b, h)
                    if h % 2 == 1 and h // 2 + 1 < NH // 2:
                        q_low(b, h // 2 + 1)
                    if 1 <= h <= NH:
                        pT_low(b, h - 1)
                    if h < NH:
                        inverse(b, h)
                    if h >= 2:
                        o_low(b, h - 2)
                dve.wait_ge(o_added, NH * b + NH)
                for tt in range(2):
                    xc = x[:, bass.ds(2 * b + tt, 1), :].rearrange("p a h -> p (a h)")
                    last = V.scalar_tensor_tensor(xc, ps[:, 6 + tt, 0:H], tg[:, 1:2], xb[:, tt, :], ALU.mult, ALU.add)
                last.then_inc(x3_ready, 1)

            dve.wait_ge(mask_ready, 1)
            attend(0)
            with dve.Fori(1, B) as b:
                attend(b)

            dve.wait_ge(x3_ready, B)
            dve.wait_ge(xnT3_in_psum, B)
            dve.wait_ge(d_vec, 64)
            chain.link(V.tensor_scalar(wmean[:], wmean[:], 1.0 / 127.0, None, ALU.mult))

            def quantise(link, src, dst, root, amax, which):
                link(V.tensor_scalar(fs[:, 12:13], amax, root, 1e-5, ALU.mult, ALU.max))
                link(V.reciprocal(fs[:, 10:11], fs[:, 12:13]))
                link(V.tensor_scalar(fs[:, 10:11], fs[:, 10:11], 127.0, None, ALU.mult))
                link(V.tensor_scalar(fs[:, 11:12], fs[:, 12:13], wmean[:, which:which + 1], None, ALU.mult))
                link(V.tensor_scalar(src, src, root, fs[:, 10:11], ALU.mult, ALU.mult))
                link(V.tensor_scalar(src, src, MAGIC, MAGIC, ALU.add, ALU.subtract))
                return V.tensor_scalar(dst, src, 127.0, -128.0, ALU.min, ALU.max)

            def ffn(c, k):
                per = 23
                n = [0]

                def link(ins):
                    n[0] += 1
                    ins.then_inc(f_steps, 1)
                    dve.wait_ge(f_steps, per * c + n[0])

                xc = x[:, bass.ds(c, 1), :].rearrange("p a h -> p (a h)")
                xf = xb[:, k, :]
                link(V.tensor_copy(xf, xc))
                link(V.bn_stats(stats[:, 0, :], xf))
                hold()
                link(V.bn_aggr(mv[:, 0, :], stats[:, 0, :]))
                V.tensor_scalar(fs[:, 0:1], mv[:, 0, 1:2], EPS, None, ALU.add).then_inc(f_ve, 1)
                dve.wait_ge(f_root, 4 * c + 1)
                V.tensor_scalar(xn[:, k, :], xf, mv[:, 0, 0:1], fs[:, 4:5], ALU.subtract, ALU.mult).then_inc(f_xn, 1)
                dve.wait_ge(f_xn, c + 1)
                link(V.tensor_reduce(fs[:, 13:14], xn[:, k, :], AX.X, ALU.max, apply_absolute_value=True))
                dve.wait_ge(f_sq, c + 1)
                V.tensor_scalar(fs[:, 1:2], fs[:, 8:9], 1.0 / H, EPS, ALU.mult, ALU.add).then_inc(f_ve, 1)
                dve.wait_ge(f_root, 4 * c + 2)
                quantise(link, xn[:, k, :], xq, fs[:, 5:6], fs[:, 13:14], 0).then_inc(f_q, 1)
                dve.wait_ge(f_hs1, c + 1)
                for j in range(2):
                    last = V.scalar_tensor_tensor(hbuf[:, k, 512 * j:512 * j + 512], bank(1 + j), fs[:, 11:12],
                                                  b1v[:, 512 * j:512 * j + 512], ALU.mult, ALU.add)
                last.then_inc(f_h, 1)
                dve.wait_ge(f_act, c + 1)
                for j in range(2):
                    link(V.bn_stats(stats[:, j, :], hbuf[:, k, 512 * j:512 * j + 512]))
                hold()
                link(V.bn_aggr(mv[:, 1, :], stats[:, 0:2, :].rearrange("p a b -> p (a b)")))
                V.tensor_scalar(fs[:, 2:3], mv[:, 1, 1:2], EPS, None, ALU.add).then_inc(f_ve, 1)
                dve.wait_ge(f_root, 4 * c + 3)
                link(V.tensor_scalar(hbuf[:, k, :], hbuf[:, k, :], mv[:, 1, 0:1], fs[:, 6:7], ALU.subtract, ALU.mult))
                link(V.tensor_tensor(hbuf[:, k, :], hbuf[:, k, :], lng, ALU.mult))
                V.tensor_tensor(hbuf[:, k, :], hbuf[:, k, :], lnb, ALU.add).then_inc(f_hn, 1)
                dve.wait_ge(f_hn, c + 1)
                link(V.tensor_reduce(fs[:, 13:14], hbuf[:, k, :], AX.X, ALU.max, apply_absolute_value=True))
                dve.wait_ge(f_sq2, c + 1)
                V.tensor_scalar(fs[:, 1:2], fs[:, 9:10], 1.0 / FI, EPS, ALU.mult, ALU.add).then_inc(f_ve, 1)
                dve.wait_ge(f_root, 4 * c + 4)
                quantise(link, hbuf[:, k, :], hq, fs[:, 5:6], fs[:, 13:14], 1).then_inc(f_hq, 1)
                dve.wait_ge(f_y, c + 1)
                if not isinstance(c, int) or c > 1:
                    dve.wait_ge(d_out[k], 8 * (c - k))
                link(V.scalar_tensor_tensor(yb[:, k, :], ps[:, 4, 0:H], fs[:, 11:12], b2v, ALU.mult, ALU.add))
                V.scalar_tensor_tensor(yb[:, k, :], yb[:, k, :], tg[:, 3:4], xf, ALU.mult, ALU.add).then_inc(f_out, 1)
                assert n[0] == per, n[0]

            for k in range(2):
                ffn(k, k)
            with dve.Fori(1, NT // 2) as r:
                for k in range(2):
                    ffn(2 * r + k, k)


def kernel(**inputs):
    import numpy as np
    import concourse.bacc as bacc
    from concourse.bass_utils import run_bass_kernel_spmd

    nc = bacc.Bacc("TRN2", target_bir_lowering=False, num_devices=1)
    arrays, tensors = {}, {}
    for name, value in inputs.items():
        a = np.ascontiguousarray(value)
        key = "mask" if name == "mask_BxS2_bf1" else name
        if key == "mask":
            a = a.view(np.uint8)
        arrays[f"in_{key}"] = a
        tensors[key] = nc.dram_tensor(f"in_{key}", a.shape, mybir.dt.from_np(a.dtype), kind="ExternalInput").ap()
    out = nc.dram_tensor("out_0", (B, L, H), F32, kind="ExternalOutput").ap()
    build_program(nc, tensors, out)
    r = run_bass_kernel_spmd(nc, [arrays], core_ids=[0])
    return r.results[0]["out_0"]
```

```python
from contextlib import ExitStack

import concourse.bass as bass
from concourse import mybir

ALU = mybir.AluOpType
ACT = mybir.ActivationFunctionType
AX = mybir.AxisListType
F32 = mybir.dt.float32
F32R = mybir.dt.float32r
BF16 = mybir.dt.bfloat16
I32 = mybir.dt.int32
U32 = mybir.dt.uint32
U8 = mybir.dt.uint8
P = 128


class Chain:

    def __init__(self, engine, sem):
        self.engine, self.sem, self.base, self.n = engine, sem, 0, 0

    def step(self, ins):
        self.n += 1
        ins.then_inc(self.sem, 1)

    def wait(self, back=0):
        self.engine.wait_ge(self.sem, self.base + self.n - back)

    def link(self, ins):
        self.step(ins)
        self.wait()

B, L, H, DM = 4, 256, 256, 128
NT = B * L // P
NS, NCONV, DTR = 16, 4, 8
DT = H // P
E, K, CAP, I = 64, 8, 64, 96
SLOTS = E * CAP
NH, NKV, DH = 16, 8, 128
FI = 1024
FT = FI // P
EPS = 1e-5
MAGIC = 12582912.0
GROUP = 4
RING = 4
NG = E // GROUP
NPAIR = E // 2
PAD = NCONV - 1
MASKED = -1e30


def build_program(nc, t, out):
    with ExitStack() as ctx:
        mamba_scope = ExitStack()

        def sb(name, shape, dt=F32, scope=ctx):
            return scope.enter_context(nc.sbuf_tensor(name, shape, dt))

        def sem(name):
            return ctx.enter_context(nc.semaphore(name))

        ps = ctx.enter_context(nc.psum_tensor("ps", [P, 8, 512], F32))

        xin = nc.dram_tensor("expert_in", (SLOTS, H), F32, kind="Internal").ap()
        eout = nc.dram_tensor("expert_out", (SLOTS + 1, H), F32, kind="Internal").ap()

        ident = sb("ident", [P, P])
        identb = sb("identb", [P, P], BF16)
        ones = sb("ones", [P, P])
        onesb = sb("onesb", [P, P], BF16)
        before = sb("before", [P, P], BF16)
        mhalf = sb("mhalf", [P, 8])
        x = sb("x", [P, NT, H])
        xn = sb("xn", [P, NT, H])
        ctxT = sb("ctxT", [P, B, PAD + L])
        ctx_tm = sb("ctx_tm", [P, NT, DM])
        gates = sb("gates", [P, 4])
        tg = sb("tg", [P, 4])
        stats = sb("stats", [P, NT, 6])
        mv = sb("mv", [P, NT, 2])
        ve = sb("ve", [P, NT])
        rstd = sb("rstd", [P, NT])
        idx_s = sb("idx_s", [P, NT * K], I32)
        idx_g = sb("idx_g", [P, NT * K], I32)
        wv = sb("wv", [P, NT * K])
        mbias = sb("mbias", [P, B, L], BF16)
        alive = sb("alive", [P, B])
        wgu = sb("wgu", [P, RING, 2, GROUP, 2 * I])
        wdn = sb("wdn", [P, RING, GROUP, H])
        gwT = sb("gwT", [P, 2, E])

        def msb(name, shape, dt=F32):
            return sb(name, shape, dt, mamba_scope)

        convw = msb("convw", [P, DT, NCONV])
        convb = msb("convb", [P, DT])
        dtw = msb("dtw", [P, DT, DTR])
        dtb = msb("dtb", [P, DT])
        alog = msb("alog", [P, DT, NS])
        amat = msb("amat", [P, DT, NS])
        dskip = msb("dskip", [P, DT])
        u = msb("u", [P, DT, B * L])
        dtv = msb("dtv", [P, DT, B * L])
        du = msb("du", [P, DT, B * L])
        sz = msb("sz", [P, NT, L])
        nmr = msb("nmr", [P, NT])
        split = msb("split", [P, B * L], BF16)
        picks = msb("picks", [P, 32], BF16)
        sel = msb("sel", [P, 2 * NS, P], BF16)
        dbu = msb("dbu", [P, 4, 512])
        brow = msb("brow", [P, 2, 512])
        hc = msb("hc", [P, 2, 512])
        yz = msb("yz", [P, DT, 512])
        xnT = msb("xnT", [P, 4, 2, P])
        iota_e = msb("iota_e", [P, E])
        iota_slot = msb("iota_slot", [P, E])
        nmax = msb("nmax", [P, 4])
        lsub = msb("lsub", [P, 4, E])
        pexp = msb("pexp", [P, 4, E])
        top8 = msb("top8", [P, 4, K])
        eid = msb("eid", [P, 4, K], U32)
        eidf = msb("eidf", [P, 4, K])
        left = msb("left", [P, 4, E])
        chosen = msb("chosen", [P, NT, E], BF16)
        wsum = msb("wsum", [P, 4])
        over = msb("over", [P, 4, E])
        slotv = msb("slotv", [P, 4, E])
        hot = msb("hot", [P, 4, K, E])
        hst = hot[:].rearrange("p c k e -> p c (k e)")
        slotk = msb("slotk", [P, 4, K])
        keep = msb("keep", [P, 4, K])
        slotg = msb("slotg", [P, 4, K])
        mk8 = msb("mk8", [P, B, L], U8)
        gw_nat = msb("gw_nat", [E, H])
        win = msb("win", [P, DT, DM])
        xpw = msb("xpw", [DTR + 2 * NS, H])
        xpT = msb("xpT", [P, DT, P])
        dtwT = msb("dtwT", [P, H])
        wink = msb("wink", [P, DT, NCONV, DM])
        zeros = msb("zeros", [P, 8 * H])
        winT = msb("winT", [P, DT, NCONV, P])
        rest = msb("rest", [P, B * L])
        dtlow = msb("dtlow", [P, B * L])
        sp = [msb(f"sp{k}", [P, B * L]) for k in range(4)]
        mamba_scope.close()

        mqk = [sb(f"mqk{k}", [P, NH, 2, DM], F32R) for k in range(2)]
        nvo = [sb(f"nvo{k}", [P, NH, H], F32R) for k in range(2)]
        w1T = sb("w1T", [P, 2, FI], BF16)
        w2T = sb("w2T", [P, FT, H], BF16)
        wmean = sb("wmean", [P, 2])
        wscale = sb("wscale", [P, 2])
        ebuf = sb("ebuf", [P, 8 * H])
        xe = ebuf[:, 0:4 * H].rearrange("p (a h) -> p a h", a=4)
        xeT = ebuf[:, 4 * H:6 * H].rearrange("p (a b c) -> p a b c", a=2, b=2)
        eo = ebuf[:, 6 * H:8 * H].rearrange("p (a h) -> p a h", a=2)
        sg = sb("sg", [P, 2, I])
        hg = sb("hg", [P, 2, I])
        hT = sb("hT", [I, 2, P])

        prep_scope = ExitStack()

        def psb(name, shape, dt=F32):
            return sb(name, shape, dt, prep_scope)

        wq = psb("wq", [P, 2, NH * DH])
        wkv = psb("wkv", [P, 2, NKV * DH])
        wk, wvv = wkv[:, 0], wkv[:, 1]
        wo = psb("wo", [P, NH, H])
        w1 = wo[:, 0:FT, :]
        w2 = wo[:, FT:2 * FT, :].rearrange("p (a b) h -> p a (b h)", a=2)
        wqT = psb("wqT", [P, 2, 2, L])
        wkT = psb("wkT", [P, NKV, DM])
        wvT = psb("wvT", [P, NKV, DM])
        wabs = psb("wabs", [P, 2])
        wtern = wqT[:].rearrange("p a b l -> p (a b l)").bitcast(BF16)
        prep_scope.close()

        G = sb("G", [P, 2, K, H])
        xb = ebuf[:, 0:2 * H].rearrange("p (a h) -> p a h", a=2)
        mb = sb("mb", [P, L], BF16)
        spare = sb("spare", [P, 2])
        spare_pool = sb("spare_pool", [P, 2])
        idx_b = sb("idx_b", [P, 2 * K], I32)
        ve3 = sb("ve3", [P, 2])
        rstd3 = sb("rstd3", [P, 2])
        xnT3 = [sb(f"xnT3_{k}", [P, 2, L], F32R) for k in range(2)]
        cT = [sb(f"cT{k}", [P, L], F32R) for k in range(2)]
        cS = [sb(f"cS{k}", [P, 2, DM], F32R) for k in range(2)]
        qT = [sb(f"qT{k}", [P, 2, L], F32R) for k in range(2)]
        sneg = ebuf[:, 2 * H:6 * H].rearrange("p (a b l) -> p a b l", a=2, b=2)
        smin = sb("smin", [P, 2, 2])
        pr = sb("pr", [P, 2, 2, L])
        psum_ = sb("psum_", [P, 2, 2])
        pinv = sb("pinv", [P, 2, 2])
        pn = sb("pn", [P, 2, 2, L])
        pT = [sb(f"pT{k}", [P, 2, 2, L], F32R) for k in range(2)]
        oT = [sb(f"oT{k}", [P, 2, L], F32R) for k in range(2)]
        flat_a = wgu[:].rearrange("p a b c d -> p (a b c d)")
        flat_b = wdn[:].rearrange("p a b c -> p (a b c)")
        hbuf = flat_a[:, 0:2 * FI].rearrange("p (a n) -> p a n", a=2)
        lng, lnb, b1v = (flat_a[:, k * FI:(k + 1) * FI] for k in (2, 3, 4))
        b2v = flat_b[:, 0:H]
        xq = flat_b[:, H:2 * H].bitcast(BF16)
        xqT = flat_b[:, 2 * H:3 * H].bitcast(BF16)
        hq = flat_b[:, 3 * H:7 * H].bitcast(BF16)
        hqT = flat_b[:, 7 * H:11 * H].bitcast(BF16)
        yb = flat_b[:, 11 * H:13 * H].rearrange("p (a n) -> p a n", a=2)
        fve = sb("fve", [P, 2, 2])
        frt = sb("frt", [P, 2, 2])
        fms = sb("fms", [P, 2, 2])
        frm = sb("frm", [P, 2, 2])
        famax = sb("famax", [P, 2, 2])
        fqs = sb("fqs", [P, 2, 2])
        fback = sb("fback", [P, 2, 2])
        fsq = sb("fsq", [P, 2])

        d_ctx, d_win, d_small, d_x = sem("d_ctx"), sem("d_win"), sem("d_small"), sem("d_x")
        d_zero, d_kv, d_qo, d_ffn = sem("d_zero"), sem("d_kv"), sem("d_qo"), sem("d_ffn")
        d_w = [sem(f"d_w{k}") for k in range(RING)]
        d_scat = [sem("d_scat0"), sem("d_scat1")]
        consts_ready, zeros_ready = sem("consts_ready"), sem("zeros_ready")
        pads_ready, wink_ready = sem("pads_ready"), sem("wink_ready")
        ctxT_in_psum, winT_in_psum, smallT_in_psum = sem("ctxT_in_psum"), sem("winT_in_psum"), sem("smallT_in_psum")
        ctxT_ready, winT_ready, smallT_ready = sem("ctxT_ready"), sem("winT_ready"), sem("smallT_ready")
        conv_done, u_ready = sem("conv_done"), sem("u_ready")
        xdbl_done, dtlow_ready, split_ready = sem("xdbl_done"), sem("dtlow_ready"), sem("split_ready")
        dtraw_done, sp_exp, sp_u, sp_ln, dt_ready = (sem("dtraw_done"), sem("sp_exp"), sem("sp_u"), sem("sp_ln"),
                                                     sem("dt_ready"))
        sel_ready, a_exp, a_ready = sem("sel_ready"), sem("a_exp"), sem("a_ready")
        ve_ready, rstd_ready = sem("ve_ready"), sem("rstd_ready")
        nmr_ready, sz_ready, tg_ready = sem("nmr_ready"), sem("sz_ready"), sem("tg_ready")
        da_zeroed = sem("da_zeroed")
        b_spread, c_spread, b_copied = sem("b_spread"), sem("c_spread"), sem("b_copied")
        da_ready, pool_dbu, dve_dbu = sem("da_ready"), sem("pool_dbu"), sem("dve_dbu")
        scanned, hc_ready, y_added = sem("scanned"), sem("hc_ready"), sem("y_added")
        yz_ready, yT_ready, x1_ready = sem("yz_ready"), sem("yT_ready"), sem("x1_ready")
        xn_ready, xnT_in_psum, xnT_ready = sem("xn_ready"), sem("xnT_in_psum"), sem("xnT_ready")
        logits_ready, lsub_ready, pexp_ready = sem("logits_ready"), sem("lsub_ready"), sem("pexp_ready")
        chosen_ready, pos_ready, idx_ready = sem("chosen_ready"), sem("pos_ready"), sem("idx_ready")
        dve_steps, act_steps, pool_steps = sem("dve_steps"), sem("act_steps"), sem("pool_steps")
        d_out = sem("d_out")
        d_vec = sem("d_vec")
        d_xe = [sem(f"d_xe{k}") for k in range(4)]
        d_eo = [sem(f"d_eo{k}") for k in range(2)]
        kvT_in_psum, kvT_ready = sem("kvT_in_psum"), sem("kvT_ready")
        wqT_in_psum, wqT_ready = sem("wqT_in_psum"), sem("wqT_ready")
        mn_done, mn_hi, mn_ready = sem("mn_done"), sem("mn_hi"), sem("mn_ready")
        wabs_ready, wsum_done, wtern_ready = sem("wabs_ready"), sem("wsum_done"), sem("wtern_ready")
        wternT_in_psum, wternT_ready, mask_ready = sem("wternT_in_psum"), sem("wternT_ready"), sem("mask_ready")
        xeT_in_psum, xeT_ready, gu_done = sem("xeT_in_psum"), sem("xeT_ready"), sem("gu_done")
        sg_ready, hg_ready, turned_h, hT_ready, down_done, eo_ready = sem("sg_ready"), sem("hg_ready"), sem("turned_h"), sem("hT_ready"), sem("down_done"), sem("eo_ready")
        d_gath = [sem(f"d_gath{k}") for k in range(2)]
        combined, ve3_ready, rstd3_ready = sem("combined"), sem("ve3_ready"), sem("rstd3_ready")
        xn3_ready, xnT3_in_psum, xnT3_hi, xnT3_ready = (sem("xn3_ready"), sem("xnT3_in_psum"), sem("xnT3_hi"),
                                                        sem("xnT3_ready"))
        c_hi, c_ready = sem("c_hi"), sem("c_ready")
        idx_here, cs_hi, cs_ready, x2_kept = sem("idx_here"), sem("cs_hi"), sem("cs_ready"), sem("x2_kept")
        q_done, q_hi, q_ready = sem("q_done"), sem("q_hi"), sem("q_ready")
        s_done, s_masked, p_exp, p_inv, p_ready = (sem("s_done"), sem("s_masked"), sem("p_exp"), sem("p_inv"),
                                                   sem("p_ready"))
        pT_in_psum, pT_hi, pT_ready = sem("pT_in_psum"), sem("pT_hi"), sem("pT_ready")
        av_done, o_hi, o_ready, o_added = sem("av_done"), sem("o_hi"), sem("o_ready"), sem("o_added")
        x3_ready = sem("x3_ready")
        f_var = [sem("f_var0"), sem("f_var1")]
        f_root = [sem("f_root0"), sem("f_root1")]
        f_rms = [sem("f_rms0"), sem("f_rms1")]
        f_rms_root = [sem("f_rms_root0"), sem("f_rms_root1")]
        f_q, f_qT_in_psum, f_qT, f_h_done = sem("f_q"), sem("f_qT_in_psum"), sem("f_qT"), sem("f_h_done")
        f_h, f_silu, f_act, f_hn, f_sq = sem("f_h"), sem("f_silu"), sem("f_act"), sem("f_hn"), sem("f_sq")
        f_hq, f_hqT_in_psum, f_hqT, f_y, f_out = (sem("f_hq"), sem("f_hqT_in_psum"), sem("f_hqT"), sem("f_y"),
                                                  sem("f_out"))
        mb_ready = sem("mb_ready")
        f_front, f_back, f_end = sem("f_front"), sem("f_back"), sem("f_end")
        comb_steps, ln_steps, inv_steps = sem("comb_steps"), sem("ln_steps"), sem("inv_steps")

        block = ctx.enter_context(nc.Block())

        def wait_count(engine, s, n):
            if not isinstance(n, int) or n > 0:
                engine.wait_ge(s, n)

        def bank(k):
            return ps[:, k, :]

        def cols(ap, a, b):
            return ap[:, a:b]

        @block.sync
        def _(sp_):
            dma = sp_.dma_start
            dma(ctx_tm[:], t["ctx_1024"].rearrange("b (c p) d -> p (b c) d", p=P)).then_inc(d_ctx, 16)
            with nc.allow_non_contiguous_dma(reason="a few hundred values"):
                dma(win[:], t["L0_xattn_in_proj_w"].rearrange("(t p) d -> p t d", p=P)).then_inc(d_win, 16)
                dma(convw[:], t["L0_xattn_conv_w"].rearrange("(t p) a k -> p t (a k)", p=P)).then_inc(d_win, 16)
                dma(xpw[:], t["L0_xattn_x_proj_w"]).then_inc(d_small, 16)
                dma(dtw[:], t["L0_xattn_dt_proj_w"].rearrange("(t p) r -> p t r", p=P)).then_inc(d_small, 16)
                dma(gw_nat[:], t["L0_ffn_gate_w"]).then_inc(d_small, 16)
                dma(convb[:], t["L0_xattn_conv_b"].rearrange("(t p) -> p t", p=P)).then_inc(d_small, 16)
                dma(dtb[:], t["L0_xattn_dt_proj_b"].rearrange("(t p) -> p t", p=P)).then_inc(d_small, 16)
                dma(dskip[:], t["L0_xattn_D"].rearrange("(t p) -> p t", p=P)).then_inc(d_small, 16)
                dma(alog[:], t["L0_xattn_A_log"].rearrange("(t p) n -> p t n", p=P)).then_inc(d_small, 16)
                dma(gates[:, 0:2], t["g_xattn"].partition_broadcast(P)).then_inc(d_small, 16)
                dma(gates[:, 2:4], t["g_ffn"].partition_broadcast(P)).then_inc(d_small, 16)
            dma(x[:], t["x"].rearrange("b (c p) h -> p (b c) h", p=P)).then_inc(d_x, 16)
            dma(mk8[:].rearrange("p b l -> p (b l)"),
                t["mask"].rearrange("b l -> (b l)").partition_broadcast(P)).then_inc(d_small, 16)
            sp_.wait_ge(zeros_ready, 1)
            for k in range(4):
                dma(xin[1024 * k:1024 * (k + 1)].rearrange("(p r) h -> p (r h)", p=P), zeros[:]).then_inc(d_zero, 16)
            dma(eout[SLOTS:SLOTS + 1], zeros[0:1, 0:H]).then_inc(d_zero, 16)

            def weights(group, slot, wait):
                if wait is not None:
                    sp_.wait_ge(down_done, wait)
                es = slice(group * GROUP, group * GROUP + GROUP) if isinstance(group, int) else \
                    bass.ds(group * GROUP, GROUP)
                for k, name in enumerate(("L0_ffn_wg", "L0_ffn_wu")):
                    dma(wgu[:, slot, k], t[name][es].rearrange("e (p j) i -> p e (j i)", j=2)).then_inc(d_w[slot], 16)
                dma(wdn[0:I, slot], t["L0_ffn_wd"][es].rearrange("e i h -> i e h")).then_inc(d_w[slot], 16)

            for g in range(RING):
                weights(g, g, None)
            sp_.wait_ge(d_zero, 80)
            sp_.wait_ge(dt_ready, 2)
            sp_.wait_ge(split_ready, 1)
            sp_.wait_ge(mask_ready, 1)
            dma(wk, t["L1_xattn_Wk"]).then_inc(d_kv, 16)
            dma(wvv, t["L1_xattn_Wv"]).then_inc(d_kv, 16)
            dma(wq[:], t["L1_xattn_Wq"].rearrange("(j p) n -> p j n", p=P)).then_inc(d_qo, 16)
            dma(wo[:], t["L1_xattn_Wo"].rearrange("(h p) n -> p h n", p=P)).then_inc(d_qo, 16)
            sp_.wait_ge(idx_ready, 2)
            sp_.wait_ge(d_scat[0], 16 * 32)
            sp_.wait_ge(d_scat[1], 16 * 32)

            def rows(p, j, wait):
                if wait is not None:
                    sp_.wait_ge(xeT_in_psum, wait)
                at = slice(P * p, P * p + P) if isinstance(p, int) else bass.ds(P * p, P)
                dma(xe[:, j % 4], xin[at]).then_inc(d_xe[j % 4], 16)

            for p in range(4):
                rows(p, p, None)
            sp_.wait_ge(mn_done, 2 * NKV)
            dma(w1, t["L1_ffn_w1"].rearrange("(c p) h -> p c h", p=P)).then_inc(d_ffn, 16)
            dma(w2, t["L1_ffn_w2"].rearrange("(c p) n -> p c n", p=P)).then_inc(d_ffn, 16)

            def feed(r, first, last):
                for j in range(8):
                    if not (last and j >= 4):
                        rows(8 * r + j + 4, j + 4, 8 * r + j + 1)
                    if j % 2 == 0 and not (first and j < 4) and not (last and j >= 4):
                        weights(4 * r + j // 2 + 2, (j // 2 + 2) % 4, 8 * r + j - 2)

            feed(0, True, False)
            with sp_.Fori(1, NPAIR // 8 - 1) as r:
                feed(r, False, False)
            feed(NPAIR // 8 - 1, False, True)
            sp_.wait_ge(down_done, NPAIR)
            sp_.wait_ge(combined, 2)
            for dst, name in ((b1v, "L1_ffn_b1"), (lng, "L1_ffn_ln_g"), (lnb, "L1_ffn_ln_b"), (b2v, "L1_ffn_b2")):
                dma(dst, t[name].partition_broadcast(P)).then_inc(d_vec, 16)
            out_rows = out.rearrange("b (c p) h -> b p c h", p=P)
            with sp_.Fori(0, B) as b:
                sp_.wait_ge(f_out, b + 1)
                dma(out_rows[bass.ds(b, 1)].rearrange("a p c h -> (a p) c h"), yb).then_inc(d_out, 16)
            sp_.wait_ge(d_out, 16 * B)
            for k in range(2):
                sp_.wait_ge(d_eo[k], 16 * (NPAIR // 2))
            sp_.wait_ge(d_zero, 80)

        @block.gpsimd
        def _(pool):
            chain = Chain(pool, pool_steps)
            nc.gpsimd.memset(ident[:], 0.0).then_inc(pool_steps, 1)
            nc.gpsimd.memset(ones[:], 1.0).then_inc(pool_steps, 1)
            nc.gpsimd.memset(onesb[:], 1.0).then_inc(pool_steps, 1)
            nc.gpsimd.memset(picks[:], 0.0).then_inc(pool_steps, 1)
            chain.n = 4
            chain.wait()
            chain.link(nc.gpsimd.affine_select(out=ident[:], in_=ident[:], compare_op=ALU.not_equal, fill=1.0, base=0,
                                               pattern=[[-1, P]], channel_multiplier=1))
            nc.gpsimd.tensor_copy(identb[:], ident[:]).then_inc(consts_ready, 1)
            nc.gpsimd.affine_select(out=before[:], in_=onesb[:], compare_op=ALU.is_gt, fill=0.0, base=0,
                                    pattern=[[1, P]], channel_multiplier=-1).then_inc(consts_ready, 1)
            nc.gpsimd.memset(mhalf[:], -0.5).then_inc(consts_ready, 1)
            for part in (0, 64, 96):
                chain.link(nc.gpsimd.affine_select(out=picks[:], in_=picks[:], compare_op=ALU.not_equal, fill=1.0,
                                                   base=-part, pattern=[[-1, 32]], channel_multiplier=1))
            nc.gpsimd.tensor_copy(sel[:], picks[:].unsqueeze(2).to_broadcast([P, 32, P])).then_inc(sel_ready, 1)
            nc.gpsimd.iota(iota_e[:], [[1, E]], base=0, channel_multiplier=0,
                           allow_small_or_imprecise_dtypes=True).then_inc(consts_ready, 1)
            nc.gpsimd.iota(iota_slot[:], [[CAP, E]], base=0, channel_multiplier=0,
                           allow_small_or_imprecise_dtypes=True).then_inc(consts_ready, 1)
            pool.wait_ge(consts_ready, 3)
            pool.wait_ge(ve_ready, 1)
            nc.gpsimd.tensor_tensor(rstd[:], ve[:], mhalf[:], ALU.pow).then_inc(rstd_ready, 1)

            def drive(hb, m, j):
                i = 32 * hb + 4 * m + j
                pool.wait_ge(b_copied, 16 * hb + 2 * m + j // 2 + 1)
                wait_count(pool, scanned, i - 3)
                nc.gpsimd.tensor_tensor(dbu[:, j, :], du[:, j % 2, 512 * hb:512 * hb + 512], brow[:, j // 2, :],
                                        ALU.mult).then_inc(pool_dbu, 1)

            def scatter(hb, c, k):
                nc.gpsimd.indirect_dma_start(
                    xin, bass.IndirectOffsetOnAxis(ap=idx_s[:, c * K + k:c * K + k + 1], axis=0),
                    xn[:, c, :], None, bounds_check=SLOTS - 1, oob_is_err=False).then_inc(d_scat[hb], 16)

            def root(hb):
                pool.wait_ge(ve_ready, 2 + hb)
                nc.gpsimd.tensor_tensor(rstd[:, 4 * hb:4 * hb + 4], ve[:, 4 * hb:4 * hb + 4], mhalf[:, 0:4],
                                        ALU.pow).then_inc(rstd_ready, 1)

            pool.wait_ge(dt_ready, 2)
            for j in range(4):
                drive(0, 0, j)
            with pool.Fori(1, NS // 2) as m:
                for j in range(4):
                    drive(0, m, j)
            root(0)
            pool.wait_ge(d_zero, 80)
            pool.wait_ge(idx_ready, 1)
            pool.wait_ge(xn_ready, 4)
            for m in range(NS // 2):
                for jj in range(2):
                    drive(1, m, 2 * jj + 1)
                    for k in range(2):
                        scatter(0, m // 2, 4 * (m % 2) + 2 * jj + k)
            root(1)
            pool.wait_ge(idx_ready, 2)
            pool.wait_ge(xn_ready, 8)
            for c in range(4, NT):
                for k in range(K):
                    scatter(1, c, k)

            def put(p, j):
                pool.wait_ge(eo_ready, p + 1)
                at = slice(P * p, P * p + P) if isinstance(p, int) else bass.ds(P * p, P)
                pool.dma_start(eout[at], eo[:, j % 2]).then_inc(d_eo[j % 2], 16)

            with pool.Fori(0, NPAIR // 2) as r:
                for j in range(2):
                    put(2 * r + j, j)
            for k in range(2):
                pool.wait_ge(d_eo[k], 16 * (NPAIR // 2))
            pool.wait_ge(mn_ready, 2 * NKV)

            def gather(b, cc, k):
                if cc == 0 and k == 0:
                    pool.wait_ge(idx_here, b + 1)
                    nc.gpsimd.tensor_tensor(spare_pool[:], mhalf[:, 0:2], mhalf[:, 0:2], ALU.mult)
                nc.gpsimd.indirect_dma_start(
                    G[:, cc, k, :], None, eout,
                    bass.IndirectOffsetOnAxis(ap=idx_b[:, cc * K + k:cc * K + k + 1], axis=0),
                    bounds_check=SLOTS, oob_is_err=False).then_inc(d_gath[cc], 16)

            def root3(b):
                pool.wait_ge(ve3_ready, b + 1)
                nc.gpsimd.tensor_tensor(rstd3[:], ve3[:], mhalf[:, 0:2], ALU.pow)\
                    .then_inc(rstd3_ready, 1)

            def normalise(b, h):
                i = NH * b + h
                pool.wait_ge(p_inv, i + 1)
                wait_count(pool, pT_in_psum, i - 1)
                nc.gpsimd.tensor_tensor(pn[:, h % 2], pr[:, h % 2],
                                        pinv[:, h % 2, :].unsqueeze(2).to_broadcast([P, 2, L]), ALU.mult)\
                    .then_inc(p_ready, 1)

            def attend(b, first, last):
                for h in range(NH):
                    if not last and h == 13:
                        root3(b + 1)
                    if not (first and h == 0):
                        normalise(b, h - 1)
                    if not last and h < K:
                        for k in range(2):
                            gather(b + 1, h // 4, 2 * (h % 4) + k)
                if last:
                    normalise(b, NH - 1)

            for cc in range(2):
                for k in range(K):
                    gather(0, cc, k)
            root3(0)
            attend(0, True, False)
            with pool.Fori(1, B - 1) as b:
                attend(b, False, False)
            attend(B - 1, False, True)
            def roots(b, which):
                for here, src, done, dst in ((f_var, fve, f_root, frt), (f_rms, fms, f_rms_root, frm)):
                    pool.wait_ge(here[which], b + 1)
                    nc.gpsimd.tensor_tensor(dst[:, which, :], src[:, which, :], mhalf[:, 0:2], ALU.pow)\
                        .then_inc(done[which], 1)

            roots(0, 0)
            with pool.Fori(0, B - 1) as b:
                roots(b + 1, 0)
                roots(b, 1)
            roots(B - 1, 1)

        @block.scalar
        def _(act):
            chain = Chain(act, act_steps)
            A = nc.scalar.activation
            act.wait_ge(pads_ready, 1)
            for k in range(2):
                act.wait_ge(ctxT_in_psum, k + 1)
                A(ctxT[:, 2 * k:2 * k + 2, PAD:], bank(k).rearrange("p (b l) -> p b l", b=2), ACT.Copy)\
                    .then_inc(ctxT_ready, 1)
            for d in range(DT):
                act.wait_ge(winT_in_psum, d + 1)
                A(winT[:, d], bank(2 + d).rearrange("p (k e) -> p k e", k=NCONV), ACT.Copy).then_inc(winT_ready, 1)
            act.wait_ge(d_small, 160)
            for d in range(DT):
                for hb in range(2):
                    act.wait_ge(conv_done, 2 * d + hb + 1)
                    A(u[:, d, 512 * hb:512 * hb + 512], bank(2 * d + hb), ACT.Silu,
                      bias=convb[:, d:d + 1]).then_inc(u_ready, 1)
            act.wait_ge(nmr_ready, 1)
            act.wait_ge(rstd_ready, 1)
            for c in range(NT):
                last = A(sz[:, c, :], x[:, c, :], ACT.Silu, scale=rstd[:, c:c + 1], bias=nmr[:, c:c + 1])
            last.then_inc(sz_ready, 1)
            A(tg[:], gates[:], ACT.Tanh).then_inc(tg_ready, 1)
            A(amat[:], alog[:], ACT.Exp).then_inc(a_exp, 1)
            for d in range(DT):
                act.wait_ge(dtraw_done, 2 * d + 2)
                chain.link(A(sp[2 * d][:], ps[:, 2 * d:2 * d + 2, :].rearrange("p a b -> p (a b)"), ACT.Abs,
                             bias=dtb[:, d:d + 1]))
                A(sp[2 * d + 1][:], sp[2 * d][:], ACT.Exp, scale=-1.0).then_inc(sp_exp, 1)
            for d in range(DT):
                act.wait_ge(sp_u, d + 1)
                A(dtv[:, d], sp[2 * d][:], ACT.Ln).then_inc(sp_ln, 1)

            act.wait_ge(a_ready, 1)
            act.wait_ge(dt_ready, 2)
            act.wait_ge(da_zeroed, 1)

            def decay(hb, m, j):
                i, d = 32 * hb + 4 * m + j, j % 2
                wait_count(act, scanned, i - 1)
                A(bank(d).rearrange("p (b l) -> p b l", b=2)[:, :, 1:],
                  dtv[:, d, 512 * hb:512 * hb + 512].rearrange("p (b l) -> p b l", b=2)[:, :, 1:],
                  ACT.Exp, scale=amat[:, d, bass.ds(2 * m + j // 2, 1)]).then_inc(da_ready, 1)

            def copy_b(hb, m, k):
                act.wait_ge(b_spread, 16 * hb + 2 * m + k + 1)
                if hb == 0:
                    wait_count(act, pool_dbu, 2 * (2 * m + k) - 2)
                else:
                    act.wait_ge(pool_dbu, 32 if isinstance(m, int) and m == 0 else 32 + 2 * m + k - 1)
                A(brow[:, k, :], bank(4 + k), ACT.Copy).then_inc(b_copied, 1)

            def decays(hb, m, last):
                for j in range(4):
                    decay(hb, m, j)
                    if j % 2 and not last:
                        copy_b(hb, m + 1, j // 2)

            for hb in range(2):
                copy_b(hb, 0, 0)
                copy_b(hb, 0, 1)
                decays(hb, 0, False)
                with act.Fori(1, NS // 2 - 1) as m:
                    decays(hb, m, False)
                decays(hb, NS // 2 - 1, True)
                act.wait_ge(xnT_in_psum, hb + 1)
                for k in range(2):
                    A(xnT[:, 2 * k:2 * k + 2].rearrange("p a b c -> p (a b c)"), bank(6 + k), ACT.Copy)\
                        .then_inc(xnT_ready, 1)
                act.wait_ge(lsub_ready, hb + 1)
                A(pexp[:], lsub[:], ACT.Exp).then_inc(pexp_ready, 1)


            for k in range(4):
                act.wait_ge(kvT_in_psum, k + 1)
                dst = (wkT, wvT)[k // 2]
                A(dst[:, 4 * (k % 2):4 * (k % 2) + 4, :].rearrange("p a b -> p (a b)"), bank(k), ACT.Copy)\
                    .then_inc(kvT_ready, 1)
            for g in range(NKV):
                act.wait_ge(wqT_in_psum, g + 1)
                if g > 1:
                    act.wait_ge(mn_done, 2 * g - 3)
                A(wqT[:, g % 2].rearrange("p a b -> p (a b)"), bank(4 + g % 2), ACT.Copy).then_inc(wqT_ready, 1)
                for k, dst in enumerate((mqk, nvo)):
                    act.wait_ge(mn_done, 2 * g + k + 1)
                    A(dst[0][:, 2 * g:2 * g + 2].rearrange("p a b c -> p (a b c)" if k == 0 else "p a b -> p (a b)"),
                      bank(6 + k), ACT.Copy).then_inc(mn_hi, 1)
            def turn(p, j):
                act.wait_ge(xeT_in_psum, p + 1)
                if not isinstance(p, int) or p > 1:
                    act.wait_ge(gu_done, p - 1)
                A(xeT[:, j % 2].rearrange("p a b -> p (a b)"), bank(j % 2)[:, 0:2 * P], ACT.Copy).then_inc(xeT_ready, 1)

            def gate(p, j):
                act.wait_ge(gu_done, p + 1)
                if not isinstance(p, int) or p > 1:
                    act.wait_ge(hg_ready, p - 1)
                A(sg[:, j % 2, :], ps[:, 2 + j % 2, 0:I], ACT.Silu).then_inc(sg_ready, 1)

            def turned_rows(p, j):
                act.wait_ge(turned_h, p + 1)
                if not isinstance(p, int) or p > 1:
                    act.wait_ge(down_done, p - 1)
                A(hT[:, j % 2, :], ps[0:I, 6 + j % 2, 0:P], ACT.Copy).then_inc(hT_ready, 1)

            turn(0, 0)
            turn(1, 1)
            gate(0, 0)
            turn(2, 0)
            gate(1, 1)
            turned_rows(0, 0)
            turn(3, 1)
            gate(2, 0)
            turned_rows(1, 1)
            with act.Fori(1, NPAIR // 2 - 1) as r:
                for j in range(2):
                    turn(2 * r + j + 2, j)
                    gate(2 * r + j + 1, j + 1)
                    turned_rows(2 * r + j, j)
            gate(NPAIR - 1, 1)
            turned_rows(NPAIR - 2, 0)
            turned_rows(NPAIR - 1, 1)

            for k in range(4):
                act.wait_ge(wternT_in_psum, k + 1)
                dst = w1T[:, k, :] if k < 2 else w2T[:, 4 * k - 8:4 * k - 4, :].rearrange("p a b -> p (a b)")
                A(dst, bank(4 + k).bitcast(BF16), ACT.Copy).then_inc(wternT_ready, 1)

            def context_high(b):
                wait_count(act, s_done, NH * b)
                A(cT[0][:], ctxT[:, bass.ds(b, 1), PAD:].rearrange("p a l -> p (a l)"), ACT.Copy).then_inc(c_hi, 1)

            def context_rows_high(b):
                wait_count(act, av_done, NH * b)
                A(cS[0][:], ctx_tm[:, bass.ds(2 * b, 2), :], ACT.Copy).then_inc(cs_hi, 1)

            def norm_high(b):
                act.wait_ge(xnT3_in_psum, b + 1)
                A(xnT3[0][:].rearrange("p a b -> p (a b)"), bank(0), ACT.Copy).then_inc(xnT3_hi, 1)

            def keep_x2(b):
                act.wait_ge(combined, 2 * b + 2)
                A(x[:, bass.ds(2 * b, 2), :], xb, ACT.Copy).then_inc(x2_kept, 1)

            def q_high(b, h):
                i = NH * b + h
                act.wait_ge(q_done, i + 1)
                wait_count(act, s_done, i - 1)
                A(qT[0][:, h % 2], bank(0)[:, 0:L], ACT.Copy).then_inc(q_hi, 1)

            def exps(b, h):
                i = NH * b + h
                act.wait_ge(s_masked, i + 1)
                wait_count(act, p_ready, i - 1)
                for tt in range(2):
                    last = A(pr[:, h % 2, tt, :], sneg[:, h % 2, tt, :], ACT.Exp, scale=-1.0,
                             bias=smin[:, h % 2, tt:tt + 1], accum_out=psum_[:, h % 2, tt:tt + 1])
                last.then_inc(p_exp, 1)

            def pT_high(b, h):
                i = NH * b + h
                act.wait_ge(pT_in_psum, i + 1)
                wait_count(act, av_done, i - 1)
                A(pT[0][:, h % 2].rearrange("p a b -> p (a b)"), bank(3 + h % 2), ACT.Copy).then_inc(pT_hi, 1)

            def o_high(b, h):
                i = NH * b + h
                act.wait_ge(av_done, i + 1)
                wait_count(act, o_added, i - 1)
                A(oT[0][:, h % 2], bank(5)[:, 0:L], ACT.Copy).then_inc(o_hi, 1)

            def attend(b, first, last):
                for h in range(NH + 3 if last else NH):
                    if h == NH - 2 and not last:
                        norm_high(b + 1)
                    if h == 3 and not first:
                        context_rows_high(b)
                    if not (first and h < 2) and h < NH + 2:
                        pT_high(b, h - 2)
                    if h == NH - 1 and not last:
                        context_high(b + 1)
                    if not (first and h < 3):
                        o_high(b, h - 3)
                    if not (last and h + 2 >= NH):
                        q_high(b, h + 2)
                    if h < NH:
                        exps(b, h)
                    if h == NH - 3 and not last:
                        keep_x2(b + 1)

            context_high(0)
            context_rows_high(0)
            norm_high(0)
            keep_x2(0)
            q_high(0, 0)
            q_high(0, 1)
            attend(0, True, False)
            with act.Fori(1, B - 1) as b:
                attend(b, False, False)
            attend(B - 1, False, True)

            def gelu_silu(b):
                act.wait_ge(f_h, b + 1)
                for k in range(2):
                    A(hbuf[:, k, :], hbuf[:, k, :], ACT.Silu).then_inc(f_silu, 1)
                for k in range(2):
                    act.wait_ge(f_silu, 2 * b + k + 1)
                    A(hbuf[:, k, :], hbuf[:, k, :], ACT.Gelu).then_inc(f_act, 1)

            def turned(b):
                act.wait_ge(f_qT_in_psum, b + 1)
                A(xqT, bank(0).bitcast(BF16)[:, 0:2 * H], ACT.Copy).then_inc(f_qT, 1)

            def squares(b):
                for k in range(2):
                    act.wait_ge(f_hn, 2 * b + k + 1)
                    A(G[:, k, 0:FI // H, :].rearrange("p a h -> p (a h)"), hbuf[:, k, :], ACT.Square, accum_out=fsq[:, k:k + 1]).then_inc(f_sq, 1)
                for k in range(2):
                    act.wait_ge(f_hqT_in_psum, 2 * b + k + 1)
                    A(hqT[:, FI * k:FI * k + FI], bank(5 + k).bitcast(BF16), ACT.Copy).then_inc(f_hqT, 1)

            turned(0)
            gelu_silu(0)
            with act.Fori(0, B - 1) as b:
                turned(b + 1)
                squares(b)
                gelu_silu(b + 1)
            squares(B - 1)

        @block.tensor
        def _(pe):
            pe.wait_ge(consts_ready, 1)
            pe.wait_ge(d_ctx, 16)
            for k in range(2):
                for j in range(4):
                    last = pe.transpose(ps[:, k, P * j:P * j + P], ctx_tm[:, 4 * k + j, :], ident[:])
                last.then_inc(ctxT_in_psum, 1)
            for d in range(DT):
                pe.wait_ge(wink_ready, d + 1)
                for k in range(NCONV):
                    last = pe.transpose(ps[:, 2 + d, P * k:P * k + P], wink[:, d, k, :], ident[:])
                last.then_inc(winT_in_psum, 1)
            pe.wait_ge(d_small, 160)
            n_x = DTR + 2 * NS
            for d in range(DT):
                pe.transpose(ps[:, 4, n_x * d:n_x * d + n_x], xpw[:, P * d:P * d + P], ident[0:n_x, 0:n_x])
            for d in range(DT):
                pe.transpose(ps[0:DTR, 5, P * d:P * d + P], dtw[:, d, :], ident[:])
            for d in range(2):
                last = pe.transpose(ps[:, 6, E * d:E * d + E], gw_nat[:, P * d:P * d + P], ident[0:E, 0:E])
            last.then_inc(smallT_in_psum, 1)
            for d in range(DT):
                for hb in range(2):
                    pe.wait_ge(ctxT_ready, 2)
                    pe.wait_ge(winT_ready, 2)
                    for k in range(NCONV):
                        last = pe.matmul(bank(2 * d + hb), winT[:, d, k, :], ctxT[:, 2 * hb:2 * hb + 2, k:k + L],
                                         start=(k == 0), stop=(k == NCONV - 1))
                    last.then_inc(conv_done, 1)
            pe.wait_ge(smallT_ready, 1)
            for hb in range(2):
                for d in range(DT):
                    pe.wait_ge(u_ready, 2 * d + hb + 1)
                    last = pe.matmul(bank(4 + hb), xpT[:, d, :], u[:, d, 512 * hb:512 * hb + 512],
                                     start=(d == 0), stop=(d == 1))
                last.then_inc(xdbl_done, 1)
            pe.wait_ge(dtlow_ready, 1)
            pe.wait_ge(u_ready, 4)
            for d in range(DT):
                for hb in range(2):
                    pe.matmul(bank(2 * d + hb), dtwT[32:32 + DTR, P * d:P * d + P],
                              dtlow[32:32 + DTR, 512 * hb:512 * hb + 512], start=True, stop=True)\
                        .then_inc(dtraw_done, 1)
            pe.wait_ge(sel_ready, 1)
            pe.wait_ge(split_ready, 1)

            def spread(hb, row, to, s):
                pick = sel[:, bass.ds(row, 1), :].rearrange("p a m -> p (a m)")
                pe.matmul(bank(to), pick, split[:, 512 * hb:512 * hb + 512], start=True, stop=True).then_inc(s, 1)

            def spread_b(hb, m, k):
                wait_count(pe, b_copied, 16 * hb + 2 * m + k - 1)
                if hb:
                    wait_count(pe, dve_dbu, 2 * m + k - 1)
                spread(hb, 2 * m + k, 4 + k, b_spread)

            def spread_c(hb, m, k):
                spread(hb, NS + 2 * m + k, 6 + k, c_spread)

            def add_states(hb, m, first, last_turn, last_b=False):
                for j in range(4):
                    i = 32 * hb + 4 * m + j
                    pe.wait_ge(hc_ready, i + 1)
                    pe.matmul(bank(2 + j % 2), ident[:], hc[:, j % 2, :], start=(first and j < 2),
                              stop=(last_turn and j > 1)).then_inc(y_added, 1)
                    if j % 2 and not last_turn:
                        spread_c(hb, m + 1, j // 2)
                        if not last_b:
                            spread_b(hb, m + 2, j // 2)

            for hb in range(2):
                if hb:
                    pe.wait_ge(x1_ready, 1)
                    pe.wait_ge(pos_ready, 1)
                    pe.wait_ge(idx_ready, 1)
                    pe.wait_ge(yz_ready, 1)
                    pe.wait_ge(xnT_ready, 2)
                pe.wait_ge(dt_ready, 2)
                for k in range(2):
                    spread_b(hb, 0, k)
                    spread_c(hb, 0, k)
                for k in range(2):
                    spread_b(hb, 1, k)
                add_states(hb, 0, True, False)
                with pe.Fori(1, NS // 2 - 2) as m:
                    add_states(hb, m, False, False)
                add_states(hb, NS // 2 - 2, False, False, last_b=True)
                add_states(hb, NS // 2 - 1, False, True)
                pe.wait_ge(yz_ready, hb + 1)
                for b in range(2):
                    for lt in range(2):
                        for d in range(DT):
                            last = pe.transpose(ps[:, 4 + b, H * lt + P * d:H * lt + P * d + P],
                                                yz[:, d, L * b + P * lt:L * b + P * lt + P], ident[:])
                last.then_inc(yT_ready, 1)
                for c in range(4):
                    pe.wait_ge(xn_ready, 4 * hb + c + 1)
                    for d in range(2):
                        last = pe.transpose(ps[:, 6 + c // 2, H * (c % 2) + P * d:H * (c % 2) + P * d + P],
                                            xn[:, 4 * hb + c, P * d:P * d + P], ident[:])
                last.then_inc(xnT_in_psum, 1)
                pe.wait_ge(xnT_ready, 2 * hb + 2)
                pe.wait_ge(x1_ready, hb + 1)
                for c in range(4):
                    for d in range(2):
                        last = pe.matmul(ps[:, 4, E * c:E * c + E], xnT[:, c, d, :], gwT[:, d, :],
                                         start=(d == 0), stop=(d == 1))
                last.then_inc(logits_ready, 1)
                pe.wait_ge(consts_ready, 2)
                pe.wait_ge(chosen_ready, hb + 1)
                for c in range(4):
                    for e in range(4 * hb + c + 1):
                        same = e == 4 * hb + c
                        last = pe.matmul(ps[:, 5, E * c:E * c + E], (before if same else onesb)[:], chosen[:, e, :],
                                         start=(e == 0), stop=same)
                last.then_inc(pos_ready, 1)


            pe.wait_ge(idx_ready, 2)
            pe.wait_ge(d_kv, 32)
            for k in range(4):
                src = (wk, wvv)[k // 2]
                for j in range(4):
                    at = P * (4 * (k % 2) + j)
                    last = pe.transpose(ps[:, k, P * j:P * j + P], src[:, at:at + P], ident[:])
                last.then_inc(kvT_in_psum, 1)

            def turn_wq(g):
                if g > 1:
                    pe.wait_ge(wqT_ready, g - 1)
                for hh in range(2):
                    for j in range(2):
                        last = pe.transpose(ps[:, 4 + g % 2, L * hh + P * j:L * hh + P * j + P],
                                            wq[:, j, P * (2 * g + hh):P * (2 * g + hh) + P], ident[:])
                last.then_inc(wqT_in_psum, 1)

            pe.wait_ge(d_qo, 32)
            turn_wq(0)
            pe.wait_ge(kvT_ready, 4)
            for g in range(NKV):
                if g + 1 < NKV:
                    turn_wq(g + 1)
                pe.wait_ge(wqT_ready, g + 1)
                if g:
                    pe.wait_ge(mn_ready, 2 * g - 1)
                for hh in range(2):
                    for j in range(2):
                        last = pe.matmul(ps[:, 6, L * hh + P * j:L * hh + P * j + P],
                                         wqT[:, g % 2, hh, P * j:P * j + P], wkT[:, g, :], start=True, stop=True)
                last.then_inc(mn_done, 1)
                if g:
                    pe.wait_ge(mn_ready, 2 * g)
                for hh in range(2):
                    last = pe.matmul(ps[:, 7, L * hh:L * hh + L], wvT[:, g, :], wo[:, 2 * g + hh, :],
                                     start=True, stop=True)
                last.then_inc(mn_done, 1)
            def turn_rows(p, j):
                pe.wait_ge(d_xe[j % 4], 16 * (p // 4 + 1) if isinstance(p, int) else 4 * (p - j % 4) + 16)
                if not isinstance(p, int) or p > 1:
                    pe.wait_ge(xeT_ready, p - 1)
                for k in range(2):
                    last = pe.transpose(ps[:, j % 2, P * k:P * k + P], xe[:, j % 4, k::2], ident[:])
                last.then_inc(xeT_in_psum, 1)

            def gate_up(p, j, r):
                slot = j // 2 % 4
                if j % 2 == 0:
                    pe.wait_ge(d_w[slot], 48 * r + 48)
                pe.wait_ge(xeT_ready, p + 1)
                if not isinstance(p, int) or p > 1:
                    pe.wait_ge(hg_ready, p - 1)
                for e in range(2):
                    for k in range(2):
                        last = pe.matmul(ps[CAP * e:CAP * e + CAP, 2 + j % 2, 0:2 * I]
                                         .rearrange("p (w i) -> p w i", w=2),
                                         xeT[:, j % 2, k, CAP * e:CAP * e + CAP],
                                         wgu[:, slot, :, 2 * (j % 2) + e, I * k:I * k + I],
                                         start=(k == 0), stop=(k == 1))
                last.then_inc(gu_done, 1)

            def turn_h(p, j):
                pe.wait_ge(hg_ready, p + 1)
                if not isinstance(p, int) or p > 1:
                    pe.wait_ge(hT_ready, p - 1)
                pe.transpose(ps[0:I, 6 + j % 2, 0:P], hg[:, j % 2, :], ident[:]).then_inc(turned_h, 1)

            def down(p, j):
                slot = j // 2 % 4
                pe.wait_ge(hT_ready, p + 1)
                if not isinstance(p, int) or p > 1:
                    pe.wait_ge(eo_ready, p - 1)
                for e in range(2):
                    last = pe.matmul(ps[CAP * e:CAP * e + CAP, 4 + j % 2, 0:H], hT[:, j % 2, CAP * e:CAP * e + CAP],
                                     wdn[0:I, slot, 2 * (j % 2) + e, :], start=True, stop=True)
                last.then_inc(down_done, 1)

            def expert_turn(r, first, last):
                for j in range(8):
                    if not (last and j == 7):
                        turn_rows(8 * r + j + 1, j + 1)
                    gate_up(8 * r + j, j, r)
                    if not (first and j == 0):
                        turn_h(8 * r + j - 1, (j - 1) % 8)
                    if not (first and j < 2):
                        down(8 * r + j - 2, (j - 2) % 8)

            pe.wait_ge(mn_ready, 2 * NKV)
            turn_rows(0, 0)
            expert_turn(0, True, False)
            with pe.Fori(1, NPAIR // 8 - 1) as r:
                expert_turn(r, False, False)
            expert_turn(NPAIR // 8 - 1, False, True)
            turn_h(NPAIR - 1, 7)
            down(NPAIR - 2, 6)
            down(NPAIR - 1, 7)

            pe.wait_ge(wabs_ready, 1)
            pe.matmul(ps[:, 3, 0:2], ones[:], wabs[:], start=True, stop=True).then_inc(wsum_done, 1)
            for k in range(4):
                if k % 2 == 0:
                    pe.wait_ge(wtern_ready, k // 2 + 1)
                for j in range(8):
                    if k < 2:
                        src, at = wtern[:, H * j + P * k:H * j + P * k + P], P * j
                    else:
                        src = wtern[:, FI * (j % 2) + P * (4 * (k - 2) + j // 2):][:, 0:P]
                        at = H * (j // 2) + P * (j % 2)
                    last = pe.transpose(bank(4 + k).bitcast(BF16)[:, at:at + P], src, identb[:])
                last.then_inc(wternT_in_psum, 1)

            def mm3(o, lhs, rhs, start, stop):
                pe.matmul(o, lhs[0], rhs[0], start=start, stop=False)
                pe.matmul(o, lhs[0], rhs[1], start=False, stop=False)
                return pe.matmul(o, lhs[1], rhs[0], start=False, stop=stop)

            def turn_xn3(b):
                pe.wait_ge(xn3_ready, b + 1)
                if isinstance(b, int) and b == 0:
                    pe.wait_ge(eo_ready, NPAIR)
                else:
                    pe.wait_ge(q_ready, NH * b)
                for j in range(2):
                    for cc in range(2):
                        last = pe.transpose(ps[:, 0, L * j + P * cc:L * j + P * cc + P],
                                            xn[:, cc, P * j:P * j + P], ident[:])
                last.then_inc(xnT3_in_psum, 1)

            def queries(b, h):
                i = NH * b + h
                if h % NH == 0:
                    pe.wait_ge(xnT3_ready, b + h // NH + 1)
                wait_count(pe, q_ready, i)
                for j in range(2):
                    last = mm3(ps[:, 0, 0:L], [m[:, h % NH, j, :] for m in mqk],
                               [v[:, j, :] for v in xnT3], j == 0, j == 1)
                last.then_inc(q_done, 1)

            def scores(b, h):
                i = NH * b + h
                pe.wait_ge(q_ready, i + 1)
                if h == 0:
                    pe.wait_ge(c_ready, b + 1)
                wait_count(pe, s_masked, i - 1)
                for tt in range(2):
                    last = mm3(ps[:, 1 + h % 2, L * tt:L * tt + L],
                               [q[:, h % 2, P * tt:P * tt + P] for q in qT], [v[:] for v in cT], True, True)
                last.then_inc(s_done, 1)

            def turn_p(b, h):
                i = NH * b + h
                pe.wait_ge(p_ready, i + 1)
                wait_count(pe, pT_ready, i - 1)
                for st in range(2):
                    for tt in range(2):
                        last = pe.transpose(ps[:, 3 + h % 2, L * st + P * tt:L * st + P * tt + P],
                                            pn[:, h % 2, tt, P * st:P * st + P], ident[:])
                last.then_inc(pT_in_psum, 1)

            def values(b, h):
                i = NH * b + h
                pe.wait_ge(pT_ready, i + 1)
                if h == 0:
                    pe.wait_ge(cs_ready, b + 1)
                wait_count(pe, o_ready, i)
                for st in range(2):
                    last = mm3(ps[:, 5, 0:L], [v[:, st, :] for v in cS], [v[:, h % 2, st, :] for v in pT],
                               st == 0, st == 1)
                last.then_inc(av_done, 1)

            def project(b, h):
                i = NH * b + h
                pe.wait_ge(o_ready, i + 1)
                if h == 0:
                    wait_count(pe, x3_ready, b)
                for tt in range(2):
                    last = mm3(ps[:, 6 + tt, 0:H], [v[:, h % 2, P * tt:P * tt + P] for v in oT],
                               [n[:, h % NH, :] for n in nvo], h % NH == 0, h % NH == NH - 1)
                last.then_inc(o_added, 1)

            def attend(b, first, last):
                for h in range(NH + 4 if last else NH):
                    if h == NH - 2 and not last:
                        turn_xn3(b + 1)
                    if not (first and h < 2) and h < NH + 2:
                        turn_p(b, h - 2)
                    if h < NH:
                        scores(b, h)
                    if not (first and h < 3) and h < NH + 3:
                        values(b, h - 3)
                    if not (last and h + 2 >= NH):
                        queries(b, h + 2)
                    if not (first and h < 4):
                        project(b, h - 4)

            turn_xn3(0)
            queries(0, 0)
            queries(0, 1)
            attend(0, True, False)
            with pe.Fori(1, B - 1) as b:
                attend(b, False, False)
            attend(B - 1, False, True)

            def into(b):
                pe.wait_ge(f_q, b + 1)
                for k in range(2):
                    for j in range(2):
                        last = pe.transpose(bank(0).bitcast(BF16)[:, H * k + P * j:H * k + P * j + P],
                                            xq[:, H * k + P * j:H * k + P * j + P], identb[:])
                last.then_inc(f_qT_in_psum, 1)
                pe.wait_ge(f_qT, b + 1)
                for k in range(2):
                    for n in range(2):
                        for j in range(2):
                            last = pe.matmul(bank(1 + 2 * k + n), xqT[:, H * k + P * j:H * k + P * j + P],
                                             w1T[:, j, 512 * n:512 * n + 512], start=(j == 0), stop=(j == 1))
                last.then_inc(f_h_done, 1)

            def out_of(b):
                for k in range(2):
                    pe.wait_ge(f_hq, 2 * b + k + 1)
                    for j in range(FT):
                        at = FI * k + P * j
                        last = pe.transpose(bank(5 + k).bitcast(BF16)[:, P * j:P * j + P], hq[:, at:at + P], identb[:])
                    last.then_inc(f_hqT_in_psum, 1)
                for k in range(2):
                    pe.wait_ge(f_hqT, 2 * b + k + 1)
                    for j in range(FT):
                        at = FI * k + P * j
                        last = pe.matmul(ps[:, 7, H * k:H * k + H], hqT[:, at:at + P], w2T[:, j, :],
                                         start=(j == 0), stop=(j == FT - 1))
                last.then_inc(f_y, 1)

            pe.wait_ge(x3_ready, B)
            into(0)
            with pe.Fori(0, B - 1) as b:
                into(b + 1)
                out_of(b)
            out_of(B - 1)

        @block.vector
        def _(dve):
            V = nc.vector
            chain = Chain(dve, dve_steps)
            V.memset(zeros[:], 0.0).then_inc(zeros_ready, 1)
            V.memset(ctxT[:, :, 0:PAD], 0.0).then_inc(pads_ready, 1)
            chain.step(V.memset(xpT[:], 0.0))
            chain.step(V.memset(split[32:64, :], 0.0))
            dve.wait_ge(d_win, 32)
            for d in range(DT):
                for k in range(NCONV):
                    last = V.tensor_scalar(wink[:, d, k, :], win[:, d, :], convw[:, d, k:k + 1], None, ALU.mult)
                last.then_inc(wink_ready, 1)
            chain.wait()
            dve.wait_ge(smallT_in_psum, 1)
            n_x = DTR + 2 * NS
            small = ps[:, 4, 0:DT * n_x].rearrange("p (d r) -> p d r", d=DT)
            for at in (0, 64, 96):
                V.tensor_copy(xpT[:, :, at:at + 2 * NS], small[:, :, DTR:])
            V.tensor_copy(xpT[:, :, 32:32 + DTR], small[:, :, 0:DTR])
            V.tensor_copy(dtwT[32:32 + DTR, :], ps[0:DTR, 5, 0:H])
            V.tensor_copy(gwT[:], ps[:, 6, 0:2 * E].rearrange("p (d e) -> p d e", d=2)).then_inc(smallT_ready, 1)
            dve.wait_ge(d_small, 160)
            chain.link(V.tensor_copy(mbias[:], mk8[:]))
            chain.link(V.tensor_reduce(alive[:], mbias[:], AX.X, ALU.max))
            V.tensor_scalar(mbias[:], mbias[:], -1.0, -MASKED, ALU.add, ALU.mult).then_inc(mask_ready, 1)
            dve.wait_ge(d_x, 16)
            for c in range(NT):
                chain.step(V.bn_stats(stats[:, c, :], x[:, c, :]))
            chain.wait()
            for c in range(NT):
                chain.step(V.bn_aggr(mv[:, c, :], stats[:, c, :]))
            chain.wait()
            V.tensor_scalar(ve[:], mv[:, :, 1], EPS, None, ALU.add).then_inc(ve_ready, 1)
            dve.wait_ge(rstd_ready, 1)
            V.scalar_tensor_tensor(nmr[:], mv[:, :, 0], -1.0, rstd[:], ALU.mult, ALU.mult).then_inc(nmr_ready, 1)
            dve.wait_ge(xdbl_done, 2)
            xdbl = ps[:, 4:6, :].rearrange("p a b -> p (a b)")
            V.tensor_copy(dtlow[32:32 + DTR, :], xdbl[32:32 + DTR, :]).then_inc(dtlow_ready, 1)
            chain.step(V.tensor_copy(split[0:32, :], xdbl[0:32, :]))
            chain.link(V.tensor_copy(split[64:128, :], xdbl[64:128, :]))
            chain.link(V.tensor_tensor(rest[64:128, :], xdbl[64:128, :], split[64:128, :], ALU.subtract))
            chain.link(V.tensor_copy(split[64:128, :], rest[64:128, :]))
            chain.link(V.tensor_tensor(rest[96:128, :], rest[96:128, :], split[96:128, :], ALU.subtract))
            V.tensor_copy(split[96:128, :], rest[96:128, :]).then_inc(split_ready, 1)
            dve.wait_ge(a_exp, 1)
            V.tensor_scalar(amat[:], amat[:], -1.0, None, ALU.mult).then_inc(a_ready, 1)
            for d in range(DT):
                dve.wait_ge(sp_exp, d + 1)
                V.tensor_scalar(sp[2 * d][:], sp[2 * d + 1][:], 1.0, None, ALU.add).then_inc(sp_u, 1)
            for d in range(DT):
                dve.wait_ge(sp_u, d + 1)
                chain.link(V.scalar_tensor_tensor(sp[2 * d + 1][:], sp[2 * d][:], -1.0, sp[2 * d + 1][:],
                                                  ALU.add, ALU.subtract))
                dve.wait_ge(sp_ln, d + 1)
                chain.step(V.tensor_tensor(dtv[:, d], dtv[:, d], sp[2 * d + 1][:], ALU.subtract))
                chain.link(V.tensor_scalar(sp[2 * d][:], ps[:, 2 * d:2 * d + 2, :].rearrange("p a b -> p (a b)"),
                                           dtb[:, d:d + 1], 0.0, ALU.add, ALU.max))
                chain.link(V.tensor_tensor(dtv[:, d], dtv[:, d], sp[2 * d][:], ALU.add))
                chain.step(V.tensor_tensor(du[:, d], dtv[:, d], u[:, d], ALU.mult))
                V.tensor_copy(nmax[:, 0:1], dtb[:, 0:1]).then_inc(dt_ready, 1)
            chain.wait()
            for k in range(2):
                last = V.memset(bank(k).rearrange("p (b l) -> p b l", b=2)[:, :, 0:1], 0.0)
            last.then_inc(da_zeroed, 1)

            def drive(m, j):
                dve.wait_ge(b_copied, 16 + 2 * m + j // 2 + 1)
                dve.wait_ge(scanned, 32 + 4 * m + j - 3)
                V.tensor_tensor(dbu[:, j, :], du[:, 0, 512:1024], bank(4 + j // 2), ALU.mult).then_inc(dve_dbu, 1)

            def scan(hb, m, j):
                i = 32 * hb + 4 * m + j
                dve.wait_ge(da_ready, i + 1)
                if hb == 0:
                    dve.wait_ge(pool_dbu, i + 1)
                elif j % 2:
                    dve.wait_ge(pool_dbu, 32 + 2 * m + j // 2 + 1)
                else:
                    dve.wait_ge(dve_dbu, 2 * m + j // 2 + 1)
                wait_count(dve, hc_ready, i - 3)
                V.tensor_tensor_scan(hst[:, j, :], bank(j % 2), dbu[:, j, :], 0.0, ALU.mult, ALU.add)\
                    .then_inc(scanned, 1)

            def read_out(hb, m, j):
                i = 32 * hb + 4 * m + j
                dve.wait_ge(scanned, i + 1)
                dve.wait_ge(c_spread, 16 * hb + 2 * m + j // 2 + 1)
                wait_count(dve, y_added, i - 1)
                V.tensor_tensor(hc[:, j % 2, :], hst[:, j, :], bank(6 + j // 2), ALU.mult).then_inc(hc_ready, 1)

            def scan_four(hb, m, first, last_turn):
                for j in range(4):
                    scan(hb, m, j)
                    if hb and j == 1:
                        drive(m, 2)
                    if hb and j == 3 and not last_turn:
                        drive(m + 1, 0)
                    if j:
                        read_out(hb, m, j - 1)
                    elif not first:
                        read_out(hb, m - 1, 3)

            for hb in range(2):
                if hb:
                    drive(0, 0)
                scan_four(hb, 0, True, False)
                with dve.Fori(1, NS // 2 - 1) as m:
                    scan_four(hb, m, False, False)
                scan_four(hb, NS // 2 - 1, False, True)
                read_out(hb, NS // 2 - 1, 3)
                dve.wait_ge(y_added, 32 * (hb + 1))
                dve.wait_ge(sz_ready, 1)
                for d in range(DT):
                    chain.step(V.scalar_tensor_tensor(yz[:, d, :], u[:, d, 512 * hb:512 * hb + 512],
                                                      dskip[:, d:d + 1], bank(2 + d), ALU.mult, ALU.add))
                chain.wait()
                for d in range(DT):
                    last = V.tensor_tensor(yz[:, d, :].rearrange("p (b l) -> p b l", b=2),
                                           yz[:, d, :].rearrange("p (b l) -> p b l", b=2),
                                           sz[:, 4 * hb + d:4 * hb + 4:2, :], ALU.mult)
                last.then_inc(yz_ready, 1)
                dve.wait_ge(yT_ready, hb + 1)
                dve.wait_ge(tg_ready, 1)
                half = x[:, 4 * hb:4 * hb + 4, :].rearrange("p c h -> p (c h)")
                for b in range(2):
                    part = half[:, 512 * b:512 * b + 512]
                    chain.step(V.scalar_tensor_tensor(part, bank(4 + b), tg[:, 0:1], part, ALU.mult, ALU.add))
                chain.wait()
                for c in range(4 * hb, 4 * hb + 4):
                    last = V.bn_stats(stats[:, c, :], x[:, c, :])
                    chain.step(last)
                chain.wait()
                for c in range(4 * hb, 4 * hb + 4):
                    chain.step(V.bn_aggr(mv[:, c, :], stats[:, c, :]))
                chain.wait()
                V.tensor_scalar(ve[:, 4 * hb:4 * hb + 4], mv[:, 4 * hb:4 * hb + 4, 1], EPS, None, ALU.add)\
                    .then_inc(ve_ready, 1)
                V.tensor_copy(wsum[:, 0:1], tg[:, 0:1]).then_inc(x1_ready, 1)
                dve.wait_ge(rstd_ready, 2 + hb)
                for c in range(4 * hb, 4 * hb + 4):
                    V.tensor_scalar(xn[:, c, :], x[:, c, :], mv[:, c, 0:1], rstd[:, c:c + 1],
                                    ALU.subtract, ALU.mult).then_inc(xn_ready, 1)
                dve.wait_ge(logits_ready, hb + 1)
                logits = ps[:, 4, 0:4 * E].rearrange("p (c e) -> p c e", c=4)
                chain.link(V.tensor_reduce(nmax[:], logits, AX.X, ALU.max))
                V.tensor_tensor(lsub[:], logits, nmax[:].unsqueeze(2).to_broadcast([P, 4, E]), ALU.subtract)\
                    .then_inc(lsub_ready, 1)
                dve.wait_ge(pexp_ready, hb + 1)
                for c in range(4):
                    chain.step(V.max(top8[:, c, :], pexp[:, c, :]))
                chain.wait()
                for c in range(4):
                    V.max_index(eid[:, c, :], top8[:, c, :], pexp[:, c, :])
                    chain.step(V.match_replace(left[:, c, :], top8[:, c, :], pexp[:, c, :], -1.0))
                chain.wait()
                V.tensor_scalar(chosen[:, 4 * hb:4 * hb + 4, :], left[:], -1.0, None, ALU.is_equal)\
                    .then_inc(chosen_ready, 1)
                chain.step(V.tensor_copy(eidf[:], eid[:]))
                chain.step(V.tensor_reduce(wsum[:], top8[:], AX.X, ALU.add))
                chain.wait()
                chain.link(V.reciprocal(wsum[:], wsum[:]))
                chain.step(V.tensor_tensor(hot[:], iota_e[:].unsqueeze(1).unsqueeze(1).to_broadcast([P, 4, K, E]),
                                           eidf[:].unsqueeze(3).to_broadcast([P, 4, K, E]), ALU.is_equal))
                dve.wait_ge(pos_ready, hb + 1)
                pos = ps[:, 5, 0:4 * E].rearrange("p (c e) -> p c e", c=4)
                chain.step(V.tensor_scalar(over[:], pos, float(CAP), 2.0 * SLOTS, ALU.is_ge, ALU.mult))
                chain.step(V.tensor_tensor(slotv[:], pos, iota_slot[:].unsqueeze(1).to_broadcast([P, 4, E]), ALU.add))
                chain.wait()
                chain.link(V.tensor_tensor(slotv[:], slotv[:], over[:], ALU.add))
                for c in range(4):
                    chain.step(V.tensor_tensor(hot[:, c], hot[:, c],
                                               slotv[:, c, :].unsqueeze(1).to_broadcast([P, K, E]), ALU.mult))
                chain.wait()
                chain.link(V.tensor_reduce(slotk[:], hot[:], AX.X, ALU.add))
                span = slice(4 * K * hb, 4 * K * (hb + 1))
                flat = slotk[:].rearrange("p c k -> p (c k)")
                chain.step(V.tensor_scalar(keep[:], slotk[:], float(SLOTS), None, ALU.is_lt))
                chain.step(V.tensor_scalar(slotg[:], slotk[:], float(SLOTS), None, ALU.min))
                V.tensor_copy(idx_s[:, span], flat)
                chain.wait()
                chain.step(V.tensor_tensor(keep[:], keep[:], top8[:], ALU.mult))
                V.tensor_copy(idx_g[:, span], slotg[:].rearrange("p c k -> p (c k)"))
                chain.wait()
                V.tensor_tensor(wv[:, span].rearrange("p (c k) -> p c k", c=4), keep[:],
                                wsum[:].unsqueeze(2).to_broadcast([P, 4, K]), ALU.mult).then_inc(idx_ready, 1)

            for g in range(NKV):
                for k, dst in enumerate((mqk, nvo)):
                    dve.wait_ge(mn_hi, 2 * g + k + 1)
                    shape = "p a b c -> p (a b c)" if k == 0 else "p a b -> p (a b)"
                    V.tensor_tensor(dst[1][:, 2 * g:2 * g + 2].rearrange(shape), bank(6 + k),
                                    dst[0][:, 2 * g:2 * g + 2].rearrange(shape).bitcast(F32), ALU.subtract)\
                        .then_inc(mn_ready, 1)
            def gated(p, j):
                dve.wait_ge(sg_ready, p + 1)
                if not isinstance(p, int) or p > 1:
                    dve.wait_ge(turned_h, p - 1)
                V.tensor_tensor(hg[:, j % 2, :], sg[:, j % 2, :], ps[:, 2 + j % 2, I:2 * I], ALU.mult)\
                    .then_inc(hg_ready, 1)

            def take_out(p, j):
                dve.wait_ge(down_done, p + 1)
                if not isinstance(p, int) or p > 1:
                    dve.wait_ge(d_eo[j % 2], 16 * (p // 2) if isinstance(p, int) else 8 * (p - j % 2))
                V.tensor_copy(eo[:, j % 2, :], ps[:, 4 + j % 2, 0:H]).then_inc(eo_ready, 1)

            gated(0, 0)
            gated(1, 1)
            gated(2, 0)
            take_out(0, 0)
            gated(3, 1)
            take_out(1, 1)
            with dve.Fori(1, NPAIR // 2 - 1) as r:
                for j in range(2):
                    gated(2 * r + j + 2, j)
                    take_out(2 * r + j, j)
            take_out(NPAIR - 2, 0)
            take_out(NPAIR - 1, 1)

            def hold():
                V.memset(spare[:, 0:1], 0.0)

            def add_choice(b, cc, k):
                c = 2 * b + cc
                w = wv[:, bass.ds(c * K + k, 1)]
                if k == 0:
                    dve.wait_ge(d_gath[cc], 16 * K * (b + 1))
                    last = V.tensor_scalar(G[:, cc, 0, :], G[:, cc, 0, :], w, None, ALU.mult)
                else:
                    dve.wait_ge(comb_steps, 8 * c + k)
                    last = V.scalar_tensor_tensor(G[:, cc, 0, :], G[:, cc, k, :], w, G[:, cc, 0, :],
                                                  ALU.mult, ALU.add)
                last.then_inc(comb_steps, 1)

            def add_experts(b, cc):
                c = 2 * b + cc
                xc = x[:, bass.ds(c, 1), :].rearrange("p a h -> p (a h)")
                dve.wait_ge(comb_steps, 8 * c + 8)
                if cc == 0:
                    wait_count(dve, x2_kept, b)
                V.scalar_tensor_tensor(xb[:, cc, :], G[:, cc, 0, :], tg[:, 2:3], xc, ALU.mult, ALU.add)\
                    .then_inc(combined, 1)
                dve.wait_ge(combined, c + 1)
                V.bn_stats(stats[:, cc, :], xb[:, cc, :]).then_inc(ln_steps, 1)
                dve.wait_ge(ln_steps, 2 * c + 1)
                hold()
                V.bn_aggr(mv[:, cc, :], stats[:, cc, :]).then_inc(ln_steps, 1)
                if cc == 1:
                    dve.wait_ge(ln_steps, 4 * b + 4)
                    V.tensor_scalar(ve3[:], mv[:, 0:2, 1], EPS, None, ALU.add)\
                        .then_inc(ve3_ready, 1)

            def next_indices(b):
                V.tensor_copy(idx_b[:], idx_g[:, bass.ds(2 * b * K, 2 * K)]).then_inc(idx_here, 1)

            def norm3(b):
                dve.wait_ge(rstd3_ready, b + 1)
                if isinstance(b, int) and b == 0:
                    dve.wait_ge(d_scat[0], 16 * 32)
                else:
                    dve.wait_ge(xnT3_in_psum, b)
                for cc in range(2):
                    last = V.tensor_scalar(xn[:, cc, :], xb[:, cc, :], mv[:, cc, 0:1], rstd3[:, cc:cc + 1],
                                           ALU.subtract, ALU.mult)
                last.then_inc(xn3_ready, 1)

            def low(dst, src, hi, s):
                V.tensor_tensor(dst, src, hi.bitcast(F32), ALU.subtract).then_inc(s, 1)

            def batch_mask(b):
                wait_count(dve, s_masked, NH * b)
                V.tensor_copy(mb[:], mbias[:, bass.ds(b, 1), :].rearrange("p a l -> p (a l)")).then_inc(mb_ready, 1)

            def context_low(b):
                dve.wait_ge(c_hi, b + 1)
                low(cT[1][:], ctxT[:, bass.ds(b, 1), PAD:].rearrange("p a l -> p (a l)"), cT[0][:], c_ready)

            def context_rows_low(b):
                dve.wait_ge(cs_hi, b + 1)
                low(cS[1][:].rearrange("p a b -> p (a b)"),
                    ctx_tm[:, bass.ds(2 * b, 2), :].rearrange("p a b -> p (a b)"),
                    cS[0][:].rearrange("p a b -> p (a b)"), cs_ready)

            def norm_low(b):
                dve.wait_ge(xnT3_hi, b + 1)
                low(xnT3[1][:].rearrange("p a b -> p (a b)"), bank(0), xnT3[0][:].rearrange("p a b -> p (a b)"),
                    xnT3_ready)

            def q_low(b, h):
                i = NH * b + h
                dve.wait_ge(q_hi, i + 1)
                wait_count(dve, s_done, i - 1)
                low(qT[1][:, h % 2], bank(0)[:, 0:L], qT[0][:, h % 2], q_ready)

            def masked(b, h):
                i = NH * b + h
                dve.wait_ge(s_done, i + 1)
                wait_count(dve, p_exp, i - 1)
                if h == 0:
                    dve.wait_ge(mb_ready, b + 1)
                hold()
                for tt in range(2):
                    last = V.tensor_tensor_reduce(sneg[:, h % 2, tt, :], ps[:, 1 + h % 2, L * tt:L * tt + L], mb[:],
                                                  -(DH ** -0.5), 3e38, ALU.add, ALU.min,
                                                  accum_out=smin[:, h % 2, tt:tt + 1])
                last.then_inc(s_masked, 1)

            def inverse(b, h):
                i = NH * b + h
                dve.wait_ge(p_exp, i + 1)
                wait_count(dve, p_ready, i - 1)
                V.reciprocal(pinv[:, h % 2, :], psum_[:, h % 2, :]).then_inc(inv_steps, 1)
                dve.wait_ge(inv_steps, i + 1)
                V.tensor_scalar(pinv[:, h % 2, :], pinv[:, h % 2, :], alive[:, bass.ds(b + h // NH, 1)], None,
                                ALU.mult).then_inc(p_inv, 1)

            def pT_low(b, h):
                i = NH * b + h
                dve.wait_ge(pT_hi, i + 1)
                wait_count(dve, av_done, i - 1)
                low(pT[1][:, h % 2].rearrange("p a b -> p (a b)"), bank(3 + h % 2),
                    pT[0][:, h % 2].rearrange("p a b -> p (a b)"), pT_ready)

            def o_low(b, h):
                i = NH * b + h
                dve.wait_ge(o_hi, i + 1)
                wait_count(dve, o_added, i - 1)
                low(oT[1][:, h % 2], bank(5)[:, 0:L], oT[0][:, h % 2], o_ready)

            def add_attention(b):
                dve.wait_ge(o_added, NH * b + NH)
                dve.wait_ge(x2_kept, b + 1)
                for tt in range(2):
                    xc = x[:, bass.ds(2 * b + tt, 1), :].rearrange("p a h -> p (a h)")
                    last = V.scalar_tensor_tensor(xc, ps[:, 6 + tt, 0:H], tg[:, 1:2], xc, ALU.mult, ALU.add)
                last.then_inc(x3_ready, 1)

            def attend(b, first, last):
                if not last:
                    next_indices(b + 1)
                for h in range(NH + 3 if last else NH):
                    if h == NH - 2 and not last:
                        norm_low(b + 1)
                    if h == 3 and not first:
                        context_rows_low(b)
                    if h == 4 and not first:
                        add_attention(b - 1)
                    if not (first and h < 1) and h < NH + 1:
                        inverse(b, h - 1)
                    if not (first and h < 2) and h < NH + 2:
                        pT_low(b, h - 2)
                    if h < NH:
                        masked(b, h)
                    if h == NH - 1 and not last:
                        batch_mask(b + 1)
                        context_low(b + 1)
                    if not (first and h < 3):
                        o_low(b, h - 3)
                    if not (last and h + 2 >= NH):
                        q_low(b, h + 2)
                    if 5 <= h < 13 and not last:
                        for k in range(2):
                            add_choice(b + 1, (h - 5) // 4, 2 * ((h - 5) % 4) + k)
                    if h in (9, 12) and not last:
                        add_experts(b + 1, h // 12)
                    if h == 13 and not last:
                        norm3(b + 1)
                if last:
                    add_attention(b)

            next_indices(0)
            dve.wait_ge(mask_ready, 1)
            batch_mask(0)
            dve.wait_ge(d_ffn, 32)
            chain.step(V.tensor_reduce(wabs[:, 0:1], w1.rearrange("p a h -> p (a h)"), AX.X, ALU.add,
                                       apply_absolute_value=True))
            V.tensor_reduce(wabs[:, 1:2], w2.rearrange("p a b -> p (a b)"), AX.X, ALU.add,
                            apply_absolute_value=True).then_inc(wabs_ready, 1)
            dve.wait_ge(wsum_done, 1)
            chain.link(V.tensor_scalar(wmean[:], ps[:, 3, 0:2], 1.0 / (H * FI), 1e-5, ALU.mult, ALU.max))
            chain.link(V.reciprocal(wscale[:], wmean[:]))
            for k, flat in enumerate((w1.rearrange("p a h -> p (a h)"), w2.rearrange("p a b -> p (a b)"))):
                chain.link(V.tensor_scalar(flat, flat, wscale[:, k:k + 1], MAGIC, ALU.mult, ALU.add))
                chain.link(V.tensor_scalar(flat, flat, MAGIC, 1.0, ALU.subtract, ALU.min))
                if k:
                    dve.wait_ge(wternT_in_psum, 2)
                V.tensor_scalar(wtern, flat, -1.0, None, ALU.max).then_inc(wtern_ready, 1)

            for cc in range(2):
                for k in range(K):
                    add_choice(0, cc, k)
                add_experts(0, cc)
            norm3(0)
            context_low(0)
            context_rows_low(0)
            norm_low(0)
            q_low(0, 0)
            q_low(0, 1)
            attend(0, True, False)
            with dve.Fori(1, B - 1) as b:
                attend(b, False, False)
            attend(B - 1, False, True)

            dve.wait_ge(x3_ready, B)
            dve.wait_ge(xnT3_in_psum, B)
            dve.wait_ge(d_vec, 64)
            chain.link(V.tensor_scalar(wmean[:], wmean[:], 1.0 / 127.0, None, ALU.mult))

            def steps_of(s, per, b):
                n = [0]

                def step(ins):
                    n[0] += 1
                    assert n[0] <= per
                    ins.then_inc(s, 1)

                def sync():
                    dve.wait_ge(s, per * b + n[0])
                return step, sync

            def scales(step, sync, w):
                step(V.tensor_tensor(famax[:, w, :], famax[:, w, :], frm[:, w, :], ALU.mult))
                sync()
                step(V.tensor_scalar(famax[:, w, :], famax[:, w, :], 1e-5, None, ALU.max))
                sync()
                step(V.reciprocal(fqs[:, w, :], famax[:, w, :]))
                step(V.tensor_scalar(fback[:, w, :], famax[:, w, :], wmean[:, w:w + 1], None, ALU.mult))
                sync()
                step(V.scalar_tensor_tensor(fqs[:, w, :], fqs[:, w, :], 127.0, frm[:, w, :], ALU.mult, ALU.mult))
                sync()

            def front(b):
                step, sync = steps_of(f_front, 17, b)
                step(V.tensor_copy(xb, x[:, bass.ds(2 * b, 2), :]))
                sync()
                for k in range(2):
                    step(V.bn_stats(stats[:, k, :], xb[:, k, :]))
                sync()
                hold()
                for k in range(2):
                    step(V.bn_aggr(mv[:, k, :], stats[:, k, :]))
                sync()
                V.tensor_scalar(fve[:, 0, :], mv[:, 0:2, 1], EPS, None, ALU.add).then_inc(f_var[0], 1)
                dve.wait_ge(f_root[0], b + 1)
                for k in range(2):
                    step(V.tensor_scalar(xn[:, k, :], xb[:, k, :], mv[:, k, 0:1], frt[:, 0, k:k + 1],
                                         ALU.subtract, ALU.mult))
                step(V.tensor_tensor(fms[:, 0, :], mv[:, 0:2, 1], frt[:, 0, :], ALU.mult))
                sync()
                step(V.tensor_tensor(fms[:, 0, :], fms[:, 0, :], frt[:, 0, :], ALU.mult))
                sync()
                V.tensor_scalar(fms[:, 0, :], fms[:, 0, :], EPS, None, ALU.add).then_inc(f_rms[0], 1)
                step(V.tensor_reduce(famax[:, 0, :], xn[:, 0:2, :], AX.X, ALU.max, apply_absolute_value=True))
                sync()
                dve.wait_ge(f_rms_root[0], b + 1)
                scales(step, sync, 0)
                for k in range(2):
                    last = V.tensor_scalar(xn[:, k, :], xn[:, k, :], fqs[:, 0, k:k + 1], MAGIC, ALU.mult, ALU.add)
                step(last)
                sync()
                flat = xn[:, 0:2, :].rearrange("p a h -> p (a h)")
                step(V.tensor_scalar(flat, flat, MAGIC, 127.0, ALU.subtract, ALU.min))
                sync()
                V.tensor_scalar(xq, flat, -128.0, None, ALU.max).then_inc(f_q, 1)

            def hidden(b):
                dve.wait_ge(f_h_done, b + 1)
                wait_count(dve, f_hq, 2 * b)
                for k in range(2):
                    for j in range(2):
                        last = V.scalar_tensor_tensor(hbuf[:, k, 512 * j:512 * j + 512], bank(1 + 2 * k + j),
                                                      fback[:, 0, k:k + 1], b1v[:, 512 * j:512 * j + 512],
                                                      ALU.mult, ALU.add)
                last.then_inc(f_h, 1)

            def back(b):
                step, sync = steps_of(f_back, 17, b)
                for k in range(2):
                    dve.wait_ge(f_act, 2 * b + k + 1)
                    for j in range(2):
                        step(V.bn_stats(stats[:, 2 + 2 * k + j, :], hbuf[:, k, 512 * j:512 * j + 512]))
                sync()
                hold()
                for k in range(2):
                    step(V.bn_aggr(mv[:, 2 + k, :], stats[:, 2 + 2 * k:4 + 2 * k, :].rearrange("p a b -> p (a b)")))
                sync()
                V.tensor_scalar(fve[:, 1, :], mv[:, 2:4, 1], EPS, None, ALU.add).then_inc(f_var[1], 1)
                for k in range(2):
                    step(V.scalar_tensor_tensor(hbuf[:, k, :], hbuf[:, k, :], mv[:, 2 + k, 0:1], lng,
                                                ALU.subtract, ALU.mult))
                dve.wait_ge(f_root[1], b + 1)
                sync()
                for k in range(2):
                    V.scalar_tensor_tensor(hbuf[:, k, :], hbuf[:, k, :], frt[:, 1, k:k + 1], lnb,
                                           ALU.mult, ALU.add).then_inc(f_hn, 1)
                dve.wait_ge(f_hn, 2 * b + 2)
                step(V.tensor_reduce(famax[:, 1, :], hbuf[:], AX.X, ALU.max, apply_absolute_value=True))
                dve.wait_ge(f_sq, 2 * b + 2)
                V.tensor_scalar(fms[:, 1, :], fsq[:], 1.0 / FI, EPS, ALU.mult, ALU.add).then_inc(f_rms[1], 1)
                dve.wait_ge(f_rms_root[1], b + 1)
                sync()
                scales(step, sync, 1)
                for k in range(2):
                    last = V.tensor_scalar(hbuf[:, k, :], hbuf[:, k, :], fqs[:, 1, k:k + 1], MAGIC, ALU.mult, ALU.add)
                step(last)
                sync()
                for k in range(2):
                    step(V.tensor_scalar(hbuf[:, k, :], hbuf[:, k, :], MAGIC, 127.0, ALU.subtract, ALU.min))
                    sync()
                    V.tensor_scalar(hq[:, FI * k:FI * k + FI], hbuf[:, k, :], -128.0, None, ALU.max)                        .then_inc(f_hq, 1)

            def finish(b):
                dve.wait_ge(f_y, b + 1)
                wait_count(dve, d_out, 16 * b)
                for k in range(2):
                    last = V.scalar_tensor_tensor(yb[:, k, :], ps[:, 7, H * k:H * k + H], fback[:, 1, k:k + 1], b2v,
                                                  ALU.mult, ALU.add)
                last.then_inc(f_end, 1)
                dve.wait_ge(f_end, b + 1)
                V.scalar_tensor_tensor(yb, yb, tg[:, 3:4], x[:, bass.ds(2 * b, 2), :], ALU.mult, ALU.add)                    .then_inc(f_out, 1)

            def turn(b):
                front(b + 1)
                back(b)
                hidden(b + 1)
                finish(b)

            front(0)
            hidden(0)
            turn(0)
            with dve.Fori(1, B - 1) as b:
                turn(b)
            back(B - 1)
            finish(B - 1)


def kernel(**inputs):
    import numpy as np
    import concourse.bacc as bacc
    from concourse.bass_utils import run_bass_kernel_spmd

    nc = bacc.Bacc("TRN2", target_bir_lowering=False, num_devices=1)
    arrays, tensors = {}, {}
    for name, value in inputs.items():
        a = np.ascontiguousarray(value)
        key = "mask" if name == "mask_BxS2_bf1" else name
        if key == "mask":
            a = a.view(np.uint8)
        arrays[f"in_{key}"] = a
        tensors[key] = nc.dram_tensor(f"in_{key}", a.shape, mybir.dt.from_np(a.dtype), kind="ExternalInput").ap()
    out = nc.dram_tensor("out_0", (B, L, H), F32, kind="ExternalOutput").ap()
    build_program(nc, tensors, out)
    r = run_bass_kernel_spmd(nc, [arrays], core_ids=[0])
    return r.results[0]["out_0"]
```

```python
from contextlib import ExitStack

import concourse.bass as bass
from concourse import mybir

ALU = mybir.AluOpType
ACT = mybir.ActivationFunctionType
AX = mybir.AxisListType
F32 = mybir.dt.float32
F32R = mybir.dt.float32r
BF16 = mybir.dt.bfloat16
I32 = mybir.dt.int32
U32 = mybir.dt.uint32
U8 = mybir.dt.uint8
P = 128


class Chain:

    def __init__(self, engine, sem):
        self.engine, self.sem, self.base, self.n = engine, sem, 0, 0

    def step(self, ins):
        self.n += 1
        ins.then_inc(self.sem, 1)

    def wait(self, back=0):
        self.engine.wait_ge(self.sem, self.base + self.n - back)

    def link(self, ins):
        self.step(ins)
        self.wait()

B, L, H, DM = 4, 256, 256, 128
NT = B * L // P
NS, NCONV, DTR = 16, 4, 8
DT = H // P
E, K, CAP, I = 64, 8, 64, 96
SLOTS = E * CAP
NH, NKV, DH = 16, 8, 128
FI = 1024
FT = FI // P
EPS = 1e-5
MAGIC = 12582912.0
GROUP = 4
RING = 4
NG = E // GROUP
NPAIR = E // 2
PAD = NCONV - 1
MASKED = -1e30


def build_program(nc, t, out):
    with ExitStack() as ctx:
        mamba_scope = ExitStack()

        def sb(name, shape, dt=F32, scope=ctx):
            return scope.enter_context(nc.sbuf_tensor(name, shape, dt))

        def sem(name):
            return ctx.enter_context(nc.semaphore(name))

        ps = ctx.enter_context(nc.psum_tensor("ps", [P, 8, 512], F32))

        xin = nc.dram_tensor("expert_in", (SLOTS, H), F32, kind="Internal").ap()
        eout = nc.dram_tensor("expert_out", (SLOTS + 1, H), F32, kind="Internal").ap()

        ident = sb("ident", [P, P])
        identb = sb("identb", [P, P], BF16)
        ones = sb("ones", [P, P])
        onesb = sb("onesb", [P, P], BF16)
        before = sb("before", [P, P], BF16)
        mhalf = sb("mhalf", [P, 8])
        x = sb("x", [P, NT, H])
        xn = sb("xn", [P, NT, H])
        ctxT = sb("ctxT", [P, B, PAD + L])
        ctx_tm = sb("ctx_tm", [P, NT, DM])
        gates = sb("gates", [P, 4])
        tg = sb("tg", [P, 4])
        stats = sb("stats", [P, NT, 6])
        mv = sb("mv", [P, NT, 2])
        ve = sb("ve", [P, NT])
        rstd = sb("rstd", [P, NT])
        idx_s = sb("idx_s", [P, NT * K], I32)
        idx_g = sb("idx_g", [P, NT * K], I32)
        wv = sb("wv", [P, NT * K])
        mbias = sb("mbias", [P, B, L], BF16)
        alive = sb("alive", [P, B])
        wgu = sb("wgu", [P, RING, 2, GROUP, 2 * I])
        wdn = sb("wdn", [P, RING, GROUP, H])
        gwT = sb("gwT", [P, 2, E])

        def msb(name, shape, dt=F32):
            return sb(name, shape, dt, mamba_scope)

        convw = msb("convw", [P, DT, NCONV])
        convb = msb("convb", [P, DT])
        dtw = msb("dtw", [P, DT, DTR])
        dtb = msb("dtb", [P, DT])
        alog = msb("alog", [P, DT, NS])
        amat = msb("amat", [P, DT, NS])
        dskip = msb("dskip", [P, DT])
        u = msb("u", [P, DT, B * L])
        dtv = msb("dtv", [P, DT, B * L])
        du = msb("du", [P, DT, B * L])
        sz = msb("sz", [P, NT, L])
        nmr = msb("nmr", [P, NT])
        split = msb("split", [P, B * L], BF16)
        picks = msb("picks", [P, 32], BF16)
        sel = msb("sel", [P, 2 * NS, P], BF16)
        dbu = msb("dbu", [P, 4, 512])
        brow = msb("brow", [P, 2, 512])
        hc = msb("hc", [P, 2, 512])
        yz = msb("yz", [P, DT, 512])
        xnT = msb("xnT", [P, 4, 2, P])
        iota_e = msb("iota_e", [P, E])
        iota_slot = msb("iota_slot", [P, E])
        nmax = msb("nmax", [P, 4])
        lsub = msb("lsub", [P, 4, E])
        pexp = msb("pexp", [P, 4, E])
        top8 = msb("top8", [P, 4, K])
        eid = msb("eid", [P, 4, K], U32)
        eidf = msb("eidf", [P, 4, K])
        left = msb("left", [P, 4, E])
        chosen = msb("chosen", [P, NT, E], BF16)
        wsum = msb("wsum", [P, 4])
        over = msb("over", [P, 4, E])
        slotv = msb("slotv", [P, 4, E])
        hot = msb("hot", [P, 4, K, E])
        hst = hot[:].rearrange("p c k e -> p c (k e)")
        slotk = msb("slotk", [P, 4, K])
        keep = msb("keep", [P, 4, K])
        slotg = msb("slotg", [P, 4, K])
        mk8 = msb("mk8", [P, B, L], U8)
        gw_nat = msb("gw_nat", [E, H])
        win = msb("win", [P, DT, DM])
        xpw = msb("xpw", [DTR + 2 * NS, H])
        xpT = msb("xpT", [P, DT, P])
        dtwT = msb("dtwT", [P, H])
        wink = msb("wink", [P, DT, NCONV, DM])
        zeros = msb("zeros", [P, 8 * H])
        winT = msb("winT", [P, DT, NCONV, P])
        rest = msb("rest", [P, B * L])
        dtlow = msb("dtlow", [P, B * L])
        sp = [msb(f"sp{k}", [P, B * L]) for k in range(4)]
        mamba_scope.close()

        mqk = [sb(f"mqk{k}", [P, NH, 2, DM], F32R) for k in range(2)]
        nvo = [sb(f"nvo{k}", [P, NH, H], F32R) for k in range(2)]
        w1T = sb("w1T", [P, 2, FI], BF16)
        w2T = sb("w2T", [P, FT, H], BF16)
        wmean = sb("wmean", [P, 2])
        wscale = sb("wscale", [P, 2])
        ebuf = sb("ebuf", [P, 8 * H])
        xe = ebuf[:, 0:4 * H].rearrange("p (a h) -> p a h", a=4)
        xeT = ebuf[:, 4 * H:6 * H].rearrange("p (a b c) -> p a b c", a=2, b=2)
        eo = xn[:, 4:8, :]
        sg = sb("sg", [P, 2, I])
        hg = sb("hg", [P, 2, I])
        hT = sb("hT", [I, 2, P])

        prep_scope = ExitStack()

        def psb(name, shape, dt=F32):
            return sb(name, shape, dt, prep_scope)

        wq = psb("wq", [P, 2, NH * DH])
        wkv = psb("wkv", [P, 2, NKV * DH])
        wk, wvv = wkv[:, 0], wkv[:, 1]
        wo = psb("wo", [P, NH, H])
        w1 = wo[:, 0:FT, :]
        w2 = wo[:, FT:2 * FT, :].rearrange("p (a b) h -> p a (b h)", a=2)
        wqT = psb("wqT", [P, 2, 2, L])
        wkT, wvT = (v[:].rearrange("p a b -> p (a b)").bitcast(F32).rearrange("p (g d) -> p g d", g=NKV)
                    for v in (w1T, w2T))
        wabs = psb("wabs", [P, 2])
        wtern = wqT[:].rearrange("p a b l -> p (a b l)").bitcast(BF16)
        wgu_last = psb("wgu_last", [P, 2, GROUP, 2 * I])
        wdn_last = psb("wdn_last", [P, GROUP, H])
        prep_scope.close()

        def gate_up_weights(slot):
            return wgu[:, slot] if slot < RING else wgu_last[:]

        def down_weights(slot):
            return wdn[:, slot] if slot < RING else wdn_last[:]


        G = sb("G", [P, 2, K, H])
        xb = ebuf[:, 0:2 * H].rearrange("p (a h) -> p a h", a=2)
        mb = sb("mb", [P, L], BF16)
        spare = sb("spare", [P, 2])
        spare_pool = sb("spare_pool", [P, 2])
        spare_act = sb("spare_act", [P, 2])
        idx_b = sb("idx_b", [P, 2 * K], I32)
        ve3 = sb("ve3", [P, 2])
        rstd3 = sb("rstd3", [P, 2])
        xnT3 = [sb(f"xnT3_{k}", [P, 2, L], F32R) for k in range(2)]
        cT = [sb(f"cT{k}", [P, L], F32R) for k in range(2)]
        cS = [sb(f"cS{k}", [P, 2, DM], F32R) for k in range(2)]
        qT = [sb(f"qT{k}", [P, 2, L], F32R) for k in range(2)]
        sneg = ebuf[:, 2 * H:6 * H].rearrange("p (a b l) -> p a b l", a=2, b=2)
        smin = sb("smin", [P, 2, 2])
        pr = sb("pr", [P, 2, 2, L])
        psum_ = sb("psum_", [P, 2, 2])
        pinv = sb("pinv", [P, 2, 2])
        pn = sb("pn", [P, 2, 2, L])
        pT = [sb(f"pT{k}", [P, 2, 2, L], F32R) for k in range(2)]
        oT = [sb(f"oT{k}", [P, 2, L], F32R) for k in range(2)]
        flat_a = wgu[:].rearrange("p a b c d -> p (a b c d)")
        flat_b = wdn[:].rearrange("p a b c -> p (a b c)")
        hbuf = flat_a[:, 0:2 * FI].rearrange("p (a n) -> p a n", a=2)
        lng, lnb, b1v = (flat_a[:, k * FI:(k + 1) * FI] for k in (2, 3, 4))
        b2v = flat_b[:, 0:H]
        xq = flat_b[:, H:2 * H].bitcast(BF16)
        xqT = flat_b[:, 2 * H:3 * H].bitcast(BF16)
        hq = flat_b[:, 3 * H:7 * H].bitcast(BF16)
        hqT = flat_b[:, 7 * H:11 * H].bitcast(BF16)
        yb = flat_b[:, 11 * H:13 * H].rearrange("p (a n) -> p a n", a=2)
        hmid = [G[:, k, 0:FI // H, :].rearrange("p a h -> p (a h)") for k in range(2)]
        scratch = [G[:, k, FI // H:2 * FI // H, :].rearrange("p a h -> p (a h)") for k in range(2)] + \
            [v[:].rearrange("p a b l -> p (a b l)") for v in (pr, pn)]
        fve = sb("fve", [P, 2, 2])
        frt = sb("frt", [P, 2, 2])
        fms = sb("fms", [P, 2, 2])
        frm = sb("frm", [P, 2, 2])
        famax = sb("famax", [P, 2, 2])
        fqs = sb("fqs", [P, 2, 2])
        fback = sb("fback", [P, 2, 2])
        fsq = sb("fsq", [P, 2])
        fsum = sb("fsum", [P, 2])
        fmean = sb("fmean", [P, 2])
        fdev = sb("fdev", [P, 2])

        d_ctx, d_mask, d_win, d_small, d_x = sem("d_ctx"), sem("d_mask"), sem("d_win"), sem("d_small"), sem("d_x")
        d_zero, d_kv, d_qo, d_ffn = sem("d_zero"), sem("d_kv"), sem("d_qo"), sem("d_ffn")
        d_w = [sem(f"d_w{k}") for k in range(RING)]
        d_scat = sem("d_scat")
        consts_ready, zeros_ready = sem("consts_ready"), sem("zeros_ready")
        wink_ready = sem("wink_ready")
        ctxT_in_psum, winT_in_psum, smallT_in_psum = sem("ctxT_in_psum"), sem("winT_in_psum"), sem("smallT_in_psum")
        ctxT_ready, winT_ready, smallT_ready = sem("ctxT_ready"), sem("winT_ready"), sem("smallT_ready")
        conv_done, u_ready = sem("conv_done"), sem("u_ready")
        xdbl_done, split_high = sem("xdbl_done"), sem("split_high")
        dtlow_ready, split_ready = sem("dtlow_ready"), sem("split_ready")
        sp_relu, du_ready = sem("sp_relu"), sem("du_ready")
        dtraw_done, sp_exp, sp_u, sp_ln, dt_ready = (sem("dtraw_done"), sem("sp_exp"), sem("sp_u"), sem("sp_ln"),
                                                     sem("dt_ready"))
        sel_ready, a_exp, a_ready = sem("sel_ready"), sem("a_exp"), sem("a_ready")
        ve_ready, rstd_ready = sem("ve_ready"), sem("rstd_ready")
        nmr_ready, tg_ready = sem("nmr_ready"), sem("tg_ready")
        b_spread, c_spread, b_copied = sem("b_spread"), sem("c_spread"), sem("b_copied")
        da_ready, pool_dbu, dve_dbu = sem("da_ready"), sem("pool_dbu"), sem("dve_dbu")
        scanned, hc_ready, y_added = sem("scanned"), sem("hc_ready"), sem("y_added")
        yz_ready, yT_ready, x1_ready = sem("yz_ready"), sem("yT_ready"), sem("x1_ready")
        xn_ready, xnT_in_psum, xnT_ready = sem("xn_ready"), sem("xnT_in_psum"), sem("xnT_ready")
        logits_ready, lsub_ready, pexp_ready = sem("logits_ready"), sem("lsub_ready"), sem("pexp_ready")
        slots_ready, chosen_ready = sem("slots_ready"), sem("chosen_ready")
        pos_ready, idx_ready = sem("pos_ready"), sem("idx_ready")
        dve_steps, act_steps, pool_steps = sem("dve_steps"), sem("act_steps"), sem("pool_steps")
        d_out = sem("d_out")
        d_xe = [sem(f"d_xe{k}") for k in range(4)]
        d_eo = [sem(f"d_eo{k}") for k in range(4)]
        kvT_in_psum, kvT_ready = sem("kvT_in_psum"), sem("kvT_ready")
        wqT_in_psum, wqT_ready = sem("wqT_in_psum"), sem("wqT_ready")
        mn_done, mn_hi, mn_ready = sem("mn_done"), sem("mn_hi"), sem("mn_ready")
        wabs_ready, wsum_done, wtern_ready = sem("wabs_ready"), sem("wsum_done"), sem("wtern_ready")
        wternT_in_psum, wternT_ready, mask_ready = sem("wternT_in_psum"), sem("wternT_ready"), sem("mask_ready")
        xeT_in_psum, xeT_ready, gu_done = sem("xeT_in_psum"), sem("xeT_ready"), sem("gu_done")
        sg_ready, hg_ready, turned_h = sem("sg_ready"), sem("hg_ready"), sem("turned_h")
        hT_ready, down_done, eo_ready = sem("hT_ready"), sem("down_done"), sem("eo_ready")
        d_gath = [[sem(f"d_gath{cc}{half}") for half in range(2)] for cc in range(2)]
        combined, ve3_ready, rstd3_ready = sem("combined"), sem("ve3_ready"), sem("rstd3_ready")
        xn3_ready, xnT3_in_psum, xnT3_hi, xnT3_ready = (sem("xn3_ready"), sem("xnT3_in_psum"), sem("xnT3_hi"),
                                                        sem("xnT3_ready"))
        c_hi, c_ready = sem("c_hi"), sem("c_ready")
        idx_here, x2_kept = sem("idx_here"), sem("x2_kept")
        q_done, q_hi, q_ready = sem("q_done"), sem("q_hi"), sem("q_ready")
        s_done, s_masked, p_exp, p_inv, p_ready = (sem("s_done"), sem("s_masked"), sem("p_exp"), sem("p_inv"),
                                                   sem("p_ready"))
        pT_in_psum, pT_hi, pT_ready = sem("pT_in_psum"), sem("pT_hi"), sem("pT_ready")
        av_done, o_hi, o_ready, o_added = sem("av_done"), sem("o_hi"), sem("o_ready"), sem("o_added")
        x3_ready = sem("x3_ready")
        f_var = [sem("f_var0"), sem("f_var1")]
        f_root = [sem("f_root0"), sem("f_root1")]
        f_q, f_qT_in_psum, f_qT, f_h_done = sem("f_q"), sem("f_qT_in_psum"), sem("f_qT"), sem("f_h_done")
        f_h, f_silu, f_hn, f_clip = sem("f_h"), sem("f_silu"), sem("f_hn"), sem("f_clip")
        f_act = sem("f_act")
        f_hq, f_hqT_in_psum, f_hqT, f_y, f_out = (sem("f_hq"), sem("f_hqT_in_psum"), sem("f_hqT"), sem("f_y"),
                                                  sem("f_out"))
        mb_ready = sem("mb_ready")
        f_mean = sem("f_mean")
        f_front, f_back, f_end = sem("f_front"), sem("f_back"), sem("f_end")
        comb_steps, ln_steps, inv_steps = sem("comb_steps"), sem("ln_steps"), sem("inv_steps")

        block = ctx.enter_context(nc.Block())

        def wait_count(engine, s, n):
            if not isinstance(n, int) or n > 0:
                engine.wait_ge(s, n)

        def bank(k):
            return ps[:, k, :]

        def cols(ap, a, b):
            return ap[:, a:b]

        @block.sync
        def _(sp_):
            dma = sp_.dma_start
            dma(ctx_tm[:], t["ctx_1024"].rearrange("b (c p) d -> p (b c) d", p=P)).then_inc(d_ctx, 16)
            with nc.allow_non_contiguous_dma(reason="a few hundred values"):
                dma(win[:], t["L0_xattn_in_proj_w"].rearrange("(t p) d -> p t d", p=P)).then_inc(d_win, 16)
                dma(convw[:], t["L0_xattn_conv_w"].rearrange("(t p) a k -> p t (a k)", p=P)).then_inc(d_win, 16)
                dma(xpw[:], t["L0_xattn_x_proj_w"]).then_inc(d_small, 16)
                dma(dtw[:], t["L0_xattn_dt_proj_w"].rearrange("(t p) r -> p t r", p=P)).then_inc(d_small, 16)
                dma(gw_nat[:], t["L0_ffn_gate_w"]).then_inc(d_small, 16)
                dma(convb[:], t["L0_xattn_conv_b"].rearrange("(t p) -> p t", p=P)).then_inc(d_small, 16)
                dma(dtb[:], t["L0_xattn_dt_proj_b"].rearrange("(t p) -> p t", p=P)).then_inc(d_small, 16)
                dma(dskip[:], t["L0_xattn_D"].rearrange("(t p) -> p t", p=P)).then_inc(d_small, 16)
                dma(alog[:], t["L0_xattn_A_log"].rearrange("(t p) n -> p t n", p=P)).then_inc(d_small, 16)
                dma(gates[:, 0:2], t["g_xattn"].partition_broadcast(P)).then_inc(d_small, 16)
                dma(gates[:, 2:4], t["g_ffn"].partition_broadcast(P)).then_inc(d_small, 16)
            dma(x[:], t["x"].rearrange("b (c p) h -> p (b c) h", p=P)).then_inc(d_x, 16)
            dma(mk8[:].rearrange("p b l -> p (b l)"),
                t["mask"].rearrange("b l -> (b l)").partition_broadcast(P)).then_inc(d_mask, 16)
            sp_.wait_ge(zeros_ready, 1)
            for k in range(4):
                dma(xin[1024 * k:1024 * (k + 1)].rearrange("(p r) h -> p (r h)", p=P), zeros[:]).then_inc(d_zero, 16)
            dma(eout[SLOTS:SLOTS + 1], zeros[0:1, 0:H]).then_inc(d_zero, 16)

            def weights(group, slot, wait):
                if wait is not None:
                    sp_.wait_ge(down_done, wait)
                es = slice(group * GROUP, group * GROUP + GROUP) if isinstance(group, int) else \
                    bass.ds(group * GROUP, GROUP)
                done = d_w[slot] if slot < RING else d_ffn
                for k, name in enumerate(("L0_ffn_wg", "L0_ffn_wu")):
                    dma(gate_up_weights(slot)[:, k],
                        t[name][es].rearrange("e (p j) i -> p e (j i)", j=2)).then_inc(done, 16)
                dma(down_weights(slot)[0:I], t["L0_ffn_wd"][es].rearrange("e i h -> i e h")).then_inc(done, 16)

            for g in range(RING):
                weights(g, g, None)
            sp_.wait_ge(d_zero, 80)
            sp_.wait_ge(dt_ready, 2)
            sp_.wait_ge(split_ready, 1)
            sp_.wait_ge(mask_ready, 1)
            dma(wk, t["L1_xattn_Wk"]).then_inc(d_kv, 16)
            dma(wvv, t["L1_xattn_Wv"]).then_inc(d_kv, 16)
            dma(wq[:], t["L1_xattn_Wq"].rearrange("(j p) n -> p j n", p=P)).then_inc(d_qo, 16)
            dma(wo[:], t["L1_xattn_Wo"].rearrange("(h p) n -> p h n", p=P)).then_inc(d_qo, 16)
            weights(NG - 1, RING, None)
            sp_.wait_ge(idx_ready, 2)
            sp_.wait_ge(mn_done, 2 * NKV)
            sp_.wait_ge(d_ffn, 48)
            dma(w1, t["L1_ffn_w1"].rearrange("(c p) h -> p c h", p=P)).then_inc(d_ffn, 16)
            dma(w2, t["L1_ffn_w2"].rearrange("(c p) n -> p c n", p=P)).then_inc(d_ffn, 16)
            sp_.wait_ge(d_scat, 16 * NT * K)

            def rows(p, j, wait):
                if wait is not None:
                    sp_.wait_ge(xeT_in_psum, wait)
                at = slice(P * p, P * p + P) if isinstance(p, int) else bass.ds(P * p, P)
                dma(xe[:, j % 4], xin[at]).then_inc(d_xe[j % 4], 16)

            for p in range(4):
                rows(p, p, None)

            def feed(r, first, last):
                for j in range(8):
                    if not (last and j >= 4):
                        rows(8 * r + j + 4, j + 4, 8 * r + j + 1)
                    if j % 2 == 0 and not (first and j < 4) and not (last and j >= 2):
                        weights(4 * r + j // 2 + 2, (j // 2 + 2) % 4, 8 * r + j - 2)

            feed(0, True, False)
            with sp_.Fori(1, NPAIR // 8 - 1) as r:
                feed(r, False, False)
            feed(NPAIR // 8 - 1, False, True)
            sp_.wait_ge(down_done, NPAIR)
            sp_.wait_ge(combined, 2)
            for dst, name in ((b1v, "L1_ffn_b1"), (lng, "L1_ffn_ln_g"), (lnb, "L1_ffn_ln_b"), (b2v, "L1_ffn_b2")):
                dma(dst, t[name].partition_broadcast(P)).then_inc(d_kv, 16)
            out_rows = out.rearrange("b (c p) h -> b p c h", p=P)
            with sp_.Fori(0, B) as b:
                sp_.wait_ge(f_out, b + 1)
                dma(out_rows[bass.ds(b, 1)].rearrange("a p c h -> (a p) c h"), yb).then_inc(d_out, 16)
            sp_.wait_ge(d_out, 16 * B)
            for k in range(4):
                sp_.wait_ge(d_eo[k], 16 * (NPAIR // 4))
            sp_.wait_ge(d_zero, 80)

        @block.gpsimd
        def _(pool):
            chain = Chain(pool, pool_steps)
            nc.gpsimd.memset(ident[:], 0.0).then_inc(pool_steps, 1)
            nc.gpsimd.memset(ones[:], 1.0).then_inc(pool_steps, 1)
            nc.gpsimd.memset(onesb[:], 1.0).then_inc(pool_steps, 1)
            nc.gpsimd.memset(picks[:], 0.0).then_inc(pool_steps, 1)
            chain.n = 4
            chain.wait()
            chain.link(nc.gpsimd.affine_select(out=ident[:], in_=ident[:], compare_op=ALU.not_equal, fill=1.0, base=0,
                                               pattern=[[-1, P]], channel_multiplier=1))
            nc.gpsimd.tensor_copy(identb[:], ident[:]).then_inc(consts_ready, 1)
            nc.gpsimd.affine_select(out=before[:], in_=onesb[:], compare_op=ALU.is_gt, fill=0.0, base=0,
                                    pattern=[[1, P]], channel_multiplier=-1).then_inc(consts_ready, 1)
            nc.gpsimd.memset(mhalf[:], -0.5).then_inc(consts_ready, 1)
            for part in (0, 64, 96):
                chain.link(nc.gpsimd.affine_select(out=picks[:], in_=picks[:], compare_op=ALU.not_equal, fill=1.0,
                                                   base=-part, pattern=[[-1, 32]], channel_multiplier=1))
            nc.gpsimd.tensor_copy(sel[:], picks[:].unsqueeze(2).to_broadcast([P, 32, P])).then_inc(sel_ready, 1)
            nc.gpsimd.iota(iota_e[:], [[1, E]], base=0, channel_multiplier=0,
                           allow_small_or_imprecise_dtypes=True).then_inc(consts_ready, 1)
            nc.gpsimd.iota(iota_slot[:], [[CAP, E]], base=0, channel_multiplier=0,
                           allow_small_or_imprecise_dtypes=True).then_inc(consts_ready, 1)
            pool.wait_ge(consts_ready, 3)
            pool.wait_ge(ve_ready, 1)
            nc.gpsimd.tensor_tensor(rstd[:], ve[:], mhalf[:], ALU.pow).then_inc(rstd_ready, 1)

            def drive(hb, m, j):
                i = 32 * hb + 4 * m + j
                pool.wait_ge(b_copied, 16 * hb + 2 * m + j // 2 + 1)
                wait_count(pool, scanned, i - 3)
                nc.gpsimd.tensor_tensor(dbu[:, j, :], du[:, j % 2, 512 * hb:512 * hb + 512], brow[:, j // 2, :],
                                        ALU.mult).then_inc(pool_dbu, 1)

            def scatter(hb, c, k):
                nc.gpsimd.indirect_dma_start(
                    xin, bass.IndirectOffsetOnAxis(ap=idx_s[:, c * K + k:c * K + k + 1], axis=0),
                    xn[:, c, :], None, bounds_check=SLOTS - 1, oob_is_err=False).then_inc(d_scat, 16)

            def root(hb):
                pool.wait_ge(ve_ready, 2 + hb)
                nc.gpsimd.tensor_tensor(rstd[:, 4 * hb:4 * hb + 4], ve[:, 4 * hb:4 * hb + 4], mhalf[:, 0:4],
                                        ALU.pow).then_inc(rstd_ready, 1)

            pool.wait_ge(dt_ready, 1)
            pool.wait_ge(u_ready, 4)
            chain.link(nc.gpsimd.tensor_tensor(du[:, 0], dtv[:, 0], u[:, 0], ALU.mult))
            pool.wait_ge(du_ready, 1)
            for j in range(4):
                drive(0, 0, j)
            with pool.Fori(1, NS // 2) as m:
                for j in range(4):
                    drive(0, m, j)
            root(0)
            pool.wait_ge(d_zero, 80)
            pool.wait_ge(slots_ready, 4)
            pool.wait_ge(xn_ready, 4)
            for m in range(NS // 2):
                drive(1, m, 1)
                scatter(0, 2 * m // K, 2 * m % K)
                drive(1, m, 2)
                drive(1, m, 3)
                scatter(0, 2 * m // K, 2 * m % K + 1)
            root(1)
            for c in range(2, 4):
                for k in range(K):
                    scatter(0, c, k)
            pool.wait_ge(xn_ready, 8)
            for c in range(4, NT):
                pool.wait_ge(slots_ready, c + 1)
                for k in range(K):
                    scatter(1, c, k)

            def put(p, j):
                pool.wait_ge(eo_ready, p + 1)
                at = slice(P * p, P * p + P) if isinstance(p, int) else bass.ds(P * p, P)
                pool.dma_start(eout[at], eo[:, j % 4]).then_inc(d_eo[j % 4], 16)

            with pool.Fori(0, NPAIR // 4) as r:
                for j in range(4):
                    put(4 * r + j, j)
            for k in range(4):
                pool.wait_ge(d_eo[k], 16 * (NPAIR // 4))
            pool.wait_ge(mn_ready, 2 * NKV)

            def gather(b, cc, k):
                if cc == 0 and k == 0:
                    pool.wait_ge(idx_here, b + 1)
                    nc.gpsimd.tensor_tensor(spare_pool[:], mhalf[:, 0:2], mhalf[:, 0:2], ALU.mult)
                nc.gpsimd.indirect_dma_start(
                    G[:, cc, k, :], None, eout,
                    bass.IndirectOffsetOnAxis(ap=idx_b[:, cc * K + k:cc * K + k + 1], axis=0),
                    bounds_check=SLOTS, oob_is_err=False).then_inc(d_gath[cc][2 * k // K], 16)

            def root3(b):
                pool.wait_ge(ve3_ready, b + 1)
                nc.gpsimd.tensor_tensor(rstd3[:], ve3[:], mhalf[:, 0:2], ALU.pow)\
                    .then_inc(rstd3_ready, 1)

            def normalise(b, h):
                i = NH * b + h
                pool.wait_ge(p_inv, i + 1)
                wait_count(pool, pT_in_psum, i - 1)
                nc.gpsimd.tensor_tensor(pn[:, h % 2], pr[:, h % 2],
                                        pinv[:, h % 2, :].unsqueeze(2).to_broadcast([P, 2, L]), ALU.mult)\
                    .then_inc(p_ready, 1)

            def root_of(b, which, k):
                src, dst = ((fve, frt), (fms, frm))[k]
                pool.wait_ge(f_var[which], 2 * b + k + 1)
                nc.gpsimd.tensor_tensor(dst[:, which, :], src[:, which, :], mhalf[:, 0:2], ALU.pow)\
                    .then_inc(f_root[which], 1)

            def roots(b, which):
                for k in range(2):
                    root_of(b, which, k)

            def attend(b, first, last):
                for h in range(NH):
                    if not (first and h == 0):
                        normalise(b, h - 1)
                    if not last and h == 12:
                        root3(b + 1)
                    if last and h in (6, 8):
                        root_of(0, 0, (h - 6) // 2)
                    if not last and h < K:
                        for k in range(2):
                            gather(b + 1, h // 4, 2 * (h % 4) + k)
                if last:
                    normalise(b, NH - 1)

            for cc in range(2):
                for k in range(K):
                    gather(0, cc, k)
            root3(0)
            attend(0, True, False)
            with pool.Fori(1, B - 1) as b:
                attend(b, False, False)
            attend(B - 1, False, True)
            with pool.Fori(0, B - 1) as b:
                roots(b + 1, 0)
                roots(b, 1)
            roots(B - 1, 1)

        @block.scalar
        def _(act):
            chain = Chain(act, act_steps)
            A = nc.scalar.activation
            act.wait_ge(zeros_ready, 2)
            for k in range(2):
                act.wait_ge(ctxT_in_psum, k + 1)
                A(ctxT[:, 2 * k:2 * k + 2, PAD:], bank(k).rearrange("p (b l) -> p b l", b=2), ACT.Copy)\
                    .then_inc(ctxT_ready, 1)
            for d in range(DT):
                act.wait_ge(winT_in_psum, d + 1)
                A(winT[:, d], bank(2 + d).rearrange("p (k e) -> p k e", k=NCONV), ACT.Copy).then_inc(winT_ready, 1)
            act.wait_ge(d_small, 144)
            for d in range(DT):
                for hb in range(2):
                    act.wait_ge(conv_done, 2 * d + hb + 1)
                    A(u[:, d, 512 * hb:512 * hb + 512], bank(2 * d + hb), ACT.Silu,
                      bias=convb[:, d:d + 1]).then_inc(u_ready, 1)
            act.wait_ge(nmr_ready, 1)
            act.wait_ge(rstd_ready, 1)
            for c in range(NT):
                last = A(sz[:, c, :], x[:, c, :], ACT.Silu, scale=rstd[:, c:c + 1], bias=nmr[:, c:c + 1])
            act.wait_ge(xdbl_done, 2)
            xdbl = ps[:, 4:6, :].rearrange("p a b -> p (a b)")
            for rows in (slice(64, 128), slice(0, 32)):
                A(split[rows, :], xdbl[rows, :], ACT.Copy).then_inc(split_high, 1)
            A(tg[:], gates[:], ACT.Tanh).then_inc(tg_ready, 1)
            A(amat[:], alog[:], ACT.Exp).then_inc(a_exp, 1)
            for d in range(DT):
                act.wait_ge(dtraw_done, 2 * d + 2)
                chain.link(A(sp[2 * d][:], ps[:, 2 * d:2 * d + 2, :].rearrange("p a b -> p (a b)"), ACT.Abs,
                             bias=dtb[:, d:d + 1]))
                A(sp[2 * d + 1][:], sp[2 * d][:], ACT.Exp, scale=-1.0).then_inc(sp_exp, 1)
            for d in range(DT):
                act.wait_ge(sp_u, d + 1)
                A(dtv[:, d], sp[2 * d][:], ACT.Ln).then_inc(sp_ln, 1)
                A((rest, dtlow)[d][:], ps[:, 2 * d:2 * d + 2, :].rearrange("p a b -> p (a b)"), ACT.Relu,
                  bias=dtb[:, d:d + 1]).then_inc(sp_relu, 1)

            act.wait_ge(a_ready, 2)
            act.wait_ge(dt_ready, 2)

            def decay(hb, m, j):
                i, d = 32 * hb + 4 * m + j, j % 2
                wait_count(act, scanned, i - 1)
                A(bank(d).rearrange("p (b l) -> p b l", b=2)[:, :, 1:],
                  dtv[:, d, 512 * hb:512 * hb + 512].rearrange("p (b l) -> p b l", b=2)[:, :, 1:],
                  ACT.Exp, scale=amat[:, d, bass.ds(2 * m + j // 2, 1)]).then_inc(da_ready, 1)

            def copy_b(hb, m, k):
                act.wait_ge(b_spread, 16 * hb + 2 * m + k + 1)
                if hb == 0:
                    wait_count(act, pool_dbu, 2 * (2 * m + k) - 2)
                else:
                    act.wait_ge(pool_dbu, 32 if isinstance(m, int) and m == 0 else 32 + 3 * m - 2 + 2 * k)
                A(brow[:, k, :], bank(4 + k), ACT.Copy).then_inc(b_copied, 1)

            def decays(hb, m, last):
                for j in range(4):
                    decay(hb, m, j)
                    if j % 2 and not last:
                        copy_b(hb, m + 1, j // 2)

            for hb in range(2):
                copy_b(hb, 0, 0)
                copy_b(hb, 0, 1)
                decays(hb, 0, False)
                with act.Fori(1, NS // 2 - 1) as m:
                    decays(hb, m, False)
                decays(hb, NS // 2 - 1, True)
                act.wait_ge(xnT_in_psum, hb + 1)
                for k in range(2):
                    A(xnT[:, 2 * k:2 * k + 2].rearrange("p a b c -> p (a b c)"), bank(6 + k), ACT.Copy)\
                        .then_inc(xnT_ready, 1)
                act.wait_ge(lsub_ready, hb + 1)
                A(pexp[:], lsub[:], ACT.Exp).then_inc(pexp_ready, 1)

            for k in range(4):
                act.wait_ge(kvT_in_psum, k + 1)
                dst = (wkT, wvT)[k // 2]
                A(dst[:, 4 * (k % 2):4 * (k % 2) + 4, :].rearrange("p a b -> p (a b)"), bank(k), ACT.Copy)\
                    .then_inc(kvT_ready, 1)
            def turned_wq(g):
                act.wait_ge(wqT_in_psum, g + 1)
                if g > 1:
                    act.wait_ge(mn_done, 2 * g - 3)
                A(wqT[:, g % 2].rearrange("p a b -> p (a b)"), bank(4 + g % 2), ACT.Copy).then_inc(wqT_ready, 1)

            turned_wq(0)
            for g in range(NKV):
                if g + 1 < NKV:
                    turned_wq(g + 1)
                for k, dst in enumerate((mqk, nvo)):
                    act.wait_ge(mn_done, 2 * g + k + 1)
                    A(dst[0][:, 2 * g:2 * g + 2].rearrange("p a b c -> p (a b c)" if k == 0 else "p a b -> p (a b)"),
                      bank(6 - 4 * (g % 2) + k), ACT.Copy).then_inc(mn_hi, 1)
            def turn(p, j):
                act.wait_ge(xeT_in_psum, p + 1)
                if not isinstance(p, int) or p > 1:
                    act.wait_ge(gu_done, p - 1)
                A(xeT[:, j % 2].rearrange("p a b -> p (a b)"), bank(j % 2)[:, 0:2 * P], ACT.Copy).then_inc(xeT_ready, 1)

            def gate(p, j):
                act.wait_ge(gu_done, p + 1)
                if not isinstance(p, int) or p > 1:
                    act.wait_ge(hg_ready, p - 1)
                A(sg[:, j % 2, :], ps[:, 2 + j % 2, 0:I], ACT.Silu).then_inc(sg_ready, 1)

            def turned_rows(p, j):
                act.wait_ge(turned_h, p + 1)
                if not isinstance(p, int) or p > 1:
                    act.wait_ge(down_done, p - 1)
                A(hT[:, j % 2, :], ps[0:I, 6 + j % 2, 0:P], ACT.Copy).then_inc(hT_ready, 1)

            turn(0, 0)
            turn(1, 1)
            gate(0, 0)
            turn(2, 0)
            gate(1, 1)
            turned_rows(0, 0)
            turn(3, 1)
            gate(2, 0)
            turned_rows(1, 1)
            with act.Fori(1, NPAIR // 2 - 1) as r:
                for j in range(2):
                    turn(2 * r + j + 2, j)
                    gate(2 * r + j + 1, j + 1)
                    turned_rows(2 * r + j, j)
            gate(NPAIR - 1, 1)
            turned_rows(NPAIR - 2, 0)
            turned_rows(NPAIR - 1, 1)

            for k in range(4):
                act.wait_ge(wternT_in_psum, k + 1)
                dst = w1T[:, k, :] if k < 2 else w2T[:, 4 * k - 8:4 * k - 4, :].rearrange("p a b -> p (a b)")
                A(dst, bank(4 + k).bitcast(BF16), ACT.Copy).then_inc(wternT_ready, 1)

            def context_high(b):
                wait_count(act, s_done, NH * b)
                A(cT[0][:], ctxT[:, bass.ds(b, 1), PAD:].rearrange("p a l -> p (a l)"), ACT.Copy).then_inc(c_hi, 1)

            def context_rows_high(b):
                wait_count(act, av_done, NH * b)
                A(cS[0][:], ctx_tm[:, bass.ds(2 * b, 2), :], ACT.Copy).then_inc(c_hi, 1)

            def norm_high(b):
                act.wait_ge(xnT3_in_psum, b + 1)
                A(xnT3[0][:].rearrange("p a b -> p (a b)"), bank(0), ACT.Copy).then_inc(xnT3_hi, 1)

            def keep_x2(b):
                act.wait_ge(combined, 2 * b + 2)
                A(x[:, bass.ds(2 * b, 2), :], xb, ACT.Copy).then_inc(x2_kept, 1)

            def q_high(b, h):
                i = NH * b + h
                act.wait_ge(q_done, i + 1)
                wait_count(act, s_done, i - 1)
                A(qT[0][:, h % 2], bank(0)[:, 0:L], ACT.Copy).then_inc(q_hi, 1)

            def exps(b, h):
                i = NH * b + h
                act.wait_ge(s_masked, i + 1)
                wait_count(act, p_ready, i - 1)
                for tt in range(2):
                    last = A(pr[:, h % 2, tt, :], sneg[:, h % 2, tt, :], ACT.Exp, scale=-1.0,
                             bias=smin[:, h % 2, tt:tt + 1], accum_out=psum_[:, h % 2, tt:tt + 1])
                last.then_inc(p_exp, 1)

            def pT_high(b, h):
                i = NH * b + h
                act.wait_ge(pT_in_psum, i + 1)
                wait_count(act, av_done, i - 1)
                A(pT[0][:, h % 2].rearrange("p a b -> p (a b)"), bank(3 + h % 2), ACT.Copy).then_inc(pT_hi, 1)

            def o_high(b, h):
                i = NH * b + h
                act.wait_ge(av_done, i + 1)
                wait_count(act, o_added, i - 1)
                A(oT[0][:, h % 2], bank(5)[:, 0:L], ACT.Copy).then_inc(o_hi, 1)

            def preload(at, function):
                A(spare_act[:, at:at + 1], mhalf[:, 0:1], function)

            def turned(b):
                act.wait_ge(f_qT_in_psum, b + 1)
                A(xqT, bank(0).bitcast(BF16)[:, 0:2 * H], ACT.Copy).then_inc(f_qT, 1)

            def attend(b, first, last):
                for h in range(NH + 3 if last else NH):
                    if h == NH - 2 and not last:
                        norm_high(b + 1)
                    if h == 3 and not first:
                        context_rows_high(b)
                    if not (first and h < 2) and h < NH + 2:
                        pT_high(b, h - 2)
                    if h == NH - 1 and not last:
                        context_high(b + 1)
                    if not (first and h < 3):
                        o_high(b, h - 3)
                    if not (last and h + 2 >= NH):
                        q_high(b, h + 2)
                    if h < NH:
                        exps(b, h)
                    if h == 12 and not last:
                        keep_x2(b + 1)
                    if h == NH:
                        turned(0)
                        preload(1, ACT.Silu)

            preload(0, ACT.Exp)
            context_high(0)
            context_rows_high(0)
            norm_high(0)
            keep_x2(0)
            q_high(0, 0)
            q_high(0, 1)
            attend(0, True, False)
            with act.Fori(1, B - 1) as b:
                attend(b, False, False)
            attend(B - 1, False, True)

            def gelu_silu(b):
                for k in range(2):
                    act.wait_ge(f_h, 2 * b + k + 1)
                    A(hbuf[:, k, :], hbuf[:, k, :], ACT.Silu).then_inc(f_silu, 1)
                for k in range(2):
                    act.wait_ge(f_silu, 2 * b + k + 1)
                    A(hbuf[:, k, :], hbuf[:, k, :], ACT.Gelu, accum_out=fsum[:, k:k + 1]).then_inc(f_act, 1)
                act.wait_ge(f_mean, b + 1)
                for k in range(2):
                    last = A(scratch[k], hbuf[:, k, :], ACT.Square,
                             bias=fmean[:, k:k + 1], accum_out=fdev[:, k:k + 1])
                last.then_inc(f_act, 1)

            def squares(b):
                for k in range(2):
                    act.wait_ge(f_hn, 2 * b + k + 1)
                    A(scratch[2 + k], hbuf[:, k, :], ACT.Square, accum_out=fsq[:, k:k + 1]).then_inc(f_act, 1)
                for k in range(2):
                    act.wait_ge(f_clip, 2 * b + k + 1)
                    A(hq[:, FI * k:FI * k + FI], hbuf[:, k, :], ACT.Copy, bias=-MAGIC).then_inc(f_hq, 1)
                for k in range(2):
                    act.wait_ge(f_hqT_in_psum, 2 * b + k + 1)
                    A(hqT[:, FI * k:FI * k + FI], bank(5 + k).bitcast(BF16), ACT.Copy).then_inc(f_hqT, 1)

            gelu_silu(0)
            with act.Fori(0, B - 1) as b:
                turned(b + 1)
                squares(b)
                gelu_silu(b + 1)
            squares(B - 1)

        @block.tensor
        def _(pe):
            pe.wait_ge(consts_ready, 1)
            pe.wait_ge(d_ctx, 16)
            for k in range(2):
                for j in range(4):
                    last = pe.transpose(ps[:, k, P * j:P * j + P], ctx_tm[:, 4 * k + j, :], ident[:])
                last.then_inc(ctxT_in_psum, 1)
            for d in range(DT):
                pe.wait_ge(wink_ready, d + 1)
                for k in range(NCONV):
                    last = pe.transpose(ps[:, 2 + d, P * k:P * k + P], wink[:, d, k, :], ident[:])
                last.then_inc(winT_in_psum, 1)
            for d in range(DT):
                for hb in range(2):
                    pe.wait_ge(ctxT_ready, 2)
                    pe.wait_ge(winT_ready, 2)
                    for k in range(NCONV):
                        last = pe.matmul(bank(2 * d + hb), winT[:, d, k, :], ctxT[:, 2 * hb:2 * hb + 2, k:k + L],
                                         start=(k == 0), stop=(k == NCONV - 1))
                    last.then_inc(conv_done, 1)
            pe.wait_ge(d_small, 144)
            n_x = DTR + 2 * NS
            for d in range(DT):
                pe.transpose(ps[:, 4, n_x * d:n_x * d + n_x], xpw[:, P * d:P * d + P], ident[0:n_x, 0:n_x])
            for d in range(DT):
                pe.transpose(ps[0:DTR, 5, P * d:P * d + P], dtw[:, d, :], ident[:])
            for d in range(2):
                last = pe.transpose(ps[:, 6, E * d:E * d + E], gw_nat[:, P * d:P * d + P], ident[0:E, 0:E])
            last.then_inc(smallT_in_psum, 1)
            pe.wait_ge(smallT_ready, 1)
            for hb in range(2):
                for d in range(DT):
                    pe.wait_ge(u_ready, 2 * d + hb + 1)
                    last = pe.matmul(bank(4 + hb), xpT[:, d, :], u[:, d, 512 * hb:512 * hb + 512],
                                     start=(d == 0), stop=(d == 1))
                last.then_inc(xdbl_done, 1)
            pe.wait_ge(dtlow_ready, 1)
            pe.wait_ge(u_ready, 4)
            for d in range(DT):
                for hb in range(2):
                    pe.matmul(bank(2 * d + hb), dtwT[32:32 + DTR, P * d:P * d + P],
                              dtlow[32:32 + DTR, 512 * hb:512 * hb + 512], start=True, stop=True)\
                        .then_inc(dtraw_done, 1)
            pe.wait_ge(sel_ready, 1)
            pe.wait_ge(split_ready, 1)

            def spread(hb, row, to, s):
                pick = sel[:, bass.ds(row, 1), :].rearrange("p a m -> p (a m)")
                pe.matmul(bank(to), pick, split[:, 512 * hb:512 * hb + 512], start=True, stop=True).then_inc(s, 1)

            def spread_b(hb, m, k):
                wait_count(pe, b_copied, 16 * hb + 2 * m + k - 1)
                if hb and k == 0:
                    wait_count(pe, dve_dbu, m)
                spread(hb, 2 * m + k, 4 + k, b_spread)

            def spread_c(hb, m, k):
                spread(hb, NS + 2 * m + k, 6 + k, c_spread)

            def add_states(hb, m, first, last_turn, last_b=False):
                for j in range(4):
                    i = 32 * hb + 4 * m + j
                    pe.wait_ge(hc_ready, i + 1)
                    pe.matmul(bank(2 + j % 2), ident[:], hc[:, j % 2, :], start=(first and j < 2),
                              stop=(last_turn and j > 1)).then_inc(y_added, 1)
                    if j % 2 and not last_turn:
                        spread_c(hb, m + 1, j // 2)
                        if not last_b:
                            spread_b(hb, m + 2, j // 2)

            for hb in range(2):
                if hb:
                    pe.wait_ge(x1_ready, 1)
                    pe.wait_ge(pos_ready, 1)
                    pe.wait_ge(idx_ready, 1)
                    pe.wait_ge(yz_ready, 1)
                    pe.wait_ge(xnT_ready, 2)
                pe.wait_ge(dt_ready, 2)
                for k in range(2):
                    spread_b(hb, 0, k)
                    spread_c(hb, 0, k)
                for k in range(2):
                    spread_b(hb, 1, k)
                add_states(hb, 0, True, False)
                with pe.Fori(1, NS // 2 - 2) as m:
                    add_states(hb, m, False, False)
                add_states(hb, NS // 2 - 2, False, False, last_b=True)
                add_states(hb, NS // 2 - 1, False, True)
                pe.wait_ge(yz_ready, hb + 1)
                for b in range(2):
                    for lt in range(2):
                        for d in range(DT):
                            last = pe.transpose(ps[:, 4 + b, H * lt + P * d:H * lt + P * d + P],
                                                yz[:, d, L * b + P * lt:L * b + P * lt + P], ident[:])
                last.then_inc(yT_ready, 1)
                for c in range(4):
                    pe.wait_ge(xn_ready, 4 * hb + c + 1)
                    for d in range(2):
                        last = pe.transpose(ps[:, 6 + c // 2, H * (c % 2) + P * d:H * (c % 2) + P * d + P],
                                            xn[:, 4 * hb + c, P * d:P * d + P], ident[:])
                last.then_inc(xnT_in_psum, 1)
                pe.wait_ge(xnT_ready, 2 * hb + 2)
                pe.wait_ge(x1_ready, hb + 1)
                for c in range(4):
                    for d in range(2):
                        last = pe.matmul(ps[:, 4, E * c:E * c + E], xnT[:, c, d, :], gwT[:, d, :],
                                         start=(d == 0), stop=(d == 1))
                last.then_inc(logits_ready, 1)
                pe.wait_ge(consts_ready, 2)
                pe.wait_ge(chosen_ready, hb + 1)
                for c in range(4):
                    for e in range(4 * hb + c + 1):
                        same = e == 4 * hb + c
                        last = pe.matmul(ps[:, 5, E * c:E * c + E], (before if same else onesb)[:], chosen[:, e, :],
                                         start=(e == 0), stop=same)
                last.then_inc(pos_ready, 1)

            pe.wait_ge(idx_ready, 2)
            pe.wait_ge(d_kv, 32)
            for k in range(4):
                src = (wk, wvv)[k // 2]
                for j in range(4):
                    at = P * (4 * (k % 2) + j)
                    last = pe.transpose(ps[:, k, P * j:P * j + P], src[:, at:at + P], ident[:])
                last.then_inc(kvT_in_psum, 1)

            def turn_wq(g):
                if g > 1:
                    pe.wait_ge(wqT_ready, g - 1)
                for hh in range(2):
                    for j in range(2):
                        last = pe.transpose(ps[:, 4 + g % 2, L * hh + P * j:L * hh + P * j + P],
                                            wq[:, j, P * (2 * g + hh):P * (2 * g + hh) + P], ident[:])
                last.then_inc(wqT_in_psum, 1)

            pe.wait_ge(d_qo, 32)
            turn_wq(0)
            pe.wait_ge(kvT_ready, 4)
            for g in range(NKV):
                if g + 1 < NKV:
                    turn_wq(g + 1)
                pe.wait_ge(wqT_ready, g + 1)
                if g > 1:
                    pe.wait_ge(mn_ready, 2 * g - 3)
                for hh in range(2):
                    for j in range(2):
                        last = pe.matmul(ps[:, 6 - 4 * (g % 2), L * hh + P * j:L * hh + P * j + P],
                                         wqT[:, g % 2, hh, P * j:P * j + P], wkT[:, g, :], start=True, stop=True)
                last.then_inc(mn_done, 1)
                if g > 1:
                    pe.wait_ge(mn_ready, 2 * g - 2)
                for hh in range(2):
                    last = pe.matmul(ps[:, 7 - 4 * (g % 2), L * hh:L * hh + L], wvT[:, g, :], wo[:, 2 * g + hh, :],
                                     start=True, stop=True)
                last.then_inc(mn_done, 1)
            def turn_rows(p, j):
                pe.wait_ge(d_xe[j % 4], 16 * (p // 4 + 1) if isinstance(p, int) else 4 * (p - j % 4) + 16)
                if not isinstance(p, int) or p > 1:
                    pe.wait_ge(xeT_ready, p - 1)
                for k in range(2):
                    last = pe.transpose(ps[:, j % 2, P * k:P * k + P], xe[:, j % 4, k::2], ident[:])
                last.then_inc(xeT_in_psum, 1)

            def slot_of(p, j):
                return RING if isinstance(p, int) and p >= NPAIR - 2 else j // 2 % 4

            def gate_up(p, j, r):
                slot = slot_of(p, j)
                if slot == RING:
                    pe.wait_ge(d_ffn, 48)
                elif j % 2 == 0:
                    pe.wait_ge(d_w[slot], 48 * r + 48)
                pe.wait_ge(xeT_ready, p + 1)
                if not isinstance(p, int) or p > 1:
                    pe.wait_ge(hg_ready, p - 1)
                for e in range(2):
                    for k in range(2):
                        last = pe.matmul(ps[CAP * e:CAP * e + CAP, 2 + j % 2, 0:2 * I]
                                         .rearrange("p (w i) -> p w i", w=2),
                                         xeT[:, j % 2, k, CAP * e:CAP * e + CAP],
                                         gate_up_weights(slot)[:, :, 2 * (j % 2) + e, I * k:I * k + I],
                                         start=(k == 0), stop=(k == 1))
                last.then_inc(gu_done, 1)

            def turn_h(p, j):
                pe.wait_ge(hg_ready, p + 1)
                if not isinstance(p, int) or p > 1:
                    pe.wait_ge(hT_ready, p - 1)
                pe.transpose(ps[0:I, 6 + j % 2, 0:P], hg[:, j % 2, :], ident[:]).then_inc(turned_h, 1)

            def down(p, j):
                slot = slot_of(p, j)
                pe.wait_ge(hT_ready, p + 1)
                if not isinstance(p, int) or p > 1:
                    pe.wait_ge(eo_ready, p - 1)
                for e in range(2):
                    last = pe.matmul(ps[CAP * e:CAP * e + CAP, 4 + j % 2, 0:H], hT[:, j % 2, CAP * e:CAP * e + CAP],
                                     down_weights(slot)[0:I, 2 * (j % 2) + e, :], start=True, stop=True)
                last.then_inc(down_done, 1)

            def expert_turn(r, first, last):
                for j in range(8):
                    if not (last and j == 7):
                        turn_rows(8 * r + j + 1, j + 1)
                    gate_up(8 * r + j, j, r)
                    if not (first and j == 0):
                        turn_h(8 * r + j - 1, (j - 1) % 8)
                    if not (first and j < 2):
                        down(8 * r + j - 2, (j - 2) % 8)

            pe.wait_ge(mn_ready, 2 * NKV)
            turn_rows(0, 0)
            expert_turn(0, True, False)
            with pe.Fori(1, NPAIR // 8 - 1) as r:
                expert_turn(r, False, False)
            expert_turn(NPAIR // 8 - 1, False, True)
            turn_h(NPAIR - 1, 7)
            down(NPAIR - 2, 6)
            down(NPAIR - 1, 7)

            pe.wait_ge(wabs_ready, 1)
            pe.matmul(ps[:, 3, 0:2], ones[:], wabs[:], start=True, stop=True).then_inc(wsum_done, 1)
            for k in range(4):
                if k % 2 == 0:
                    pe.wait_ge(wtern_ready, k // 2 + 1)
                for j in range(8):
                    if k < 2:
                        src, at = wtern[:, H * j + P * k:H * j + P * k + P], P * j
                    else:
                        src = wtern[:, FI * (j % 2) + P * (4 * (k - 2) + j // 2):][:, 0:P]
                        at = H * (j // 2) + P * (j % 2)
                    last = pe.transpose(bank(4 + k).bitcast(BF16)[:, at:at + P], src, identb[:])
                last.then_inc(wternT_in_psum, 1)

            def mm3(o, lhs, rhs, start, stop):
                pe.matmul(o, lhs[0], rhs[0], start=start, stop=False)
                pe.matmul(o, lhs[0], rhs[1], start=False, stop=False)
                return pe.matmul(o, lhs[1], rhs[0], start=False, stop=stop)

            def turn_xn3(b):
                pe.wait_ge(xn3_ready, b + 1)
                if isinstance(b, int) and b == 0:
                    pe.wait_ge(eo_ready, NPAIR)
                else:
                    pe.wait_ge(q_ready, NH * b)
                for j in range(2):
                    for cc in range(2):
                        last = pe.transpose(ps[:, 0, L * j + P * cc:L * j + P * cc + P],
                                            xn[:, cc, P * j:P * j + P], ident[:])
                last.then_inc(xnT3_in_psum, 1)

            def queries(b, h):
                i = NH * b + h
                if h % NH == 0:
                    pe.wait_ge(xnT3_ready, b + h // NH + 1)
                wait_count(pe, q_ready, i)
                for j in range(2):
                    last = mm3(ps[:, 0, 0:L], [m[:, h % NH, j, :] for m in mqk],
                               [v[:, j, :] for v in xnT3], j == 0, j == 1)
                last.then_inc(q_done, 1)

            def scores(b, h):
                i = NH * b + h
                pe.wait_ge(q_ready, i + 1)
                if h == 0:
                    pe.wait_ge(c_ready, 2 * b + 1)
                wait_count(pe, s_masked, i - 1)
                for tt in range(2):
                    last = mm3(ps[:, 1 + h % 2, L * tt:L * tt + L],
                               [q[:, h % 2, P * tt:P * tt + P] for q in qT], [v[:] for v in cT], True, True)
                last.then_inc(s_done, 1)

            def turn_p(b, h):
                i = NH * b + h
                pe.wait_ge(p_ready, i + 1)
                wait_count(pe, pT_ready, i - 1)
                for st in range(2):
                    for tt in range(2):
                        last = pe.transpose(ps[:, 3 + h % 2, L * st + P * tt:L * st + P * tt + P],
                                            pn[:, h % 2, tt, P * st:P * st + P], ident[:])
                last.then_inc(pT_in_psum, 1)

            def values(b, h):
                i = NH * b + h
                pe.wait_ge(pT_ready, i + 1)
                if h == 0:
                    pe.wait_ge(c_ready, 2 * b + 2)
                wait_count(pe, o_ready, i)
                for st in range(2):
                    last = mm3(ps[:, 5, 0:L], [v[:, st, :] for v in cS], [v[:, h % 2, st, :] for v in pT],
                               st == 0, st == 1)
                last.then_inc(av_done, 1)

            def project(b, h):
                i = NH * b + h
                pe.wait_ge(o_ready, i + 1)
                if h == 0:
                    wait_count(pe, x3_ready, b)
                for tt in range(2):
                    last = mm3(ps[:, 6 + tt, 0:H], [v[:, h % 2, P * tt:P * tt + P] for v in oT],
                               [n[:, h % NH, :] for n in nvo], h % NH == 0, h % NH == NH - 1)
                last.then_inc(o_added, 1)

            def turn_in(b):
                pe.wait_ge(f_q, b + 1)
                for k in range(2):
                    for j in range(2):
                        last = pe.transpose(bank(0).bitcast(BF16)[:, H * k + P * j:H * k + P * j + P],
                                            xq[:, H * k + P * j:H * k + P * j + P], identb[:])
                last.then_inc(f_qT_in_psum, 1)

            def into(b, k):
                if k == 0:
                    pe.wait_ge(f_qT, b + 1)
                for n in range(2):
                    for j in range(2):
                        last = pe.matmul(bank(1 + 2 * k + n), xqT[:, H * k + P * j:H * k + P * j + P],
                                         w1T[:, j, 512 * n:512 * n + 512], start=(j == 0), stop=(j == 1))
                last.then_inc(f_h_done, 1)

            def attend(b, first, last):
                for h in range(NH + 4 if last else NH):
                    if h == NH - 2 and not last:
                        turn_xn3(b + 1)
                    if not (first and h < 2) and h < NH + 2:
                        turn_p(b, h - 2)
                    if h < NH:
                        scores(b, h)
                    if not (first and h < 3) and h < NH + 3:
                        values(b, h - 3)
                    if not (last and h + 2 >= NH):
                        queries(b, h + 2)
                    if not (first and h < 4):
                        project(b, h - 4)
                    if h == NH:
                        turn_in(0)
                    if h == NH + 1:
                        pe.wait_ge(s_masked, NH * B)
                        into(0, 0)
                    if h == NH + 2:
                        into(0, 1)

            turn_xn3(0)
            queries(0, 0)
            queries(0, 1)
            attend(0, True, False)
            with pe.Fori(1, B - 1) as b:
                attend(b, False, False)
            attend(B - 1, False, True)

            def out_of(b):
                for k in range(2):
                    pe.wait_ge(f_hq, 2 * b + k + 1)
                    for j in range(FT):
                        at = FI * k + P * j
                        last = pe.transpose(bank(5 + k).bitcast(BF16)[:, P * j:P * j + P], hq[:, at:at + P], identb[:])
                    last.then_inc(f_hqT_in_psum, 1)
                for k in range(2):
                    pe.wait_ge(f_hqT, 2 * b + k + 1)
                    for j in range(FT):
                        at = FI * k + P * j
                        last = pe.matmul(ps[:, 7, H * k:H * k + H], hqT[:, at:at + P], w2T[:, j, :],
                                         start=(j == 0), stop=(j == FT - 1))
                last.then_inc(f_y, 1)

            pe.wait_ge(x3_ready, B)
            with pe.Fori(0, B - 1) as b:
                turn_in(b + 1)
                for k in range(2):
                    into(b + 1, k)
                out_of(b)
            out_of(B - 1)

        @block.vector
        def _(dve):
            V = nc.vector
            chain = Chain(dve, dve_steps)
            V.memset(zeros[:], 0.0).then_inc(zeros_ready, 1)
            V.memset(ctxT[:, :, 0:PAD], 0.0).then_inc(zeros_ready, 1)
            chain.step(V.memset(xpT[:], 0.0))
            chain.step(V.memset(split[32:64, :], 0.0))
            dve.wait_ge(d_win, 32)
            for d in range(DT):
                for k in range(NCONV):
                    last = V.tensor_scalar(wink[:, d, k, :], win[:, d, :], convw[:, d, k:k + 1], None, ALU.mult)
                last.then_inc(wink_ready, 1)
            dve.wait_ge(d_x, 16)
            for c in range(NT):
                chain.step(V.bn_stats(stats[:, c, :], x[:, c, :]))
            chain.wait()
            for c in range(NT):
                chain.step(V.bn_aggr(mv[:, c, :], stats[:, c, :]))
            chain.wait()
            V.tensor_scalar(ve[:], mv[:, :, 1], EPS, None, ALU.add).then_inc(ve_ready, 1)
            dve.wait_ge(rstd_ready, 1)
            V.scalar_tensor_tensor(nmr[:], mv[:, :, 0], -1.0, rstd[:], ALU.mult, ALU.mult).then_inc(nmr_ready, 1)
            chain.wait()
            dve.wait_ge(smallT_in_psum, 1)
            n_x = DTR + 2 * NS
            small = ps[:, 4, 0:DT * n_x].rearrange("p (d r) -> p d r", d=DT)
            for at in (0, 64, 96):
                V.tensor_copy(xpT[:, :, at:at + 2 * NS], small[:, :, DTR:])
            V.tensor_copy(xpT[:, :, 32:32 + DTR], small[:, :, 0:DTR])
            V.tensor_copy(dtwT[32:32 + DTR, :], ps[0:DTR, 5, 0:H])
            V.tensor_copy(gwT[:], ps[:, 6, 0:2 * E].rearrange("p (d e) -> p d e", d=2)).then_inc(smallT_ready, 1)
            dve.wait_ge(d_small, 144)
            dve.wait_ge(d_mask, 16)
            chain.link(V.tensor_copy(mbias[:], mk8[:]))
            chain.link(V.tensor_reduce(alive[:], mbias[:], AX.X, ALU.max))
            V.tensor_scalar(mbias[:], mbias[:], -1.0, -MASKED, ALU.add, ALU.mult).then_inc(mask_ready, 1)
            dve.wait_ge(xdbl_done, 2)
            xdbl = ps[:, 4:6, :].rearrange("p a b -> p (a b)")
            V.tensor_copy(dtlow[32:32 + DTR, :], xdbl[32:32 + DTR, :]).then_inc(dtlow_ready, 1)
            dve.wait_ge(split_high, 2)
            chain.link(V.tensor_tensor(rest[64:128, :], xdbl[64:128, :], split[64:128, :], ALU.subtract))
            chain.link(V.tensor_copy(split[64:128, :], rest[64:128, :]))
            chain.link(V.tensor_tensor(rest[96:128, :], rest[96:128, :], split[96:128, :], ALU.subtract))
            V.tensor_copy(split[96:128, :], rest[96:128, :]).then_inc(split_ready, 1)
            dve.wait_ge(a_exp, 1)
            V.tensor_scalar(amat[:], amat[:], -1.0, None, ALU.mult).then_inc(a_ready, 1)
            for d in range(DT):
                dve.wait_ge(sp_exp, d + 1)
                V.tensor_scalar(sp[2 * d][:], sp[2 * d + 1][:], 1.0, None, ALU.add).then_inc(sp_u, 1)
            for d in range(DT):
                dve.wait_ge(sp_u, d + 1)
                chain.link(V.scalar_tensor_tensor(sp[2 * d + 1][:], sp[2 * d][:], -1.0, sp[2 * d + 1][:],
                                                  ALU.add, ALU.subtract))
                dve.wait_ge(sp_ln, d + 1)
                chain.link(V.tensor_tensor(dtv[:, d], dtv[:, d], sp[2 * d + 1][:], ALU.subtract))
                dve.wait_ge(sp_relu, d + 1)
                V.tensor_tensor(dtv[:, d], dtv[:, d], (rest, dtlow)[d][:], ALU.add).then_inc(dt_ready, 1)
            dve.wait_ge(dt_ready, 2)
            V.tensor_tensor(du[:, 1], dtv[:, 1], u[:, 1], ALU.mult).then_inc(du_ready, 1)
            for k in range(2):
                last = V.memset(bank(k).rearrange("p (b l) -> p b l", b=2)[:, :, 0:1], 0.0)
            last.then_inc(a_ready, 1)

            def drive(m):
                dve.wait_ge(b_copied, 16 + 2 * m + 1)
                dve.wait_ge(scanned, 32 + 4 * m - 3)
                V.tensor_tensor(dbu[:, 0, :], du[:, 0, 512:1024], bank(4), ALU.mult).then_inc(dve_dbu, 1)

            def scan(hb, m, j):
                i = 32 * hb + 4 * m + j
                dve.wait_ge(da_ready, i + 1)
                if hb == 0:
                    dve.wait_ge(pool_dbu, i + 1)
                elif j:
                    dve.wait_ge(pool_dbu, 32 + 3 * m + j)
                else:
                    dve.wait_ge(dve_dbu, m + 1)
                wait_count(dve, hc_ready, i - 3)
                V.tensor_tensor_scan(hst[:, j, :], bank(j % 2), dbu[:, j, :], 0.0, ALU.mult, ALU.add)\
                    .then_inc(scanned, 1)

            def read_out(hb, m, j):
                i = 32 * hb + 4 * m + j
                dve.wait_ge(scanned, i + 1)
                dve.wait_ge(c_spread, 16 * hb + 2 * m + j // 2 + 1)
                wait_count(dve, y_added, i - 1)
                V.tensor_tensor(hc[:, j % 2, :], hst[:, j, :], bank(6 + j // 2), ALU.mult).then_inc(hc_ready, 1)

            def scan_four(hb, m, first, last_turn):
                for j in range(4):
                    scan(hb, m, j)
                    if hb and j == 3 and not last_turn:
                        drive(m + 1)
                    if j:
                        read_out(hb, m, j - 1)
                    elif not first:
                        read_out(hb, m - 1, 3)

            for hb in range(2):
                if hb:
                    drive(0)
                scan_four(hb, 0, True, False)
                with dve.Fori(1, NS // 2 - 1) as m:
                    scan_four(hb, m, False, False)
                scan_four(hb, NS // 2 - 1, False, True)
                read_out(hb, NS // 2 - 1, 3)
                dve.wait_ge(y_added, 32 * (hb + 1))
                dve.wait_ge(tg_ready, 1)
                for d in range(DT):
                    chain.step(V.scalar_tensor_tensor(yz[:, d, :], u[:, d, 512 * hb:512 * hb + 512],
                                                      dskip[:, d:d + 1], bank(2 + d), ALU.mult, ALU.add))
                chain.wait()
                for d in range(DT):
                    last = V.tensor_tensor(yz[:, d, :].rearrange("p (b l) -> p b l", b=2),
                                           yz[:, d, :].rearrange("p (b l) -> p b l", b=2),
                                           sz[:, 4 * hb + d:4 * hb + 4:2, :], ALU.mult)
                last.then_inc(yz_ready, 1)
                dve.wait_ge(yT_ready, hb + 1)
                dve.wait_ge(tg_ready, 1)
                half = x[:, 4 * hb:4 * hb + 4, :].rearrange("p c h -> p (c h)")
                for b in range(2):
                    part = half[:, 512 * b:512 * b + 512]
                    chain.step(V.scalar_tensor_tensor(part, bank(4 + b), tg[:, 0:1], part, ALU.mult, ALU.add))
                chain.wait()
                for c in range(4 * hb, 4 * hb + 4):
                    last = V.bn_stats(stats[:, c, :], x[:, c, :])
                    chain.step(last)
                chain.wait()
                for c in range(4 * hb, 4 * hb + 4):
                    chain.step(V.bn_aggr(mv[:, c, :], stats[:, c, :]))
                chain.wait()
                V.tensor_scalar(ve[:, 4 * hb:4 * hb + 4], mv[:, 4 * hb:4 * hb + 4, 1], EPS, None, ALU.add)\
                    .then_inc(ve_ready, 1)
                V.tensor_copy(wsum[:, 0:1], tg[:, 0:1]).then_inc(x1_ready, 1)
                dve.wait_ge(rstd_ready, 2 + hb)
                for c in range(4 * hb, 4 * hb + 4):
                    V.tensor_scalar(xn[:, c, :], x[:, c, :], mv[:, c, 0:1], rstd[:, c:c + 1],
                                    ALU.subtract, ALU.mult).then_inc(xn_ready, 1)
                dve.wait_ge(logits_ready, hb + 1)
                logits = ps[:, 4, 0:4 * E].rearrange("p (c e) -> p c e", c=4)
                chain.link(V.tensor_reduce(nmax[:], logits, AX.X, ALU.max))
                V.tensor_tensor(lsub[:], logits, nmax[:].unsqueeze(2).to_broadcast([P, 4, E]), ALU.subtract)\
                    .then_inc(lsub_ready, 1)
                dve.wait_ge(pexp_ready, hb + 1)
                for c in range(4):
                    chain.step(V.max(top8[:, c, :], pexp[:, c, :]))
                chain.wait()
                for c in range(4):
                    V.max_index(eid[:, c, :], top8[:, c, :], pexp[:, c, :])
                    chain.step(V.match_replace(left[:, c, :], top8[:, c, :], pexp[:, c, :], -1.0))
                chain.wait()
                V.tensor_scalar(chosen[:, 4 * hb:4 * hb + 4, :], left[:], -1.0, None, ALU.is_equal)\
                    .then_inc(chosen_ready, 1)
                chain.step(V.tensor_copy(eidf[:], eid[:]))
                chain.step(V.tensor_reduce(wsum[:], top8[:], AX.X, ALU.add))
                chain.wait()
                chain.link(V.reciprocal(wsum[:], wsum[:]))
                chain.step(V.tensor_tensor(hot[:], iota_e[:].unsqueeze(1).unsqueeze(1).to_broadcast([P, 4, K, E]),
                                           eidf[:].unsqueeze(3).to_broadcast([P, 4, K, E]), ALU.is_equal))
                dve.wait_ge(pos_ready, hb + 1)
                pos = ps[:, 5, 0:4 * E].rearrange("p (c e) -> p c e", c=4)
                chain.step(V.tensor_scalar(over[:], pos, float(CAP), 2.0 * SLOTS, ALU.is_ge, ALU.mult))
                chain.step(V.tensor_tensor(slotv[:], pos, iota_slot[:].unsqueeze(1).to_broadcast([P, 4, E]), ALU.add))
                chain.wait()
                chain.link(V.tensor_tensor(slotv[:], slotv[:], over[:], ALU.add))
                for c in range(6):
                    if c < 4:
                        chain.step(V.tensor_tensor(hot[:, c], hot[:, c],
                                                   slotv[:, c, :].unsqueeze(1).to_broadcast([P, K, E]), ALU.mult))
                    if 1 <= c < 5:
                        chain.wait(back=1 if c < 4 else 0)
                        chain.step(V.tensor_reduce(slotk[:, c - 1, :], hot[:, c - 1], AX.X, ALU.add))
                    if c > 1:
                        chain.wait(back=2 if c < 4 else 1 if c < 5 else 0)
                        at = K * (4 * hb + c - 2)
                        V.tensor_copy(idx_s[:, at:at + K], slotk[:, c - 2, :]).then_inc(slots_ready, 1)
                span = slice(4 * K * hb, 4 * K * (hb + 1))
                chain.step(V.tensor_scalar(keep[:], slotk[:], float(SLOTS), None, ALU.is_lt))
                chain.step(V.tensor_scalar(slotg[:], slotk[:], float(SLOTS), None, ALU.min))
                chain.wait()
                chain.step(V.tensor_tensor(keep[:], keep[:], top8[:], ALU.mult))
                V.tensor_copy(idx_g[:, span], slotg[:].rearrange("p c k -> p (c k)"))
                chain.wait()
                V.tensor_tensor(wv[:, span].rearrange("p (c k) -> p c k", c=4), keep[:],
                                wsum[:].unsqueeze(2).to_broadcast([P, 4, K]), ALU.mult).then_inc(idx_ready, 1)

            for g in range(NKV):
                for k, dst in enumerate((mqk, nvo)):
                    dve.wait_ge(mn_hi, 2 * g + k + 1)
                    shape = "p a b c -> p (a b c)" if k == 0 else "p a b -> p (a b)"
                    V.tensor_tensor(dst[1][:, 2 * g:2 * g + 2].rearrange(shape), bank(6 - 4 * (g % 2) + k),
                                    dst[0][:, 2 * g:2 * g + 2].rearrange(shape).bitcast(F32), ALU.subtract)\
                        .then_inc(mn_ready, 1)
            def gated(p, j):
                dve.wait_ge(sg_ready, p + 1)
                if not isinstance(p, int) or p > 1:
                    dve.wait_ge(turned_h, p - 1)
                V.tensor_tensor(hg[:, j % 2, :], sg[:, j % 2, :], ps[:, 2 + j % 2, I:2 * I], ALU.mult)\
                    .then_inc(hg_ready, 1)

            def take_out(p, j):
                dve.wait_ge(down_done, p + 1)
                if not isinstance(p, int) or p > 3:
                    dve.wait_ge(d_eo[j % 4], 16 * (p // 4) if isinstance(p, int) else 4 * (p - j % 4))
                V.tensor_copy(eo[:, j % 4, :], ps[:, 4 + j % 2, 0:H]).then_inc(eo_ready, 1)

            gated(0, 0)
            gated(1, 1)
            for p in range(4):
                gated(p + 2, p)
                take_out(p, p)
            with dve.Fori(1, NPAIR // 4 - 1) as r:
                for j in range(4):
                    gated(4 * r + j + 2, j)
                    take_out(4 * r + j, j)
            for p in range(NPAIR - 4, NPAIR):
                if p + 2 < NPAIR:
                    gated(p + 2, p % 4)
                take_out(p, p % 4)

            def hold():
                V.memset(spare[:, 0:1], 0.0)

            def add_choice(b, cc, k):
                c = 2 * b + cc
                w = wv[:, bass.ds(c * K + k, 1)]
                if k % (K // 2) == 0:
                    dve.wait_ge(d_gath[cc][2 * k // K], 8 * K * (b + 1))
                if k == 0:
                    last = V.tensor_scalar(G[:, cc, 0, :], G[:, cc, 0, :], w, None, ALU.mult)
                else:
                    dve.wait_ge(comb_steps, 8 * c + k)
                    last = V.scalar_tensor_tensor(G[:, cc, 0, :], G[:, cc, k, :], w, G[:, cc, 0, :],
                                                  ALU.mult, ALU.add)
                last.then_inc(comb_steps, 1)

            def add_experts(b, cc):
                c = 2 * b + cc
                xc = x[:, bass.ds(c, 1), :].rearrange("p a h -> p (a h)")
                dve.wait_ge(comb_steps, 8 * c + 8)
                if cc == 0:
                    wait_count(dve, x2_kept, b)
                V.scalar_tensor_tensor(xb[:, cc, :], G[:, cc, 0, :], tg[:, 2:3], xc, ALU.mult, ALU.add)\
                    .then_inc(combined, 1)
                dve.wait_ge(combined, c + 1)
                V.bn_stats(stats[:, cc, :], xb[:, cc, :]).then_inc(ln_steps, 1)
                dve.wait_ge(ln_steps, 2 * c + 1)
                hold()
                V.bn_aggr(mv[:, cc, :], stats[:, cc, :]).then_inc(ln_steps, 1)
                if cc == 1:
                    dve.wait_ge(ln_steps, 4 * b + 4)
                    V.tensor_scalar(ve3[:], mv[:, 0:2, 1], EPS, None, ALU.add)\
                        .then_inc(ve3_ready, 1)

            def next_indices(b):
                V.tensor_copy(idx_b[:], idx_g[:, bass.ds(2 * b * K, 2 * K)]).then_inc(idx_here, 1)

            def norm3(b):
                dve.wait_ge(rstd3_ready, b + 1)
                if isinstance(b, int) and b == 0:
                    dve.wait_ge(d_scat, 16 * NT * K)
                else:
                    dve.wait_ge(xnT3_in_psum, b)
                for cc in range(2):
                    last = V.tensor_scalar(xn[:, cc, :], xb[:, cc, :], mv[:, cc, 0:1], rstd3[:, cc:cc + 1],
                                           ALU.subtract, ALU.mult)
                last.then_inc(xn3_ready, 1)

            def low(dst, src, hi, s):
                V.tensor_tensor(dst, src, hi.bitcast(F32), ALU.subtract).then_inc(s, 1)

            def batch_mask(b):
                wait_count(dve, s_masked, NH * b)
                V.tensor_copy(mb[:], mbias[:, bass.ds(b, 1), :].rearrange("p a l -> p (a l)")).then_inc(mb_ready, 1)

            def context_low(b):
                dve.wait_ge(c_hi, 2 * b + 1)
                low(cT[1][:], ctxT[:, bass.ds(b, 1), PAD:].rearrange("p a l -> p (a l)"), cT[0][:], c_ready)

            def context_rows_low(b):
                dve.wait_ge(c_hi, 2 * b + 2)
                low(cS[1][:].rearrange("p a b -> p (a b)"),
                    ctx_tm[:, bass.ds(2 * b, 2), :].rearrange("p a b -> p (a b)"),
                    cS[0][:].rearrange("p a b -> p (a b)"), c_ready)

            def norm_low(b):
                dve.wait_ge(xnT3_hi, b + 1)
                low(xnT3[1][:].rearrange("p a b -> p (a b)"), bank(0), xnT3[0][:].rearrange("p a b -> p (a b)"),
                    xnT3_ready)

            def q_low(b, h):
                i = NH * b + h
                dve.wait_ge(q_hi, i + 1)
                wait_count(dve, s_done, i - 1)
                low(qT[1][:, h % 2], bank(0)[:, 0:L], qT[0][:, h % 2], q_ready)

            def masked(b, h):
                i = NH * b + h
                dve.wait_ge(s_done, i + 1)
                wait_count(dve, p_exp, i - 1)
                if h == 0:
                    dve.wait_ge(mb_ready, b + 1)
                hold()
                for tt in range(2):
                    last = V.tensor_tensor_reduce(sneg[:, h % 2, tt, :], ps[:, 1 + h % 2, L * tt:L * tt + L], mb[:],
                                                  -(DH ** -0.5), 3e38, ALU.add, ALU.min,
                                                  accum_out=smin[:, h % 2, tt:tt + 1])
                last.then_inc(s_masked, 1)

            def inverse(b, h):
                i = NH * b + h
                dve.wait_ge(p_exp, i + 1)
                wait_count(dve, p_ready, i - 1)
                V.reciprocal(pinv[:, h % 2, :], psum_[:, h % 2, :]).then_inc(inv_steps, 1)
                dve.wait_ge(inv_steps, i + 1)
                V.tensor_scalar(pinv[:, h % 2, :], pinv[:, h % 2, :], alive[:, bass.ds(b + h // NH, 1)], None,
                                ALU.mult).then_inc(p_inv, 1)

            def pT_low(b, h):
                i = NH * b + h
                dve.wait_ge(pT_hi, i + 1)
                wait_count(dve, av_done, i - 1)
                low(pT[1][:, h % 2].rearrange("p a b -> p (a b)"), bank(3 + h % 2),
                    pT[0][:, h % 2].rearrange("p a b -> p (a b)"), pT_ready)

            def o_low(b, h):
                i = NH * b + h
                dve.wait_ge(o_hi, i + 1)
                wait_count(dve, o_added, i - 1)
                low(oT[1][:, h % 2], bank(5)[:, 0:L], oT[0][:, h % 2], o_ready)

            def add_attention(b):
                dve.wait_ge(o_added, NH * b + NH)
                dve.wait_ge(x2_kept, b + 1)
                for tt in range(2):
                    xc = x[:, bass.ds(2 * b + tt, 1), :].rearrange("p a h -> p (a h)")
                    last = V.scalar_tensor_tensor(xc, ps[:, 6 + tt, 0:H], tg[:, 1:2], xc, ALU.mult, ALU.add)
                last.then_inc(x3_ready, 1)

            def steps_of(s, per, b, done=0):
                n = [done]

                def step(ins):
                    n[0] += 1
                    assert n[0] <= per
                    ins.then_inc(s, 1)

                def sync():
                    dve.wait_ge(s, per * b + n[0])
                return step, sync

            def scales(step, sync, w):
                step(V.tensor_tensor(famax[:, w, :], famax[:, w, :], frm[:, w, :], ALU.mult))
                sync()
                step(V.tensor_scalar(famax[:, w, :], famax[:, w, :], 1e-5, None, ALU.max))
                sync()
                step(V.reciprocal(fqs[:, w, :], famax[:, w, :]))
                step(V.tensor_scalar(fback[:, w, :], famax[:, w, :], wmean[:, w:w + 1], None, ALU.mult))
                sync()
                step(V.scalar_tensor_tensor(fqs[:, w, :], fqs[:, w, :], 127.0, frm[:, w, :], ALU.mult, ALU.mult))
                sync()

            def front_stats(b):
                step, sync = steps_of(f_front, 17, b)
                step(V.tensor_copy(xb, x[:, bass.ds(2 * b, 2), :]))
                sync()
                for k in range(2):
                    step(V.bn_stats(stats[:, k, :], xb[:, k, :]))
                sync()
                hold()
                for k in range(2):
                    step(V.bn_aggr(mv[:, k, :], stats[:, k, :]))
                sync()
                V.tensor_scalar(fve[:, 0, :], mv[:, 0:2, 1], EPS, None, ALU.add).then_inc(f_var[0], 1)

            def front_norm(b):
                step, sync = steps_of(f_front, 17, b, 5)
                dve.wait_ge(f_root[0], 2 * b + 1)
                for k in range(2):
                    step(V.tensor_scalar(xn[:, k, :], xb[:, k, :], mv[:, k, 0:1], frt[:, 0, k:k + 1],
                                         ALU.subtract, ALU.mult))
                step(V.tensor_tensor(fms[:, 0, :], mv[:, 0:2, 1], frt[:, 0, :], ALU.mult))
                sync()
                step(V.tensor_tensor(fms[:, 0, :], fms[:, 0, :], frt[:, 0, :], ALU.mult))
                sync()
                V.tensor_scalar(fms[:, 0, :], fms[:, 0, :], EPS, None, ALU.add).then_inc(f_var[0], 1)
                step(V.tensor_reduce(famax[:, 0, :], xn[:, 0:2, :], AX.X, ALU.max, apply_absolute_value=True))

            def front_scales(b):
                step, sync = steps_of(f_front, 17, b, 10)
                sync()
                dve.wait_ge(f_root[0], 2 * b + 2)
                scales(step, sync, 0)

            def front_round(b):
                step, sync = steps_of(f_front, 17, b, 15)
                for k in range(2):
                    last = V.tensor_scalar(xn[:, k, :], xn[:, k, :], fqs[:, 0, k:k + 1], MAGIC, ALU.mult, ALU.add)
                step(last)
                sync()
                flat = xn[:, 0:2, :].rearrange("p a h -> p (a h)")
                step(V.tensor_scalar(flat, flat, MAGIC, 127.0, ALU.subtract, ALU.min))
                sync()
                V.tensor_scalar(xq, flat, -128.0, None, ALU.max).then_inc(f_q, 1)

            def hidden(b, k):
                dve.wait_ge(f_h_done, 2 * b + k + 1)
                wait_count(dve, f_hq, 2 * b - 1 + k if not isinstance(b, int) or b else 0)
                for j in range(2):
                    last = V.scalar_tensor_tensor(hbuf[:, k, 512 * j:512 * j + 512], bank(1 + 2 * k + j),
                                                  fback[:, 0, k:k + 1], b1v[:, 512 * j:512 * j + 512],
                                                  ALU.mult, ALU.add)
                last.then_inc(f_h, 1)

            def middle(b):
                dve.wait_ge(f_act, 5 * b + 2)
                V.tensor_scalar(fmean[:], fsum[:], -1.0 / FI, None, ALU.mult).then_inc(f_mean, 1)

            def spread_of(b):
                dve.wait_ge(f_act, 5 * b + 3)
                V.tensor_scalar(fve[:, 1, :], fdev[:], 1.0 / FI, EPS, ALU.mult, ALU.add).then_inc(f_var[1], 1)

            def attend(b, first, last):
                if not last:
                    next_indices(b + 1)
                for h in range(NH + 3 if last else NH):
                    if h == NH - 2 and not last:
                        norm_low(b + 1)
                    if h == 3 and not first:
                        context_rows_low(b)
                    if h == 4 and not first:
                        add_attention(b - 1)
                    if not (first and h < 1) and h < NH + 1:
                        inverse(b, h - 1)
                    if not (first and h < 2) and h < NH + 2:
                        pT_low(b, h - 2)
                    if h < NH:
                        masked(b, h)
                    if h == NH - 1 and not last:
                        batch_mask(b + 1)
                        context_low(b + 1)
                    if not (first and h < 3):
                        o_low(b, h - 3)
                    if not (last and h + 2 >= NH):
                        q_low(b, h + 2)
                    if 4 <= h < 12 and not last:
                        for k in range(2):
                            add_choice(b + 1, h // 4 - 1, 2 * (h % 4) + k)
                    if h in (8, 11) and not last:
                        add_experts(b + 1, h // 11)
                    if h == 12 and not last:
                        norm3(b + 1)
                    if last and h == 5:
                        chain.link(V.tensor_scalar(wmean[:], wmean[:], 1.0 / 127.0, None, ALU.mult))
                        dve.wait_ge(xnT3_in_psum, B)
                        front_stats(0)
                    if last and h == 7:
                        front_norm(0)
                    if last and h == 9:
                        front_scales(0)
                    if last and h == 11:
                        front_round(0)
                    if h == NH + 1:
                        dve.wait_ge(d_kv, 32 + 64)
                        hidden(0, 0)
                    if h == NH + 2:
                        hidden(0, 1)
                if last:
                    add_attention(b)

            next_indices(0)
            dve.wait_ge(mask_ready, 1)
            batch_mask(0)
            dve.wait_ge(d_ffn, 48 + 32)
            chain.step(V.tensor_reduce(wabs[:, 0:1], w1.rearrange("p a h -> p (a h)"), AX.X, ALU.add,
                                       apply_absolute_value=True))
            V.tensor_reduce(wabs[:, 1:2], w2.rearrange("p a b -> p (a b)"), AX.X, ALU.add,
                            apply_absolute_value=True).then_inc(wabs_ready, 1)
            dve.wait_ge(wsum_done, 1)
            chain.link(V.tensor_scalar(wmean[:], ps[:, 3, 0:2], 1.0 / (H * FI), 1e-5, ALU.mult, ALU.max))
            chain.link(V.reciprocal(wscale[:], wmean[:]))
            for k, flat in enumerate((w1.rearrange("p a h -> p (a h)"), w2.rearrange("p a b -> p (a b)"))):
                chain.link(V.tensor_scalar(flat, flat, wscale[:, k:k + 1], MAGIC, ALU.mult, ALU.add))
                chain.link(V.tensor_scalar(flat, flat, MAGIC, 1.0, ALU.subtract, ALU.min))
                if k:
                    dve.wait_ge(wternT_in_psum, 2)
                V.tensor_scalar(wtern, flat, -1.0, None, ALU.max).then_inc(wtern_ready, 1)

            for cc in range(2):
                for k in range(K):
                    add_choice(0, cc, k)
                add_experts(0, cc)
            norm3(0)
            context_low(0)
            context_rows_low(0)
            norm_low(0)
            q_low(0, 0)
            q_low(0, 1)
            attend(0, True, False)
            with dve.Fori(1, B - 1) as b:
                attend(b, False, False)
            attend(B - 1, False, True)

            dve.wait_ge(x3_ready, B)

            def back(b):
                step, sync = steps_of(f_back, 9, b)
                dve.wait_ge(f_mean, b + 1)
                for k in range(2):
                    step(V.scalar_tensor_tensor(hmid[k], hbuf[:, k, :], fmean[:, k:k + 1], lng,
                                                ALU.add, ALU.mult))
                spread_of(b)
                dve.wait_ge(f_root[1], 2 * b + 1)
                sync()
                for k in range(2):
                    V.scalar_tensor_tensor(hbuf[:, k, :], hmid[k], frt[:, 1, k:k + 1], lnb,
                                           ALU.mult, ALU.add).then_inc(f_hn, 1)
                dve.wait_ge(f_hn, 2 * b + 2)
                step(V.tensor_reduce(famax[:, 1, :], hbuf[:], AX.X, ALU.max, apply_absolute_value=True))
                dve.wait_ge(f_act, 5 * b + 5)
                V.tensor_scalar(fms[:, 1, :], fsq[:], 1.0 / FI, EPS, ALU.mult, ALU.add).then_inc(f_var[1], 1)
                dve.wait_ge(f_root[1], 2 * b + 2)
                sync()
                scales(step, sync, 1)
                for k in range(2):
                    last = V.tensor_scalar(hbuf[:, k, :], hbuf[:, k, :], fqs[:, 1, k:k + 1], MAGIC, ALU.mult, ALU.add)
                step(last)
                sync()
                for k in range(2):
                    V.tensor_scalar(hbuf[:, k, :], hbuf[:, k, :], MAGIC + 127.0, MAGIC - 128.0, ALU.min, ALU.max)\
                        .then_inc(f_clip, 1)

            def finish(b):
                dve.wait_ge(f_y, b + 1)
                for k in range(2):
                    last = V.scalar_tensor_tensor(yb[:, k, :], ps[:, 7, H * k:H * k + H], fback[:, 1, k:k + 1], b2v,
                                                  ALU.mult, ALU.add)
                last.then_inc(f_end, 1)
                dve.wait_ge(f_end, b + 1)
                V.scalar_tensor_tensor(yb, yb, tg[:, 3:4], x[:, bass.ds(2 * b, 2), :], ALU.mult, ALU.add)\
                    .then_inc(f_out, 1)

            def turn(b, first):
                front_stats(b + 1)
                if not first:
                    finish(b - 1)
                front_norm(b + 1)
                front_scales(b + 1)
                middle(b)
                front_round(b + 1)
                back(b)
                for k in range(2):
                    hidden(b + 1, k)
                wait_count(dve, d_out, 16 * b)

            turn(0, True)
            with dve.Fori(1, B - 1) as b:
                turn(b, False)
            finish(B - 2)
            middle(B - 1)
            back(B - 1)
            dve.wait_ge(d_out, 16 * (B - 1))
            finish(B - 1)


def kernel(**inputs):
    import numpy as np
    import concourse.bacc as bacc
    from concourse.bass_utils import run_bass_kernel_spmd

    nc = bacc.Bacc("TRN2", target_bir_lowering=False, num_devices=1)
    arrays, tensors = {}, {}
    for name, value in inputs.items():
        a = np.ascontiguousarray(value)
        key = "mask" if name == "mask_BxS2_bf1" else name
        if key == "mask":
            a = a.view(np.uint8)
        arrays[f"in_{key}"] = a
        tensors[key] = nc.dram_tensor(f"in_{key}", a.shape, mybir.dt.from_np(a.dtype), kind="ExternalInput").ap()
    out = nc.dram_tensor("out_0", (B, L, H), F32, kind="ExternalOutput").ap()
    build_program(nc, tensors, out)
    r = run_bass_kernel_spmd(nc, [arrays], core_ids=[0])
    return r.results[0]["out_0"]
```
